# Optimizing a Trainium2 kernel written in Bass

```python
import numpy as np
import jax
import jax.numpy as jnp

def _softmax(x, axis=-1):
    return jax.nn.softmax(x, axis=axis)

def _gelu(x):
    return jax.nn.gelu(x, approximate=True)

def _silu(x):
    return jax.nn.silu(x)

def _sigmoid(x):
    return jax.nn.sigmoid(x)

def _layernorm(x, axis=-1, eps=1e-05):
    m = jnp.mean(x, axis=axis, keepdims=True)
    v = jnp.var(x, axis=axis, keepdims=True)
    return (x - m) / jnp.sqrt(v + eps)

def _scatter_add(tgt, idx, src, axis=0):
    return tgt.at[idx].add(src)

def _segment_sum(src, seg, n):
    return jax.ops.segment_sum(src, seg, n)
kernel_name = 'mk_hybrid_d2_jaxref_r8_af8f7c'

def setup_inputs(seed: int=0):
    np.random.seed(seed)
    _w = jnp.asarray

    def _L0_attn_a_setup():
        import jax, jax.numpy as jnp
        import numpy as np
        D_MODEL = 128
        D_STATE = 16
        D_CONV = 4
        EXPAND = 2
        D_INNER = EXPAND * D_MODEL
        DT_MIN, DT_MAX = (0.001, 0.1)
        BATCH, SEQ = (4, 256)

        def _silu(v):
            return v * jax.nn.sigmoid(v)
        key = jax.random.key(seed)
        ks = jax.random.split(key, 5)
        x = jax.random.normal(ks[0], (BATCH, SEQ, D_MODEL), jnp.float32)
        W_in = jax.random.normal(ks[1], (2 * D_INNER, D_MODEL), jnp.float32) / np.sqrt(D_MODEL)
        conv_w = jax.random.normal(ks[2], (D_INNER, D_CONV), jnp.float32) / np.sqrt(D_CONV)
        conv_b = jnp.zeros((D_INNER,), jnp.float32)
        W_xproj = jax.random.normal(ks[3], (2 * D_STATE + 1, D_INNER), jnp.float32) / np.sqrt(D_INNER)
        A_log = jnp.log(jnp.arange(1, D_STATE + 1, dtype=jnp.float32))
        D_param = jnp.ones((D_INNER,), jnp.float32)
        W_out = jax.random.normal(ks[4], (D_MODEL, D_INNER), jnp.float32) / np.sqrt(D_INNER)
        return dict(x=x, W_in=W_in, conv_w=conv_w, conv_b=conv_b, W_xproj=W_xproj, A_log=A_log, D_param=D_param, W_out=W_out)
    _L0_attn_a_in = _L0_attn_a_setup()

    def _L0_attn_b_setup():
        import jax, jax.numpy as jnp
        import numpy as np
        NUM_HEADS = 32
        EPS = 1e-15
        key = jax.random.key(seed)
        k1, k2, k3, k4 = jax.random.split(key, 4)
        B, N, C = (8, 512, 128)
        x = jax.random.normal(k1, (B, N, C), dtype=jnp.float32)
        qkv_weight = jax.random.normal(k2, (3 * C, C), dtype=jnp.float32) * C ** (-0.5)
        proj_weight = jax.random.normal(k3, (C, C), dtype=jnp.float32) * C ** (-0.5)
        proj_bias = jax.random.normal(k4, (C,), dtype=jnp.float32) * 0.01
        return {'x': x, 'qkv_weight': qkv_weight, 'proj_weight': proj_weight, 'proj_bias': proj_bias}
    _L0_attn_b_in = _L0_attn_b_setup()

    def _L0_ffn_setup():
        import jax, jax.numpy as jnp
        import numpy as np
        B, L, D = (2, 256, 128)
        E = 15
        H = D * 1
        K = 3
        T = 1.0
        key = jax.random.key(seed)
        ks = jax.random.split(key, 12)
        s = 0.02
        return {'x': jax.random.normal(ks[0], (B, L, D), dtype=jnp.float32), 'router_W': jax.random.normal(ks[1], (D, E), dtype=jnp.float32) * s, 'router_b': jnp.zeros((E,), dtype=jnp.float32), 'sW1': jax.random.normal(ks[2], (D, H), dtype=jnp.float32) * s, 'sb1': jnp.zeros((H,), dtype=jnp.float32), 'sW2': jax.random.normal(ks[3], (H, D), dtype=jnp.float32) * s, 'sb2': jnp.zeros((D,), dtype=jnp.float32), 'eW1': jax.random.normal(ks[4], (E, D, H), dtype=jnp.float32) * s, 'eb1': jnp.zeros((E, H), dtype=jnp.float32), 'eW2': jax.random.normal(ks[5], (E, H, D), dtype=jnp.float32) * s, 'eb2': jnp.zeros((E, D), dtype=jnp.float32)}
    _L0_ffn_in = _L0_ffn_setup()

    def _L1_attn_a_setup():
        import jax, jax.numpy as jnp
        import numpy as np
        H = 128
        NH = 32
        D = H // NH
        M = 2
        BMIN, BMAX = (0.85, 0.9995)
        EPS = 1e-06
        ROPE_BASE = 10000.0
        LN_EPS = 1e-05

        def _rope(u, cos, sin):
            half = D // 2
            u1, u2 = (u[..., :half], u[..., half:])
            return jnp.concatenate([u1 * cos - u2 * sin, u1 * sin + u2 * cos], axis=-1)

        def _forward(x, Wq, Wk, Wv, Wbeta, bbeta, Wmix, bmix, Wout, bout, ln_g, ln_b):
            b, t, _ = x.shape
            q = (x @ Wq.T).reshape(b, t, NH, D)
            k = (x @ Wk.T).reshape(b, t, NH, D)
            v = (x @ Wv.T).reshape(b, t, NH, D)
            half = D // 2
            inv_freq = 1.0 / ROPE_BASE ** (jnp.arange(half, dtype=jnp.float32) / half)
            freqs = jnp.arange(t, dtype=jnp.float32)[:, None] * inv_freq
            cos = jnp.cos(freqs)[None, :, None, :]
            sin = jnp.sin(freqs)[None, :, None, :]
            q = _rope(q, cos, sin)
            k = _rope(k, cos, sin)
            phi_q = jax.nn.elu(q) + 1.0
            phi_k = jax.nn.elu(k) + 1.0
            beta = jnp.clip(jax.nn.sigmoid((x @ Wbeta.T + bbeta).reshape(b, t, NH, M)), BMIN, BMAX)
            mix = jax.nn.softmax((x @ Wmix.T + bmix).reshape(b, t, NH, M), axis=-1)

            def step(carry, xs):
                S, K = carry
                pq, pk, vt, bt, mt = xs
                K = K * bt[..., None] + pk[:, :, None, :]
                S = S * bt[..., None, None] + pk[:, :, None, :, None] * vt[:, :, None, None, :]
                num = jnp.einsum('bhd,bhmdc->bhmc', pq, S)
                den = jnp.einsum('bhd,bhmd->bhm', pq, K) + EPS
                y = jnp.sum(num / den[..., None] * mt[..., None], axis=2)
                return ((S, K), y)
            S0 = jnp.zeros((b, NH, M, D, D), x.dtype)
            K0 = jnp.zeros((b, NH, M, D), x.dtype)
            tf = lambda a: jnp.moveaxis(a, 1, 0)
            _, ys = jax.lax.scan(step, (S0, K0), (tf(phi_q), tf(phi_k), tf(v), tf(beta), tf(mix)))
            y = jnp.moveaxis(ys, 0, 1).reshape(b, t, H) @ Wout.T + bout
            z = x + y
            mu = z.mean(-1, keepdims=True)
            var = ((z - mu) ** 2).mean(-1, keepdims=True)
            return (z - mu) / jnp.sqrt(var + LN_EPS) * ln_g + ln_b
        key = jax.random.key(seed)
        ks = jax.random.split(key, 8)
        b, t = (4, 128)
        x = jax.random.normal(ks[0], (b, t, H), jnp.float32)
        sc = (6.0 / (H + H)) ** 0.5
        Wq = jax.random.uniform(ks[1], (H, H), jnp.float32, -sc, sc)
        Wk = jax.random.uniform(ks[2], (H, H), jnp.float32, -sc, sc)
        Wv = jax.random.uniform(ks[3], (H, H), jnp.float32, -sc, sc)
        Wout = jax.random.uniform(ks[4], (H, H), jnp.float32, -sc, sc)
        bout = jnp.zeros((H,), jnp.float32)
        scb = (6.0 / (H + NH * M)) ** 0.5
        Wbeta = jax.random.uniform(ks[5], (NH * M, H), jnp.float32, -scb, scb)
        targets = jnp.linspace(BMIN, BMAX, M)
        bbeta = jnp.tile(jnp.log(targets / (1.0 - targets)), NH)
        Wmix = jnp.zeros((NH * M, H), jnp.float32)
        bmix = jnp.zeros((NH * M,), jnp.float32)
        ln_g = jnp.ones((H,), jnp.float32)
        ln_b = jnp.zeros((H,), jnp.float32)
        return dict(x=x, Wq=Wq, Wk=Wk, Wv=Wv, Wbeta=Wbeta, bbeta=bbeta, Wmix=Wmix, bmix=bmix, Wout=Wout, bout=bout, ln_g=ln_g, ln_b=ln_b)
    _L1_attn_a_in = _L1_attn_a_setup()

    def _L1_attn_b_setup():
        import jax, jax.numpy as jnp
        import numpy as np
        from math import sqrt
        NUM_HEADS = 16
        key = jax.random.key(seed)
        ks = jax.random.split(key, 5)
        B, S, H = (2, 256, 128)
        scale = 0.02
        return {'x': jax.random.normal(ks[0], (B, S, H), dtype=jnp.float32), 'W_qkv': jax.random.normal(ks[1], (3 * H, H), dtype=jnp.float32) * scale, 'b_qkv': jax.random.normal(ks[2], (3 * H,), dtype=jnp.float32) * scale, 'W_o': jax.random.normal(ks[3], (H, H), dtype=jnp.float32) * scale, 'b_o': jax.random.normal(ks[4], (H,), dtype=jnp.float32) * scale}
    _L1_attn_b_in = _L1_attn_b_setup()

    def _L1_ffn_setup():
        import jax, jax.numpy as jnp
        import numpy as np
        B, L, D = (2, 256, 128)
        E = 15
        H = D * 1
        K = 3
        T = 1.0
        key = jax.random.key(seed)
        ks = jax.random.split(key, 12)
        s = 0.02
        return {'x': jax.random.normal(ks[0], (B, L, D), dtype=jnp.float32), 'router_W': jax.random.normal(ks[1], (D, E), dtype=jnp.float32) * s, 'router_b': jnp.zeros((E,), dtype=jnp.float32), 'sW1': jax.random.normal(ks[2], (D, H), dtype=jnp.float32) * s, 'sb1': jnp.zeros((H,), dtype=jnp.float32), 'sW2': jax.random.normal(ks[3], (H, D), dtype=jnp.float32) * s, 'sb2': jnp.zeros((D,), dtype=jnp.float32), 'eW1': jax.random.normal(ks[4], (E, D, H), dtype=jnp.float32) * s, 'eb1': jnp.zeros((E, H), dtype=jnp.float32), 'eW2': jax.random.normal(ks[5], (E, H, D), dtype=jnp.float32) * s, 'eb2': jnp.zeros((E, D), dtype=jnp.float32)}
    _L1_ffn_in = _L1_ffn_setup()
    _d = {'L0_attn_a_x': _L0_attn_a_in['x'], 'L0_attn_a_W_in': _L0_attn_a_in['W_in'], 'L0_attn_a_conv_w': _L0_attn_a_in['conv_w'], 'L0_attn_a_conv_b': _L0_attn_a_in['conv_b'], 'L0_attn_a_W_xproj': _L0_attn_a_in['W_xproj'], 'L0_attn_a_A_log': _L0_attn_a_in['A_log'], 'L0_attn_a_D_param': _L0_attn_a_in['D_param'], 'L0_attn_a_W_out': _L0_attn_a_in['W_out'], 'L0_attn_b_qkv_weight': _L0_attn_b_in['qkv_weight'], 'L0_attn_b_proj_weight': _L0_attn_b_in['proj_weight'], 'L0_attn_b_proj_bias': _L0_attn_b_in['proj_bias'], 'L0_ffn_router_W': _L0_ffn_in['router_W'], 'L0_ffn_router_b': _L0_ffn_in['router_b'], 'L0_ffn_sW1': _L0_ffn_in['sW1'], 'L0_ffn_sb1': _L0_ffn_in['sb1'], 'L0_ffn_sW2': _L0_ffn_in['sW2'], 'L0_ffn_sb2': _L0_ffn_in['sb2'], 'L0_ffn_eW1': _L0_ffn_in['eW1'], 'L0_ffn_eb1': _L0_ffn_in['eb1'], 'L0_ffn_eW2': _L0_ffn_in['eW2'], 'L0_ffn_eb2': _L0_ffn_in['eb2'], 'L1_attn_a_Wq': _L1_attn_a_in['Wq'], 'L1_attn_a_Wk': _L1_attn_a_in['Wk'], 'L1_attn_a_Wv': _L1_attn_a_in['Wv'], 'L1_attn_a_Wbeta': _L1_attn_a_in['Wbeta'], 'L1_attn_a_bbeta': _L1_attn_a_in['bbeta'], 'L1_attn_a_Wmix': _L1_attn_a_in['Wmix'], 'L1_attn_a_bmix': _L1_attn_a_in['bmix'], 'L1_attn_a_Wout': _L1_attn_a_in['Wout'], 'L1_attn_a_bout': _L1_attn_a_in['bout'], 'L1_attn_a_ln_g': _L1_attn_a_in['ln_g'], 'L1_attn_a_ln_b': _L1_attn_a_in['ln_b'], 'L1_attn_b_W_qkv': _L1_attn_b_in['W_qkv'], 'L1_attn_b_b_qkv': _L1_attn_b_in['b_qkv'], 'L1_attn_b_W_o': _L1_attn_b_in['W_o'], 'L1_attn_b_b_o': _L1_attn_b_in['b_o'], 'L1_ffn_router_W': _L1_ffn_in['router_W'], 'L1_ffn_router_b': _L1_ffn_in['router_b'], 'L1_ffn_sW1': _L1_ffn_in['sW1'], 'L1_ffn_sb1': _L1_ffn_in['sb1'], 'L1_ffn_sW2': _L1_ffn_in['sW2'], 'L1_ffn_sb2': _L1_ffn_in['sb2'], 'L1_ffn_eW1': _L1_ffn_in['eW1'], 'L1_ffn_eb1': _L1_ffn_in['eb1'], 'L1_ffn_eW2': _L1_ffn_in['eW2'], 'L1_ffn_eb2': _L1_ffn_in['eb2']}
    _x0 = _d['L0_attn_a_x']
    _d['L0_attn_a_x'] = jax.random.normal(jax.random.fold_in(jax.random.key(seed), 1), (4, 1024, 128), dtype=_x0.dtype)
    del _x0
    return _d

def reference(L0_attn_a_x, L0_attn_a_W_in, L0_attn_a_conv_w, L0_attn_a_conv_b, L0_attn_a_W_xproj, L0_attn_a_A_log, L0_attn_a_D_param, L0_attn_a_W_out, L0_attn_b_qkv_weight, L0_attn_b_proj_weight, L0_attn_b_proj_bias, L0_ffn_router_W, L0_ffn_router_b, L0_ffn_sW1, L0_ffn_sb1, L0_ffn_sW2, L0_ffn_sb2, L0_ffn_eW1, L0_ffn_eb1, L0_ffn_eW2, L0_ffn_eb2, L1_attn_a_Wq, L1_attn_a_Wk, L1_attn_a_Wv, L1_attn_a_Wbeta, L1_attn_a_bbeta, L1_attn_a_Wmix, L1_attn_a_bmix, L1_attn_a_Wout, L1_attn_a_bout, L1_attn_a_ln_g, L1_attn_a_ln_b, L1_attn_b_W_qkv, L1_attn_b_b_qkv, L1_attn_b_W_o, L1_attn_b_b_o, L1_ffn_router_W, L1_ffn_router_b, L1_ffn_sW1, L1_ffn_sb1, L1_ffn_sW2, L1_ffn_sb2, L1_ffn_eW1, L1_ffn_eb1, L1_ffn_eW2, L1_ffn_eb2):

    def _L0_attn_a_ref(x, W_in, conv_w, conv_b, W_xproj, A_log, D_param, W_out):
        import jax, jax.numpy as jnp
        import numpy as np
        D_MODEL = 128
        D_STATE = 16
        D_CONV = 4
        EXPAND = 2
        D_INNER = EXPAND * D_MODEL
        DT_MIN, DT_MAX = (0.001, 0.1)
        BATCH, SEQ = (4, 256)

        def _silu(v):
            return v * jax.nn.sigmoid(v)
        b, l, d = x.shape
        xz = x @ W_in.T
        x_proj, z = jnp.split(xz, 2, axis=-1)
        xp = jnp.pad(x_proj, ((0, 0), (D_CONV - 1, 0), (0, 0)))
        x_conv = conv_b + sum((xp[:, k:k + l, :] * conv_w[:, k] for k in range(D_CONV)))
        x_conv = _silu(x_conv)
        x_dbl = x_conv @ W_xproj.T
        Bmat = x_dbl[..., :D_STATE]
        Cmat = x_dbl[..., D_STATE:2 * D_STATE]
        dt = jnp.clip(jax.nn.softplus(x_dbl[..., -1]), DT_MIN, DT_MAX)
        A = -jnp.exp(A_log)

        def step(h, inp):
            x_t, dt_t, B_t, C_t = inp
            dt_A = jnp.clip(dt_t[:, None] * A, -20.0, 0.0)
            A_bar = jnp.exp(dt_A)[:, None, :]
            B_bar = jnp.clip(dt_t[:, None] * B_t, -10.0, 10.0)[:, None, :]
            h = jnp.clip(A_bar * h + B_bar * x_t[:, :, None], -100.0, 100.0)
            y_t = jnp.einsum('bds,bs->bd', h, C_t)
            return (h, y_t)
        h0 = jnp.zeros((b, D_INNER, D_STATE), x.dtype)
        xs = (jnp.swapaxes(x_conv, 0, 1), jnp.swapaxes(dt, 0, 1), jnp.swapaxes(Bmat, 0, 1), jnp.swapaxes(Cmat, 0, 1))
        _, ys = jax.lax.scan(step, h0, xs)
        y = jnp.swapaxes(ys, 0, 1)
        y = y * _silu(z) + x_conv * D_param
        return y @ W_out.T

    def _L0_attn_b_ref(x, qkv_weight, proj_weight, proj_bias):
        import jax, jax.numpy as jnp
        import numpy as np
        NUM_HEADS = 32
        EPS = 1e-15
        B, N, C = x.shape
        H = NUM_HEADS
        D = C // H
        qkv = jax.nn.relu(jnp.einsum('bnc,oc->bno', x, qkv_weight))
        qkv = qkv.reshape(B, N, 3, H, D)
        q, k, v = (qkv[:, :, 0], qkv[:, :, 1], qkv[:, :, 2])
        v_pad = jnp.concatenate([v, jnp.ones((B, N, H, 1), dtype=v.dtype)], axis=-1)
        vk = jnp.einsum('bnhe,bnhd->bhed', v_pad.astype(jnp.float32), k.astype(jnp.float32))
        vk_q = jnp.einsum('bhed,bnhd->bnhe', vk, q.astype(jnp.float32))
        proj_input = (vk_q[..., :D] / (vk_q[..., D:] + EPS)).astype(qkv.dtype)
        proj_input = proj_input.reshape(B, N, C)
        y = jnp.einsum('bnc,oc->bno', proj_input, proj_weight) + proj_bias
        return y

    def _L0_ffn_ref(x, router_W, router_b, sW1, sb1, sW2, sb2, eW1, eb1, eW2, eb2):
        import jax, jax.numpy as jnp
        import numpy as np
        B, L, D = (2, 256, 128)
        E = 15
        H = D * 1
        K = 3
        T = 1.0
        b, l, d = x.shape
        n = b * l
        xt = x.reshape(n, d)
        shared = jax.nn.relu(xt @ sW1 + sb1) @ sW2 + sb2
        logits = xt @ router_W + router_b
        probs = jax.nn.softmax(logits / T, axis=-1)
        top_p, top_i = jax.lax.top_k(probs, K)
        cw = jnp.zeros((n, E), dtype=probs.dtype)
        cw = cw.at[jnp.arange(n)[:, None], top_i].set(top_p)
        h = jax.nn.relu(jnp.einsum('nd,edh->neh', xt, eW1) + eb1)
        ye = jnp.einsum('neh,ehd->ned', h, eW2) + eb2
        routed = jnp.einsum('ned,ne->nd', ye, cw)
        return (shared + routed).reshape(b, l, d)

    def _L1_attn_a_ref(x, Wq, Wk, Wv, Wbeta, bbeta, Wmix, bmix, Wout, bout, ln_g, ln_b):
        import jax, jax.numpy as jnp
        import numpy as np
        H = 128
        NH = 32
        D = H // NH
        M = 2
        BMIN, BMAX = (0.85, 0.9995)
        EPS = 1e-06
        ROPE_BASE = 10000.0
        LN_EPS = 1e-05

        def _rope(u, cos, sin):
            half = D // 2
            u1, u2 = (u[..., :half], u[..., half:])
            return jnp.concatenate([u1 * cos - u2 * sin, u1 * sin + u2 * cos], axis=-1)

        def _forward(x, Wq, Wk, Wv, Wbeta, bbeta, Wmix, bmix, Wout, bout, ln_g, ln_b):
            b, t, _ = x.shape
            q = (x @ Wq.T).reshape(b, t, NH, D)
            k = (x @ Wk.T).reshape(b, t, NH, D)
            v = (x @ Wv.T).reshape(b, t, NH, D)
            half = D // 2
            inv_freq = 1.0 / ROPE_BASE ** (jnp.arange(half, dtype=jnp.float32) / half)
            freqs = jnp.arange(t, dtype=jnp.float32)[:, None] * inv_freq
            cos = jnp.cos(freqs)[None, :, None, :]
            sin = jnp.sin(freqs)[None, :, None, :]
            q = _rope(q, cos, sin)
            k = _rope(k, cos, sin)
            phi_q = jax.nn.elu(q) + 1.0
            phi_k = jax.nn.elu(k) + 1.0
            beta = jnp.clip(jax.nn.sigmoid((x @ Wbeta.T + bbeta).reshape(b, t, NH, M)), BMIN, BMAX)
            mix = jax.nn.softmax((x @ Wmix.T + bmix).reshape(b, t, NH, M), axis=-1)

            def step(carry, xs):
                S, K = carry
                pq, pk, vt, bt, mt = xs
                K = K * bt[..., None] + pk[:, :, None, :]
                S = S * bt[..., None, None] + pk[:, :, None, :, None] * vt[:, :, None, None, :]
                num = jnp.einsum('bhd,bhmdc->bhmc', pq, S)
                den = jnp.einsum('bhd,bhmd->bhm', pq, K) + EPS
                y = jnp.sum(num / den[..., None] * mt[..., None], axis=2)
                return ((S, K), y)
            S0 = jnp.zeros((b, NH, M, D, D), x.dtype)
            K0 = jnp.zeros((b, NH, M, D), x.dtype)
            tf = lambda a: jnp.moveaxis(a, 1, 0)
            _, ys = jax.lax.scan(step, (S0, K0), (tf(phi_q), tf(phi_k), tf(v), tf(beta), tf(mix)))
            y = jnp.moveaxis(ys, 0, 1).reshape(b, t, H) @ Wout.T + bout
            z = x + y
            mu = z.mean(-1, keepdims=True)
            var = ((z - mu) ** 2).mean(-1, keepdims=True)
            return (z - mu) / jnp.sqrt(var + LN_EPS) * ln_g + ln_b
        return _forward(x, Wq, Wk, Wv, Wbeta, bbeta, Wmix, bmix, Wout, bout, ln_g, ln_b)

    def _L1_attn_b_ref(x, W_qkv, b_qkv, W_o, b_o):
        import jax, jax.numpy as jnp
        import numpy as np
        from math import sqrt
        NUM_HEADS = 16
        B, S, H = x.shape
        nh = NUM_HEADS
        hd = H // nh
        qkv = x @ W_qkv.T + b_qkv
        Q, K, V = (qkv[..., :H], qkv[..., H:2 * H], qkv[..., 2 * H:])
        Q = Q.reshape(B, S, nh, hd)
        K = K.reshape(B, S, nh, hd)
        V = V.reshape(B, S, nh, hd)
        scores = jnp.einsum('bqhd,bkhd->bhqk', Q, K)
        causal = jnp.tril(jnp.ones((S, S), dtype=bool))
        scores = jnp.where(causal, scores, -jnp.inf)
        probs = jax.nn.softmax(scores / sqrt(hd), axis=-1)
        out = jnp.einsum('bkhd,bhqk->bqhd', V, probs)
        out = out.reshape(B, S, H)
        return out @ W_o.T + b_o

    def _L1_ffn_ref(x, router_W, router_b, sW1, sb1, sW2, sb2, eW1, eb1, eW2, eb2):
        import jax, jax.numpy as jnp
        import numpy as np
        B, L, D = (2, 256, 128)
        E = 15
        H = D * 1
        K = 3
        T = 1.0
        b, l, d = x.shape
        n = b * l
        xt = x.reshape(n, d)
        shared = jax.nn.relu(xt @ sW1 + sb1) @ sW2 + sb2
        logits = xt @ router_W + router_b
        probs = jax.nn.softmax(logits / T, axis=-1)
        top_p, top_i = jax.lax.top_k(probs, K)
        cw = jnp.zeros((n, E), dtype=probs.dtype)
        cw = cw.at[jnp.arange(n)[:, None], top_i].set(top_p)
        h = jax.nn.relu(jnp.einsum('nd,edh->neh', xt, eW1) + eb1)
        ye = jnp.einsum('neh,ehd->ned', h, eW2) + eb2
        routed = jnp.einsum('ned,ne->nd', ye, cw)
        return (shared + routed).reshape(b, l, d)
    x = L0_attn_a_x
    x = x + _L0_attn_a_ref(_layernorm(x, axis=-1), L0_attn_a_W_in, L0_attn_a_conv_w, L0_attn_a_conv_b, L0_attn_a_W_xproj, L0_attn_a_A_log, L0_attn_a_D_param, L0_attn_a_W_out)
    x = x + _L0_ffn_ref(_layernorm(x, axis=-1), L0_ffn_router_W, L0_ffn_router_b, L0_ffn_sW1, L0_ffn_sb1, L0_ffn_sW2, L0_ffn_sb2, L0_ffn_eW1, L0_ffn_eb1, L0_ffn_eW2, L0_ffn_eb2)
    x = x + _L0_attn_b_ref(_layernorm(x, axis=-1), L0_attn_b_qkv_weight, L0_attn_b_proj_weight, L0_attn_b_proj_bias)
    x = x + _L0_ffn_ref(_layernorm(x, axis=-1), L0_ffn_router_W, L0_ffn_router_b, L0_ffn_sW1, L0_ffn_sb1, L0_ffn_sW2, L0_ffn_sb2, L0_ffn_eW1, L0_ffn_eb1, L0_ffn_eW2, L0_ffn_eb2)
    x = x + _L1_attn_a_ref(_layernorm(x, axis=-1), L1_attn_a_Wq, L1_attn_a_Wk, L1_attn_a_Wv, L1_attn_a_Wbeta, L1_attn_a_bbeta, L1_attn_a_Wmix, L1_attn_a_bmix, L1_attn_a_Wout, L1_attn_a_bout, L1_attn_a_ln_g, L1_attn_a_ln_b)
    x = x + _L1_ffn_ref(_layernorm(x, axis=-1), L1_ffn_router_W, L1_ffn_router_b, L1_ffn_sW1, L1_ffn_sb1, L1_ffn_sW2, L1_ffn_sb2, L1_ffn_eW1, L1_ffn_eb1, L1_ffn_eW2, L1_ffn_eb2)
    x = x + _L1_attn_b_ref(_layernorm(x, axis=-1), L1_attn_b_W_qkv, L1_attn_b_b_qkv, L1_attn_b_W_o, L1_attn_b_b_o)
    x = x + _L1_ffn_ref(_layernorm(x, axis=-1), L1_ffn_router_W, L1_ffn_router_b, L1_ffn_sW1, L1_ffn_sb1, L1_ffn_sW2, L1_ffn_sb2, L1_ffn_eW1, L1_ffn_eb1, L1_ffn_eW2, L1_ffn_eb2)
    return x

_drawn_inputs = setup_inputs


def setup_inputs(seed=0):
    import zlib

    import numpy as np

    out = dict(_drawn_inputs(seed))
    spreads = {'L0_attn_a_conv_b': (0.0, 0.1),
     'L0_attn_a_D_param': (1.0, 0.2),
     'L0_ffn_router_b': (0.0, 0.497),
     'L0_ffn_sb1': (0.0, 0.304),
     'L0_ffn_sb2': (0.0, 0.1),
     'L0_ffn_eb1': (0.0, 0.8),
     'L0_ffn_eb2': (0.0, 0.297),
     'L1_attn_a_Wmix': (0.0, 0.295),
     'L1_attn_a_bmix': (0.0, 0.8),
     'L1_attn_a_bout': (0.0, 0.1),
     'L1_attn_a_ln_g': (1.0, 0.2),
     'L1_attn_a_ln_b': (0.0, 0.1),
     'L1_ffn_router_b': (0.0, 0.8),
     'L1_ffn_sb1': (0.0, 0.579),
     'L1_ffn_sb2': (0.0, 0.1),
     'L1_ffn_eb1': (0.0, 0.8),
     'L1_ffn_eb2': (0.0, 0.543)}
    factors = {'L0_attn_b_proj_bias': 6.449,
     'L0_ffn_eW1': 5.996,
     'L0_ffn_eW2': 4.756,
     'L1_attn_a_Wq': 4.783,
     'L1_attn_a_Wbeta': 7.875,
     'L1_attn_b_W_qkv': 5.284,
     'L1_attn_b_b_qkv': 8.0,
     'L1_attn_b_W_o': 5.767,
     'L1_attn_b_b_o': 6.233,
     'L1_ffn_router_W': 4.636,
     'L1_ffn_eW1': 8.0,
     'L1_ffn_eW2': 8.0}
    for name, (base, spread) in spreads.items():
        noise = np.random.default_rng([zlib.crc32(name.encode()), seed]).standard_normal(out[name].shape)
        drawn = base * np.exp(spread * noise) if base else spread * noise
        out[name] = jnp.asarray(drawn.astype(out[name].dtype))
    for name, factor in factors.items():
        out[name] = (out[name] * factor).astype(out[name].dtype)
    return out
```

```python
from contextlib import ExitStack

import numpy as np

import concourse.bass as bass
from concourse import mybir

P = 128
BATCH, SEQ = 4, 1024
TILES = BATCH * SEQ // P
TPB = SEQ // P
GT = 4
BLK = GT * P
BLOCKS = TILES // GT
LN_EPS = 1e-5

F32 = mybir.dt.float32
BF16 = mybir.dt.bfloat16
I32 = mybir.dt.int32
ALU = mybir.AluOpType
ACT = mybir.ActivationFunctionType
AX = mybir.AxisListType

class Chain:

    def __init__(self, eng, sem, base=0):
        self.eng, self.sem, self.base, self.n = eng, sem, base, 0

    def link(self, ins):
        self.n += 1
        ins.then_inc(self.sem, 1)
        self.eng.wait_ge(self.sem, self.base + self.n)

class Banks:

    def __init__(self, psum):
        self.psum, self.taken = psum, 0

    def take(self, *dims):
        n = int(np.prod(dims)) // BLK
        banks = self.psum[:, self.taken:self.taken + n, :].rearrange("p n k -> p (n k)")
        self.taken += n
        letters = " ".join("abcd"[:len(dims)])
        return banks.rearrange(f"p ({letters}) -> p {letters}", **dict(zip("abcd", dims)))

def wide(col, n):
    return col.unsqueeze(len(col.shape)).to_broadcast(list(col.shape) + [n])

def shape_constants():
    HOST_BF16 = mybir.dt.np(BF16)
    ident = np.eye(P, dtype=np.float32)
    d = np.arange(P) % 4
    inv_freq = (np.float32(1.0) / np.float32(10000.0) ** (np.arange(2, dtype=np.float32) / np.float32(2))).astype(np.float32)
    angle = np.arange(SEQ, dtype=np.float32)[None, :] * inv_freq[d % 2][:, None]
    gather4 = np.zeros((P, 4, P), np.float32)
    for c in range(4):
        for i in range(P):
            gather4[i, c, i // 4 * 4 + c] = 1
    later = np.triu(np.ones((P, P), np.float32), 1)
    minus = np.float32(-1e30)
    t = np.arange(P)
    chunk, middle = t // 32, t // 32 * 32 + 15
    same = chunk[:, None] == chunk[None, :]
    before_mid = (same & (t[:, None] <= middle[None, :])).astype(np.float32)
    to_target = (same & (t[:, None] <= t[None, :])).astype(np.float32)
    totals = (chunk[:, None] == np.arange(4)[None, :]).astype(np.float32)
    return {
        "const": {
            "ident": ident,
            "ones": np.ones((1, BLK), np.float32),
            "minus_half": np.full((P, 8), -0.5, np.float32),
            "head4": np.kron(np.eye(P // 4, dtype=np.float32), np.ones((4, 4), np.float32)),
            "order": np.tile(np.arange(15, 0, -1, dtype=np.float32), (P, GT, 1)),
        },
        "mamba": {
            "sum_mid": to_target - before_mid,
            "sum_rest": (same & (t[:, None] > t[None, :])).astype(np.float32),
            "sum_sel": np.concatenate([totals, totals * (t <= middle).astype(np.float32)[:, None]], axis=1),
            "chunk_mask": totals,
            "chunk_causal": to_target,
            "ones_col": np.ones((P, 1), np.float32),
        },
        "ret": {
            "gather4": gather4,
            "cos": np.cos(angle),
            "sin": np.sin(angle) * np.where(d < 2, -1, 1).astype(np.float32)[:, None],
        },
        "soft": {
            "ident_bf": ident.astype(HOST_BF16),
            "causal_kq": (later.T * minus).astype(HOST_BF16),
            "causal_qk": (later * minus).astype(HOST_BF16),
            "dram_zero": np.zeros((1, 8 * SEQ), HOST_BF16),
            "dram_one": np.ones((1, 8 * SEQ), HOST_BF16),
        },
    }

class Prenorm:

    def __init__(self, nc, ctx, const, x, name, xt_ps, parities=2):
        self.nc, self.const, self.x = nc, const, x

        def sb(n, shape):
            return ctx.enter_context(nc.sbuf_tensor(f"{name}_{n}", shape, F32))

        def sem(n):
            return nc.alloc_semaphore(f"{name}_{n}")

        self.stats = sb("stats", [P, GT, 6])
        self.mv = sb("mv", [P, GT, 2])
        self.rstd = sb("rstd", [P, GT])
        self.pause = sb("pause", [1, 1])
        self.xn = sb("xn", [P, GT, P])
        self.xt = sb("xt", [P, parities, BLK])
        self.xt_ps = xt_ps
        self.stat_link, self.stats_ready = sem("stat_link"), sem("stats_ready")
        self.rstd_ready, self.xn_ready = sem("rstd_ready"), sem("xn_ready")
        self.xt_ps_ready, self.xt_ready = sem("xt_ps_ready"), sem("xt_ready")

    def statistics(self, dve, q, tile=None):
        tile = tile or (lambda j: q * GT + j)
        dve.wait_ge(self.xn_ready, q)
        for j in range(GT):
            ins = self.nc.vector.bn_stats(self.stats[:, j, :], self.x[:, tile(j), :])
        ins.then_inc(self.stat_link, 1)
        dve.wait_ge(self.stat_link, 2 * q + 1)
        self.nc.vector.memset(self.pause[:, :], 0.0)
        for j in range(GT):
            ins = self.nc.vector.bn_aggr(self.mv[:, j, :], self.stats[:, j, :])
        ins.then_inc(self.stat_link, 1)
        dve.wait_ge(self.stat_link, 2 * q + 2)
        self.nc.vector.tensor_scalar_add(self.mv[:, :, 1], self.mv[:, :, 1], LN_EPS).then_inc(self.stats_ready, 1)

    def invert(self, pool, q):
        pool.wait_ge(self.stats_ready, q + 1)
        self.nc.gpsimd.tensor_tensor(self.rstd[:, :], self.mv[:, :, 1], self.const["minus_half"][:, 0:GT],
                                     ALU.pow).then_inc(self.rstd_ready, 1)

    def scale(self, dve, q, tile=None, xn_used=None, xn_free=None):
        tile = tile or (lambda j: q * GT + j)
        dve.wait_ge(self.rstd_ready, q + 1)
        dve.wait_ge(xn_free if xn_free is not None else self.xt_ps_ready, q)
        if xn_used is not None:
            dve.wait_ge(xn_used, q)
        for j in range(GT):
            ins = self.nc.vector.tensor_scalar(self.xn[:, j, :], self.x[:, tile(j), :], self.mv[:, j, 0:1],
                                               self.rstd[:, j:j + 1], ALU.subtract, ALU.mult)
        ins.then_inc(self.xn_ready, 1)

    def transpose(self, pe, q):
        pe.wait_ge(self.xn_ready, q + 1)
        pe.wait_ge(self.xt_ready, q)
        for j in range(GT):
            ins = pe.transpose(self.xt_ps[:, j, :], self.xn[:, j, :], self.const["ident"][:, :])
        ins.then_inc(self.xt_ps_ready, 1)

    def copy(self, act, q, p, xt_used=None):
        act.wait_ge(self.xt_ps_ready, q + 1)
        if xt_used is not None:
            act.wait_ge(*xt_used)
        self.nc.scalar.copy(self.xt[:, p, :], self.xt_ps[:, :, :]).then_inc(self.xt_ready, 1)

NS = 16
SW = 32
DI = 2 * P
HALVES = 2
CONV = 4
CHUNK = 32
CHUNKS = P // CHUNK
NDBL = 2 * NS + 1
DT_MIN, DT_MAX = 0.001, 0.1
DECAY_FLOOR, INPUT_CLIP, STATE_CLIP = -20.0, 10.0, 100.0
STATE_PROVED, LOG_PROVED = 99.0, 40.0
DT_LO, DT_HI = -8.0, -2.2
STEP_ROWS = 16

def mamba_stage(nc, x, const, w, loaded, name):
    with ExitStack() as ctx:
        def sb(n, shape, dt=F32):
            return ctx.enter_context(nc.sbuf_tensor(f"{name}_{n}", shape, dt))

        def sem(n):
            return nc.alloc_semaphore(f"{name}_{n}")

        y = sb("y", [P, HALVES, BATCH, SEQ])
        gate = sb("gate", [P, HALVES, BATCH, SEQ])
        xc = sb("xc", [P, HALVES, BATCH, SEQ])
        flag = sb("flag", [1, 1], I32)
        coef_dram = nc.dram_tensor(f"{name}_coef_dram", [SEQ, 3 * BATCH * NS], F32, kind="Internal").ap()
        mamba_scan(nc, x, const, w, loaded, name, y, gate, xc, flag, coef_dram)
        mamba_steps(nc, name, y, xc, flag, coef_dram)
        mamba_output(nc, x, const, w, name, y, gate, xc)

def mamba_scan(nc, x, const, w, loaded, name, y, gate, xc, flag, coef_dram):
    with ExitStack() as ctx:
        def sb(n, shape, dt=F32):
            return ctx.enter_context(nc.sbuf_tensor(f"{name}_{n}", shape, dt))

        def sem(n):
            return nc.alloc_semaphore(f"{name}_{n}")

        banks = Banks(const["psum"])
        tr_ps = banks.take(GT, P)
        ring_ps = banks.take(2, BATCH, P)
        small_ps = banks.take(BLK)
        g_ps = tr_ps
        y_ps = banks.take(HALVES, BATCH, P)
        u_ps = banks.take(CHUNKS, DI)
        DBL, CUM, REST, SEL = 0, 160, 288, 416
        norm = Prenorm(nc, ctx, const, x, name + "_n", parities=1, xt_ps=tr_ps)

        xp = sb("xp", [P, HALVES, BATCH, CONV - 1 + P])
        tz = sb("tz", [P, HALVES, BATCH, P])
        cv = sb("cv", [P, HALVES, BATCH, P])
        tc = sb("tc", [P, HALVES, BATCH, P])
        xc_now = sb("xc_now", [P, HALVES, BATCH, P])
        xtok = sb("xtok", [P, BATCH, DI])
        dbl = sb("dbl", [P, BATCH, NDBL])
        dt1 = sb("dt1", [P, 6, BATCH])
        la = sb("la", [P, BATCH, SW])
        bbar = sb("bbar", [P, BATCH, SW])
        cc = sb("cc", [P, BATCH, SW])
        cum = sb("cum", [P, BATCH * SW])
        e_pos = sb("e_pos", [P, BATCH * SW])
        e_neg = sb("e_neg", [P, BATCH * SW])
        e_rest = sb("e_rest", [P, BATCH * SW])
        coef = sb("coef", [P, 4, BATCH * SW])
        wk = sb("wk", [P, CHUNKS, BATCH * SW])
        out_coef = sb("out_coef", [P, 3, BATCH, NS])
        bt = sb("bt", [P, P])
        ct = sb("ct", [P, BATCH, P])
        bound_a = sb("bound_a", [P, SEQ])
        bound_v = sb("bound_v", [P, SEQ])
        gt = sb("gt", [P, BATCH, P])
        sel = sb("sel", [P, 2 * CHUNKS])
        hm = sb("hm", [P, CHUNKS, DI])
        h = sb("h", [P, CHUNKS, DI])
        umax = sb("umax", [P, BATCH])
        cmax = sb("cmax", [P, TPB])
        verdict = sb("verdict", [P, 4])
        neg_a = sb("neg_a", [P, NS])

        init_done, a_ready = sem("init_done"), sem("a_ready")
        ring_ready, ring_used = sem("ring_ready"), sem("ring_used")
        halo_done, xp_ready, tz_done, cv_ready = sem("halo_done"), sem("xp_ready"), sem("tz_done"), sem("cv_ready")
        tc_done, xc2_ready, xc_ready, kept = sem("tc_done"), sem("xc2_ready"), sem("xc_ready"), sem("kept")
        dbl_ready, dtexp_ready, dtexp_done = sem("dbl_ready"), sem("dtexp_ready"), sem("dtexp_done")
        la_ready, sums_ready, cum_ready, exps_done = sem("la_ready"), sem("sums_ready"), sem("cum_ready"), sem("exps_done")
        coef_ready, tr_ready, tr_used = sem("coef_ready"), sem("tr_ready"), sem("tr_used")
        g_ready, gt_ready, u_ready, state_link = sem("g_ready"), sem("gt_ready"), sem("u_ready"), sem("state_link")
        hm_ready, y_ready, y_copied = sem("hm_ready"), sem("y_ready"), sem("y_copied")
        link_sem, coef_stored, verdict_ready, sum_ready, flag_ready = (
            sem("link"), sem("coef_stored"), sem("verdict_ready"), sem("sum_ready"), sem("flag_ready"))
        out_coef_ready = sem("out_coef_ready")

        block = ctx.enter_context(nc.Block())
        RING = 6

        @block.sync
        def _(sp):
            with sp.Fori(0, TPB) as tt:
                sp.wait_ge(out_coef_ready, tt + 1)
                sp.dma_start(coef_dram[bass.ds(tt * P, P), :], out_coef[:, :, :, :]).then_inc(coef_stored, 16)
            sp.wait_ge(coef_stored, 16 * TPB)

        @block.gpsimd
        def _(pool):
            nc.gpsimd.memset(la[:, :, :], 0.0)
            nc.gpsimd.memset(bbar[:, :, :], 0.0)
            nc.gpsimd.memset(cc[:, :, :], 0.0)
            nc.gpsimd.memset(ct[:, :, :], 0.0)
            nc.gpsimd.memset(h[:, :, :], 0.0)
            nc.gpsimd.memset(xp[:, :, :, 0:CONV - 1], 0.0).then_inc(init_done, 1)
            with pool.Fori(0, TPB) as tt:
                norm.invert(pool, tt)
                pool.wait_ge(init_done, 1)
                pool.wait_ge(xc_ready, tt + 1)
                nc.gpsimd.tensor_copy(xc[:, :, :, bass.ds(tt * P, P)], xc_now[:, :, :, :]).then_inc(kept, 1)

        @block.tensor
        def _(pe):
            pe.wait_ge(*loaded)
            pe.wait_ge(init_done, 1)
            with pe.Fori(0, TPB) as tt:
                pe.wait_ge(norm.xn_ready, tt + 1)
                pe.wait_ge(gt_ready, tt)
                for j in range(BATCH):
                    ins = pe.transpose(tr_ps[:, j, :], norm.xn[:, j, :], const["ident"][:, :])
                ins.then_inc(norm.xt_ps_ready, 1)
                pe.wait_ge(norm.xt_ready, tt + 1)
                for i in range(2 * HALVES):
                    pe.wait_ge(ring_used, RING * tt + max(i - 1, 0))
                    pe.matmul(ring_ps[:, i % 2, :, :], w["in"][:, i, :], norm.xt[:, 0, :], start=True, stop=True)\
                        .then_inc(ring_ready, 1)
                pe.wait_ge(xc_ready, tt + 1)
                for b in range(BATCH):
                    for i in range(HALVES):
                        ins = pe.matmul(small_ps[:, DBL + NDBL * b:DBL + NDBL * (b + 1)], xc_now[:, i, b, :],
                                        w["xproj"][:, i, :], start=(i == 0), stop=(i == HALVES - 1), skip_group_check=True)
                ins.then_inc(dbl_ready, 1)
                for i in range(HALVES):
                    pe.wait_ge(ring_used, RING * tt + 4 + i - 1)
                    for b in range(BATCH):
                        ins = pe.transpose(ring_ps[:, i, b, :], xc_now[:, i, b, :], const["ident"][:, :])
                    ins.then_inc(ring_ready, 1)
                pe.wait_ge(la_ready, tt + 1)
                pe.matmul(small_ps[:, CUM:CUM + P], w["sum_mid"][:, :], la[:, :, :], start=True, stop=True,
                          skip_group_check=True)
                pe.matmul(small_ps[:, REST:REST + P], w["sum_rest"][:, :], la[:, :, :], start=True, stop=True,
                          skip_group_check=True)
                pe.matmul(small_ps[:, SEL:SEL + 2 * CHUNKS], la[:, :, :], w["sum_sel"][:, :], start=True, stop=True,
                          skip_group_check=True).then_inc(sums_ready, 1)
                pe.wait_ge(coef_ready, tt + 1)
                for i in range(4):
                    ins = pe.transpose(tr_ps[:, i, :], coef[:, i, :], const["ident"][:, :])
                ins.then_inc(tr_ready, 1)
                pe.wait_ge(tr_used, tt + 1)
                pe.matmul(g_ps[:, :, :], bt[:, :], ct[:, :, :], start=True, stop=True).then_inc(g_ready, 1)
                pe.wait_ge(ring_used, RING * (tt + 1))
                for b in range(BATCH):
                    for k in range(CHUNKS):
                        ins = pe.matmul(u_ps[SW * b:SW * (b + 1), k, :], wk[:, k, SW * b:SW * (b + 1)], xtok[:, b, :],
                                        start=True, stop=True, skip_group_check=True, tile_position=(0, SW * b))
                ins.then_inc(u_ready, 1)
                pe.wait_ge(gt_ready, tt + 1)
                pe.wait_ge(y_copied, tt)
                for i in range(HALVES):
                    for b in range(BATCH):
                        pe.matmul(y_ps[:, i, b, :], xtok[:, b, P * i:P * (i + 1)], gt[:, b, :],
                                  start=(b == 0), stop=False, skip_group_check=True)
                pe.wait_ge(hm_ready, tt + 1)
                for i in range(HALVES):
                    for k in range(CHUNKS):
                        cols = slice(CHUNK * k, CHUNK * (k + 1))
                        ins = pe.matmul(y_ps[:, i, :, cols], hm[:, k, P * i:P * (i + 1)], ct[:, :, cols],
                                        start=False, stop=(k == CHUNKS - 1), skip_group_check=True)
                ins.then_inc(y_ready, 1)
            pe.wait_ge(verdict_ready, 1)
            pe.matmul(small_ps[0:1, 0:1], verdict[:, 3:4], w["ones_col"][:, :], start=True, stop=True)\
                .then_inc(sum_ready, 1)

        @block.scalar
        def _(act):
            act.wait_ge(*loaded)
            act.wait_ge(init_done, 1)
            nc.scalar.activation(neg_a[:, :], w["a_log"][:, :], ACT.Exp).then_inc(a_ready, 1)
            with act.Fori(0, TPB) as tt:
                norm.copy(act, tt, 0)
                for i in range(HALVES):
                    act.wait_ge(ring_ready, RING * tt + i + 1)
                    act.wait_ge(halo_done, tt)
                    nc.scalar.copy(xp[:, i, :, CONV - 1:], ring_ps[:, i, :, :]).then_inc(ring_used, 1)
                for i in range(HALVES):
                    act.wait_ge(ring_ready, RING * tt + 2 + i + 1)
                    nc.scalar.activation(tz[:, i, :, :], ring_ps[:, i, :, :], ACT.Tanh, scale=0.5).then_inc(tz_done, 1)
                for i in range(HALVES):
                    act.wait_ge(cv_ready, HALVES * tt + i + 1)
                    nc.scalar.activation(tc[:, i, :, :], cv[:, i, :, :], ACT.Tanh, scale=0.5).then_inc(tc_done, 1)
                act.wait_ge(xc2_ready, tt + 1)
                act.wait_ge(kept, tt)
                nc.scalar.mul(xc_now[:, :, :, :], tc[:, :, :, :], 0.5).then_inc(xc_ready, 1)
                act.wait_ge(dtexp_ready, tt + 1)
                nc.scalar.activation(dt1[:, 1, :], dt1[:, 0, :], ACT.Exp).then_inc(dtexp_done, 1)
                act.wait_ge(u_ready, tt)
                act.wait_ge(y_ready, tt)
                for i in range(HALVES):
                    act.wait_ge(ring_ready, RING * tt + 4 + i + 1)
                    nc.scalar.copy(xtok[:, :, P * i:P * (i + 1)], ring_ps[:, i, :, :]).then_inc(ring_used, 1)
                act.wait_ge(sums_ready, tt + 1)
                nc.scalar.activation(e_pos[:, :], small_ps[:, CUM:CUM + P], ACT.Exp)
                nc.scalar.activation(e_neg[:, :], small_ps[:, CUM:CUM + P], ACT.Exp, scale=-1.0)
                nc.scalar.activation(e_rest[:, :], small_ps[:, REST:REST + P], ACT.Exp)
                nc.scalar.activation(coef[:, 2, :], la[:, :, :], ACT.Exp)
                nc.scalar.activation(sel[:, :], small_ps[:, SEL:SEL + 2 * CHUNKS], ACT.Exp).then_inc(exps_done, 1)
                act.wait_ge(y_ready, tt + 1)
                nc.scalar.copy(y[:, :, :, bass.ds(tt * P, P)], y_ps[:, :, :, :]).then_inc(y_copied, 1)

        @block.vector
        def _(dve):
            dve.wait_ge(*loaded)
            dve.wait_ge(init_done, 1)
            STEPS = 38
            dve.wait_ge(a_ready, 1)
            setup = Chain(dve, link_sem)
            setup.link(nc.vector.tensor_scalar(neg_a[:, :], neg_a[:, :], -1.0, None, ALU.mult))
            with dve.Fori(0, TPB) as tt:
                chain = Chain(dve, link_sem, 1 + STEPS * tt)
                link = chain.link
                norm.statistics(dve, tt, tile=lambda j: j * TPB + tt)
                norm.scale(dve, tt, tile=lambda j: j * TPB + tt)
                now = bass.ds(tt * P, P)
                for i in range(HALVES):
                    dve.wait_ge(ring_used, RING * tt + i + 1)
                    link(nc.vector.tensor_scalar(cv[:, i, :, :], xp[:, i, :, 0:P], w["conv_w"][:, i, 0:1],
                                                 w["conv_b"][:, i:i + 1], ALU.mult, ALU.add))
                    for k in range(1, CONV):
                        ins = nc.vector.scalar_tensor_tensor(cv[:, i, :, :], xp[:, i, :, k:k + P],
                                                             w["conv_w"][:, i, k:k + 1], cv[:, i, :, :],
                                                             ALU.mult, ALU.add)
                        if k < CONV - 1:
                            link(ins)
                    ins.then_inc(cv_ready, 1)
                nc.vector.tensor_copy(xp[:, :, :, 0:CONV - 1], xp[:, :, :, P:]).then_inc(halo_done, 1)
                for i in range(HALVES):
                    dve.wait_ge(tz_done, HALVES * tt + i + 1)
                    nc.vector.scalar_tensor_tensor(gate[:, i, :, now], tz[:, i, :, :], 1.0, ring_ps[:, i, :, :],
                                                   ALU.add, ALU.mult).then_inc(ring_used, 1)
                for i in range(HALVES):
                    dve.wait_ge(tc_done, HALVES * tt + i + 1)
                    ins = nc.vector.scalar_tensor_tensor(tc[:, i, :, :], tc[:, i, :, :], 1.0, cv[:, i, :, :],
                                                         ALU.add, ALU.mult)
                ins.then_inc(xc2_ready, 1)

                dve.wait_ge(dbl_ready, tt + 1)
                link(nc.vector.tensor_copy(dbl[:, :, :], small_ps[:, DBL:DBL + NDBL * BATCH]
                                           .rearrange("p (b n) -> p b n", b=BATCH)))
                nc.vector.tensor_scalar(dt1[:, 0, :], dbl[:, :, NDBL - 1], DT_LO, DT_HI, ALU.max, ALU.min)\
                    .then_inc(dtexp_ready, 1)
                dve.wait_ge(dtexp_done, tt + 1)
                u, s, s2, poly, dt = (dt1[:, n, :] for n in range(1, 6))
                link(nc.vector.tensor_scalar_add(s, u, 2.0))
                link(nc.vector.reciprocal(s, s))
                link(nc.vector.tensor_tensor(s, s, u, ALU.mult))
                link(nc.vector.tensor_tensor(s2, s, s, ALU.mult))
                link(nc.vector.tensor_scalar(poly, s2, 2.0 / 7, 2.0 / 5, ALU.mult, ALU.add))
                link(nc.vector.tensor_tensor(poly, poly, s2, ALU.mult))
                link(nc.vector.tensor_scalar(poly, poly, 2.0 / 3, None, ALU.add))
                link(nc.vector.tensor_tensor(poly, poly, s2, ALU.mult))
                link(nc.vector.tensor_scalar(poly, poly, 2.0, None, ALU.add))
                link(nc.vector.tensor_tensor(dt, poly, s, ALU.mult))
                link(nc.vector.tensor_scalar(dt, dt, DT_MIN, DT_MAX, ALU.max, ALU.min))
                dtw = wide(dt, NS)
                a_all = neg_a[:, :].unsqueeze(1).to_broadcast([P, BATCH, NS])
                link(nc.vector.tensor_tensor(la[:, :, 0:NS], dtw, a_all, ALU.mult))
                nc.vector.tensor_scalar(la[:, :, 0:NS], la[:, :, 0:NS], DECAY_FLOOR, 0.0, ALU.max, ALU.min)\
                    .then_inc(la_ready, 1)
                link(nc.vector.tensor_tensor(bbar[:, :, 0:NS], dtw, dbl[:, :, 0:NS], ALU.mult))
                link(nc.vector.tensor_scalar(bbar[:, :, 0:NS], bbar[:, :, 0:NS], -INPUT_CLIP, INPUT_CLIP,
                                             ALU.max, ALU.min))
                link(nc.vector.tensor_copy(cc[:, :, 0:NS], dbl[:, :, NS:2 * NS]))
                dve.wait_ge(ring_used, RING * (tt + 1))
                link(nc.vector.tensor_reduce(umax[:, :], xtok[:, :, :], AX.X, ALU.max, apply_absolute_value=True))
                link(nc.vector.scalar_tensor_tensor(states_of(coef, 3), bbar[:, :, :], -1.0, bbar[:, :, :],
                                                    ALU.mult, ALU.max))
                link(nc.vector.tensor_tensor(states_of(coef, 3), states_of(coef, 3), wide(umax[:, :], SW), ALU.mult))
                dve.wait_ge(exps_done, tt + 1)
                link(nc.vector.tensor_tensor(coef[:, 0, :], flat(bbar), e_neg[:, :], ALU.mult))
                link(nc.vector.tensor_tensor(coef[:, 1, :], flat(cc), e_pos[:, :], ALU.mult))
                link(nc.vector.tensor_tensor(cum[:, :], flat(bbar), e_rest[:, :], ALU.mult))
                dve.wait_ge(u_ready, tt)
                for k in range(CHUNKS):
                    ins = nc.vector.tensor_scalar(wk[:, k, :], cum[:, :], w["chunk_mask"][:, k:k + 1], None, ALU.mult)
                ins.then_inc(coef_ready, 1)
                link(nc.vector.tensor_reduce(cmax[:, bass.ds(tt, 1)], small_ps[:, CUM:CUM + P], AX.X, ALU.max,
                                             apply_absolute_value=True))
                dve.wait_ge(coef_stored, 16 * tt)
                states = states_of(coef, 2)
                link(nc.vector.tensor_copy(out_coef[:, 0, :, :], states[:, :, 0:NS]))
                link(nc.vector.tensor_copy(out_coef[:, 1, :, :], bbar[:, :, 0:NS]))
                nc.vector.tensor_copy(out_coef[:, 2, :, :], cc[:, :, 0:NS]).then_inc(out_coef_ready, 1)

                dve.wait_ge(tr_ready, tt + 1)
                dve.wait_ge(y_ready, tt)
                link(nc.vector.tensor_copy(bt[:, :], tr_ps[:, 0, :]))
                for b in range(BATCH):
                    rows = slice(SW * b, SW * (b + 1))
                    ins = nc.vector.tensor_copy(ct[rows, b, :], tr_ps[rows, 1, :])
                link(ins)
                link(nc.vector.tensor_copy(bound_a[:, now], tr_ps[:, 2, :]))
                nc.vector.tensor_copy(bound_v[:, now], tr_ps[:, 3, :]).then_inc(tr_used, 1)
                dve.wait_ge(g_ready, tt + 1)
                nc.vector.tensor_tensor(gt[:, :, :], g_ps[:, :, :],
                                        w["chunk_causal"][:, :].unsqueeze(1).to_broadcast([P, BATCH, P]),
                                        ALU.mult).then_inc(gt_ready, 1)
                dve.wait_ge(u_ready, tt + 1)
                for k in range(CHUNKS):
                    last = h[:, (k - 1) % CHUNKS, :]
                    ins = nc.vector.tensor_scalar(hm[:, k, :], last, sel[:, CHUNKS + k:CHUNKS + k + 1], None, ALU.mult)
                    if k == CHUNKS - 1:
                        ins.then_inc(hm_ready, 1)
                    link(nc.vector.scalar_tensor_tensor(h[:, k, :], last, sel[:, k:k + 1], u_ps[:, k, :],
                                                        ALU.mult, ALU.add))
                assert chain.n == STEPS, chain.n
            end = Chain(dve, link_sem, 1 + STEPS * TPB)
            end.link(nc.vector.tensor_tensor_scan(bound_v[:, :], bound_a[:, :], bound_v[:, :], 0.0, ALU.mult, ALU.add))
            end.link(nc.vector.tensor_reduce(verdict[:, 0:1], bound_v[:, :], AX.X, ALU.max))
            end.link(nc.vector.tensor_reduce(verdict[:, 1:2], cmax[:, :], AX.X, ALU.max))
            end.link(nc.vector.tensor_scalar(verdict[:, 2:3], verdict[:, 1:2], LOG_PROVED, None, ALU.is_le))
            nc.vector.scalar_tensor_tensor(verdict[:, 3:4], verdict[:, 0:1], STATE_PROVED, verdict[:, 2:3],
                                           ALU.is_le, ALU.mult).then_inc(verdict_ready, 1)
            dve.wait_ge(sum_ready, 1)
            nc.vector.tensor_scalar(flag[:, :], small_ps[0:1, 0:1], float(P), None, ALU.not_equal).then_inc(flag_ready, 1)
            dve.wait_ge(flag_ready, 1)

def flat(t):
    return t[:, :, :].rearrange("p b s -> p (b s)")

def states_of(coef, i):
    return coef[:, i, :].rearrange("p (b s) -> p b s", b=BATCH)

def mamba_steps(nc, name, y, xc, flag, coef_dram):
    with ExitStack() as ctx:
        rows = ctx.enter_context(nc.sbuf_tensor(f"{name}_rows", [P, STEP_ROWS, 3, BATCH, NS], F32))
        hs = ctx.enter_context(nc.sbuf_tensor(f"{name}_hs", [P, HALVES, BATCH, NS], F32))
        hx = ctx.enter_context(nc.sbuf_tensor(f"{name}_hx", [P, HALVES, BATCH, NS], F32))
        rows_loaded = nc.alloc_semaphore(f"{name}_rows_loaded")
        rows_used = nc.alloc_semaphore(f"{name}_rows_used")
        step_link = nc.alloc_semaphore(f"{name}_step_link")
        block = ctx.enter_context(nc.Block())
        PIECES = SEQ // STEP_ROWS

        @block.sync
        def _(sp):
            failed = sp.value_load(flag[0:1, 0:1], min_val=0, max_val=1)
            with sp.If(failed > 0):
                with sp.Fori(0, PIECES) as n:
                    sp.wait_ge(rows_used, n)
                    src = coef_dram[bass.ds(n * STEP_ROWS, STEP_ROWS), :]
                    sp.dma_start(rows[:, :, :, :, :].rearrange("p t k b s -> p t (k b s)"),
                                 src.unsqueeze(0).to_broadcast([P, STEP_ROWS, 3 * BATCH * NS])).then_inc(rows_loaded, 16)

        @block.vector
        def _(dve):
            failed = dve.value_load(flag[0:1, 0:1], min_val=0, max_val=1)
            with dve.If(failed > 0):
                OPS = 6
                nc.vector.memset(hs[:, :, :, :], 0.0).then_inc(step_link, 1)
                dve.wait_ge(step_link, 1)
                with dve.Fori(0, PIECES) as n:
                    dve.wait_ge(rows_loaded, 16 * (n + 1))
                    chain = Chain(dve, step_link, 1 + n * (OPS * STEP_ROWS))
                    for r in range(STEP_ROWS):
                        def row(k):
                            return rows[:, r, k, :, :].unsqueeze(1).to_broadcast([P, HALVES, BATCH, NS])
                        t = n * STEP_ROWS + r
                        xt = xc[:, :, :, bass.ds(t, 1)].to_broadcast([P, HALVES, BATCH, NS])
                        chain.link(nc.vector.tensor_tensor(hx[:, :, :, :], row(1), xt, ALU.mult))
                        chain.link(nc.vector.tensor_tensor(hs[:, :, :, :], row(0), hs[:, :, :, :], ALU.mult))
                        chain.link(nc.vector.tensor_tensor(hs[:, :, :, :], hs[:, :, :, :], hx[:, :, :, :], ALU.add))
                        chain.link(nc.vector.tensor_scalar(hs[:, :, :, :], hs[:, :, :, :], -STATE_CLIP, STATE_CLIP,
                                                           ALU.max, ALU.min))
                        chain.link(nc.vector.tensor_tensor(hx[:, :, :, :], hs[:, :, :, :], row(2), ALU.mult))
                        chain.link(nc.vector.tensor_reduce(y[:, :, :, bass.ds(t, 1)], hx[:, :, :, :], AX.X, ALU.add))
                    nc.vector.tensor_copy(hx[:, 0, 0, 0:1], rows[:, 0, 0, 0, 0:1]).then_inc(rows_used, 1)
                    dve.wait_ge(rows_used, n + 1)

def mamba_output(nc, x, const, w, name, y, gate, xc):
    with ExitStack() as ctx:
        o_ps = Banks(const["psum"]).take(2, GT, P)
        mixed = ctx.enter_context(nc.sbuf_tensor(f"{name}_mixed", [P, 2, HALVES, BLK], F32))
        half_y = ctx.enter_context(nc.sbuf_tensor(f"{name}_half_y", [P, HALVES, BLK], F32))
        gated, mixed_ready = (nc.alloc_semaphore(f"{name}_{n}") for n in ("gated", "mixed_ready"))
        o_ready, added = (nc.alloc_semaphore(f"{name}_{n}") for n in ("o_ready", "added"))
        block = ctx.enter_context(nc.Block())

        @block.vector
        def _(dve):
            def mix(q, b, p):
                cols = slice(p * BLK, (p + 1) * BLK)
                dve.wait_ge(mixed_ready, q)
                for i in range(HALVES):
                    ins = nc.vector.scalar_tensor_tensor(half_y[:, i, :], y[:, i, bass.ds(b, 1), cols], 0.5,
                                                         gate[:, i, bass.ds(b, 1), cols], ALU.mult, ALU.mult)
                ins.then_inc(gated, 1)
                dve.wait_ge(gated, q + 1)
                dve.wait_ge(o_ready, 2 * b)
                for i in range(HALVES):
                    ins = nc.vector.scalar_tensor_tensor(mixed[:, p, i, :], xc[:, i, bass.ds(b, 1), cols],
                                                         w["d"][:, i:i + 1], half_y[:, i, :], ALU.mult, ALU.add)
                ins.then_inc(mixed_ready, 1)

            with dve.Fori(0, BATCH) as b:
                for p in range(2):
                    mix(2 * b + p, b, p)
                for p in range(2):
                    q = 2 * b + p
                    dve.wait_ge(o_ready, q + 1)
                    xq = x[:, bass.ds(q * GT, GT), :]
                    nc.vector.tensor_tensor(xq, o_ps[:, p, :, :], xq, ALU.add).then_inc(added, 1)

        @block.tensor
        def _(pe):
            with pe.Fori(0, BATCH) as b:
                for p in range(2):
                    q = 2 * b + p
                    pe.wait_ge(mixed_ready, q + 1)
                    pe.wait_ge(added, 2 * b)
                    for j in range(GT):
                        for i in range(HALVES):
                            ins = pe.matmul(o_ps[:, p, j, :], mixed[:, p, i, j * P:(j + 1) * P], w["out"][:, i, :],
                                            start=(i == 0), stop=(i == HALVES - 1))
                    ins.then_inc(o_ready, 1)

E = 15
NE = E + 1
TOPK = 3

def ffn_stage(nc, x, const, w, loaded, name, out=None, fetch=None):
    with ExitStack() as ctx:
        def sb(n, shape, dt=F32):
            return ctx.enter_context(nc.sbuf_tensor(f"{name}_{n}", shape, dt))

        def sem(n):
            return nc.alloc_semaphore(f"{name}_{n}")

        banks = Banks(const["psum"])
        h_ps = banks.take(2, BLK)
        y_ps = banks.take(2, GT, P)
        norm = Prenorm(nc, ctx, const, x, name + "_n", xt_ps=banks.take(GT, P))
        logit_ps = banks.take(GT, P)
        cwt_ps = banks.take(GT, P)

        h = sb("h", [P, 2, BLK])
        cw = sb("cw", [P, 2, GT, NE])
        cwt = sb("cwt", [NE, 2, BLK])
        top = sb("top", [P, GT])
        prob = sb("prob", [P, GT, E])
        left = sb("left", [P, GT, E])
        eq = sb("eq", [P, GT, E])

        logit_ready, shifted, exp_done = sem("logit_ready"), sem("shifted"), sem("exp_done")
        cw_ready, cwt_ps_ready, cwt_ready = sem("cw_ready"), sem("cwt_ps_ready"), sem("cwt_ready")
        h_ready, relu_done, y_ready, acc_done = sem("h_ready"), sem("relu_done"), sem("y_ready"), sem("acc_done")
        dve_link = sem("dve_link")
        cw_one = sem("cw_one")

        block = ctx.enter_context(nc.Block())

        def blocks(eng, body):
            with eng.Fori(0, BLOCKS // 2 - 1) as i:
                body(2 * i, 0, True)
                body(2 * i + 1, 1, True)
            body(BLOCKS - 2, 0, True)
            body(BLOCKS - 1, 1, False)

        if fetch is not None:
            @block.sync
            def _(sp):
                for dst, src in fetch[0]:
                    sp.dma_start(dst, src).then_inc(fetch[1], 16)

        if out is not None:
            stored = sem("stored")

            @block.sync
            def _(sp):
                with sp.Fori(0, BLOCKS) as g:
                    sp.wait_ge(acc_done, NE * (g + 1))
                    rows = bass.ds(g * GT, GT)
                    sp.dma_start(out[:, rows, :], x[:, rows, :]).then_inc(stored, 16)
                sp.wait_ge(stored, 16 * BLOCKS)

        @block.gpsimd
        def _(pool):
            norm.invert(pool, 0)
            blocks(pool, lambda g, p, more: norm.invert(pool, g + 1) if more else None)

        @block.tensor
        def _(pe):
            sem_loaded, count = loaded
            pe.wait_ge(sem_loaded, count)

            def route(q, p):
                pe.wait_ge(norm.xt_ready, q + 1)
                pe.wait_ge(shifted, q)
                for j in range(GT):
                    pe.matmul(logit_ps[:, j, 0:E], norm.xt[:, p, j * P:(j + 1) * P], w["router"][:, :],
                              start=True, stop=False)
                    ins = pe.matmul(logit_ps[:, j, 0:E], const["ones"][0:1, 0:P], w["router_b"][:, :],
                                    start=False, stop=True)
                ins.then_inc(logit_ready, 1)

            def transpose_cw(q, p):
                pe.wait_ge(cw_ready, q + 1)
                pe.wait_ge(cwt_ready, q)
                for j in range(GT):
                    ins = pe.transpose(cwt_ps[0:NE, j, :], cw[:, p, j, :], const["ident"][:, :])
                ins.then_inc(cwt_ps_ready, 1)

            def up(g, p, e):
                pe.wait_ge(relu_done, NE * g + max(e - 1, 0))
                pe.matmul(h_ps[:, e % 2, :], w["w1"][:, e, :], norm.xt[:, p, :],
                          start=True, stop=True).then_inc(h_ready, 1)

            def down(g, p, e):
                pe.wait_ge(relu_done, NE * g + e + 1)
                pe.wait_ge(acc_done, NE * g + max(e - 1, 0))
                if e == E:
                    pe.wait_ge(cwt_ready, g + 1)
                for j in range(GT):
                    if e == E:
                        pe.matmul(y_ps[:, e % 2, j, :], cwt[:, p, j * P:(j + 1) * P], w["b2"][:, :],
                                  start=True, stop=False)
                    ins = pe.matmul(y_ps[:, e % 2, j, :], h[:, e % 2, j * P:(j + 1) * P], w["w2"][:, e, :],
                                    start=(e != E), stop=True)
                ins.then_inc(y_ready, 1)

            def body(g, p, more):
                for e in range(NE):
                    if e == 0:
                        pe.wait_ge(norm.xt_ready, g + 1)
                    up(g, p, e)
                    if e >= 1:
                        down(g, p, e - 1)
                    if more and e == 3:
                        norm.transpose(pe, g + 1)
                    if more and e == 6:
                        route(g + 1, 1 - p)
                    if e == 1:
                        transpose_cw(g, p)
                down(g, p, E)

            norm.transpose(pe, 0)
            route(0, 0)
            blocks(pe, body)

        @block.scalar
        def _(act):
            act.wait_ge(loaded[0], loaded[1])

            def exp(q):
                act.wait_ge(shifted, q + 1)
                nc.scalar.activation(prob[:, :, :], prob[:, :, :], ACT.Exp).then_inc(exp_done, 1)

            def relu(g, e):
                act.wait_ge(h_ready, NE * g + e + 1)
                act.wait_ge(y_ready, NE * g + max(e - 1, 0))
                nc.scalar.activation(h[:, e % 2, :], h_ps[:, e % 2, :], ACT.Relu,
                                     bias=w["b1"][:, e:e + 1]).then_inc(relu_done, 1)

            def copy_cwt(q, p):
                act.wait_ge(cwt_ps_ready, q + 1)
                nc.scalar.copy(cwt[:, p, :], cwt_ps[0:NE, :, :]).then_inc(cwt_ready, 1)

            def body(g, p, more):
                for e in range(NE):
                    relu(g, e)
                    if more and e == 3:
                        norm.copy(act, g + 1, 1 - p)
                    if more and e == 9:
                        exp(g + 1)
                    if e == 1:
                        copy_cwt(g, p)

            norm.copy(act, 0, 0)
            exp(0)
            blocks(act, body)

        @block.vector
        def _(dve):
            STEPS = 1 + 3 + 6 * TOPK

            def shift(q):
                chain = Chain(dve, dve_link, STEPS * q)
                dve.wait_ge(logit_ready, q + 1)
                chain.link(nc.vector.tensor_reduce(top[:, :], logit_ps[:, :, 0:E], AX.X, ALU.max))
                nc.vector.tensor_tensor(prob[:, :, :], logit_ps[:, :, 0:E], wide(top[:, :], E),
                                        ALU.subtract).then_inc(shifted, 1)

            def choose(q, p):
                chain = Chain(dve, dve_link, STEPS * q + 1)
                dve.wait_ge(exp_done, q + 1)
                chain.link(nc.vector.tensor_reduce(top[:, :], prob[:, :, :], AX.X, ALU.add))
                chain.link(nc.vector.reciprocal(top[:, :], top[:, :]))
                chain.link(nc.vector.tensor_tensor(prob[:, :, :], prob[:, :, :], wide(top[:, :], E), ALU.mult))
                order = const["order"][:, :, :]
                for k in range(TOPK):
                    src = prob if k == 0 else left
                    chain.link(nc.vector.tensor_reduce(top[:, :], src[:, :, :], AX.X, ALU.max))
                    chain.link(nc.vector.tensor_tensor(eq[:, :, :], src[:, :, :], wide(top[:, :], E), ALU.is_equal))
                    chain.link(nc.vector.tensor_tensor(eq[:, :, :], eq[:, :, :], order, ALU.mult))
                    chain.link(nc.vector.tensor_reduce(top[:, :], eq[:, :, :], AX.X, ALU.max))
                    chain.link(nc.vector.tensor_tensor(eq[:, :, :], order, wide(top[:, :], E), ALU.is_equal))
                    chain.link(nc.vector.scalar_tensor_tensor(left[:, :, :], eq[:, :, :], -2.0, src[:, :, :],
                                                              ALU.mult, ALU.add))
                nc.vector.scalar_tensor_tensor(cw[:, p, :, 0:E], left[:, :, :], 0.0, prob[:, :, :],
                                               ALU.is_lt, ALU.mult).then_inc(cw_ready, 1)
                assert 1 + chain.n == STEPS

            def add_expert(g, p, e):
                dve.wait_ge(y_ready, NE * g + e + 1)
                dve.wait_ge(acc_done, NE * g + e)
                for j in range(GT):
                    xg = x[:, g * GT + j, :]
                    ins = nc.vector.scalar_tensor_tensor(xg, y_ps[:, e % 2, j, :], cw[:, p, j, e:e + 1], xg,
                                                         ALU.mult, ALU.add)
                ins.then_inc(acc_done, 1)

            def body(g, p, more):
                if more:
                    norm.statistics(dve, g + 1)
                dve.wait_ge(cw_ready, g + 1)
                for e in range(NE):
                    add_expert(g, p, e)
                    if more and e == 0:
                        norm.scale(dve, g + 1)
                    if more and e == 7:
                        shift(g + 1)
                    if more and e == 10:
                        choose(g + 1, 1 - p)

            nc.vector.memset(cw[:, :, :, E:NE], 1.0).then_inc(cw_one, 1)
            dve.wait_ge(cw_one, 1)
            norm.statistics(dve, 0)
            norm.scale(dve, 0)
            shift(0)
            choose(0, 0)
            blocks(dve, body)

LIN_EPS = 1e-15
BPB = BLOCKS // BATCH

def linear_attention_stage(nc, x, const, w, loaded, name):
    with ExitStack() as ctx:
        def sb(n, shape, dt=F32):
            return ctx.enter_context(nc.sbuf_tensor(f"{name}_{n}", shape, dt))

        def sem(n):
            return nc.alloc_semaphore(f"{name}_{n}")

        banks = Banks(const["psum"])
        norm = Prenorm(nc, ctx, const, x, name + "_n", xt_ps=banks.take(GT, P))
        q_ps = banks.take(BLK)
        kv_ps = banks.take(GT, 2 * P)
        vk_ps = banks.take(BLK)
        den_ps = banks.take(BLK)
        num_ps = banks.take(BLK)
        y_ps = banks.take(GT, P)
        qt = sb("qt", [P, BPB, BLK])
        kv = sb("kv", [P, GT, 2 * P + 1])
        num_w = sb("num_w", [P, P])
        den_w = sb("den_w", [P, P])
        rden = sb("rden", [P, 2, BLK])
        ratio = sb("ratio", [P, 2, BLK])

        one_set, q_ready, qt_ready = sem("one_set"), sem("q_ready"), sem("qt_ready")
        kv_ps_ready, kv_ready, vk_added = sem("kv_ps_ready"), sem("kv_ready"), sem("vk_added")
        head_link, heads_ready = sem("head_link"), sem("heads_ready")
        ratio_ps_ready, ratio_link, ratio_ready = sem("ratio_ps_ready"), sem("ratio_link"), sem("ratio_ready")
        y_ready, x_done = sem("y_ready"), sem("x_done")

        block = ctx.enter_context(nc.Block())

        @block.gpsimd
        def _(pool):
            with pool.Fori(0, BATCH) as b:
                for p in range(BPB):
                    norm.invert(pool, BPB * b + p)

        @block.tensor
        def _(pe):
            pe.wait_ge(*loaded)

            def first(b, p):
                q = BPB * b + p
                norm.transpose(pe, q)
                pe.wait_ge(norm.xt_ready, q + 1)
                pe.wait_ge(qt_ready, q)
                pe.matmul(q_ps[:, :], w["q"][:, :], norm.xt[:, p, :], start=True, stop=True).then_inc(q_ready, 1)
                pe.wait_ge(kv_ready, q)
                for j in range(GT):
                    ins = pe.matmul(kv_ps[:, j, :], norm.xt[:, p, j * P:(j + 1) * P], w["kv"][:, :],
                                    start=True, stop=True)
                ins.then_inc(kv_ps_ready, 1)

            def state(b, p):
                pe.wait_ge(kv_ready, BPB * b + p + 1)
                if p == 0:
                    pe.wait_ge(heads_ready, b)
                for j in range(GT):
                    ins = pe.matmul(vk_ps[:, 0:P + 1], kv[:, j, 0:P], kv[:, j, P:2 * P + 1],
                                    start=(p == 0 and j == 0), stop=(p == BPB - 1 and j == GT - 1))
                ins.then_inc(vk_added, 1)

            def second(b, p):
                q = BPB * b + p
                pe.wait_ge(heads_ready, b + 1)
                pe.wait_ge(qt_ready, q + 1)
                pe.wait_ge(ratio_ready, q)
                pe.matmul(num_ps[:, :], num_w[:, :], qt[:, p, :], start=True, stop=True)
                pe.matmul(den_ps[:, :], den_w[:, :], qt[:, p, :], start=True, stop=True).then_inc(ratio_ps_ready, 1)

            def project(b, p):
                q = BPB * b + p
                pe.wait_ge(ratio_ready, q + 1)
                pe.wait_ge(x_done, q)
                for j in range(GT):
                    pe.matmul(y_ps[:, j, :], ratio[:, p, j * P:(j + 1) * P], w["proj"][:, :], start=True, stop=False)
                    ins = pe.matmul(y_ps[:, j, :], const["ones"][0:1, 0:P], w["proj_b"][:, :],
                                    start=False, stop=True)
                ins.then_inc(y_ready, 1)

            with pe.Fori(0, BATCH) as b:
                first(b, 0)
                first(b, 1)
                state(b, 0)
                state(b, 1)
                second(b, 0)
                second(b, 1)
                project(b, 0)
                project(b, 1)

        @block.scalar
        def _(act):
            with act.Fori(0, BATCH) as b:
                for p in range(BPB):
                    q = BPB * b + p
                    norm.copy(act, q, p, (kv_ps_ready, BPB * b))
                    act.wait_ge(q_ready, q + 1)
                    act.wait_ge(ratio_ps_ready, BPB * b)
                    nc.scalar.activation(qt[:, p, :], q_ps[:, :], ACT.Relu).then_inc(qt_ready, 1)

        @block.vector
        def _(dve):
            nc.vector.memset(kv[:, :, 2 * P:2 * P + 1], 1.0).then_inc(one_set, 1)
            with dve.Fori(0, BATCH) as b:
                for p in range(BPB):
                    norm.statistics(dve, BPB * b + p)
                    norm.scale(dve, BPB * b + p)
                for p in range(BPB):
                    q = BPB * b + p
                    dve.wait_ge(kv_ps_ready, q + 1)
                    dve.wait_ge(vk_added, q)
                    nc.vector.tensor_scalar_max(kv[:, :, 0:2 * P], kv_ps[:, :, :], 0.0).then_inc(kv_ready, 1)
                dve.wait_ge(vk_added, BPB * (b + 1))
                nc.vector.tensor_tensor(num_w[:, :], vk_ps[:, 0:P], const["head4"][:, :], ALU.mult)\
                    .then_inc(head_link, 1)
                nc.vector.tensor_scalar(den_w[:, :], const["head4"][:, :], vk_ps[:, P:P + 1], None, ALU.mult)\
                    .then_inc(heads_ready, 1)
                for p in range(BPB):
                    q = BPB * b + p
                    dve.wait_ge(ratio_ps_ready, q + 1)
                    nc.vector.tensor_scalar_add(rden[:, p, :], den_ps[:, :], LIN_EPS).then_inc(ratio_link, 1)
                    dve.wait_ge(ratio_link, 2 * q + 1)
                    nc.vector.reciprocal(rden[:, p, :], rden[:, p, :]).then_inc(ratio_link, 1)
                    dve.wait_ge(ratio_link, 2 * q + 2)
                    dve.wait_ge(y_ready, BPB * b)
                    nc.vector.tensor_tensor(ratio[:, p, :], num_ps[:, :], rden[:, p, :], ALU.mult)\
                        .then_inc(ratio_ready, 1)
                for p in range(BPB):
                    q = BPB * b + p
                    dve.wait_ge(y_ready, q + 1)
                    xq = x[:, bass.ds(q * GT, GT), :]
                    nc.vector.tensor_tensor(xq, y_ps[:, :, :], xq, ALU.add).then_inc(x_done, 1)

HD4 = 4
DECAYS = 2
BETA_MIN, BETA_MAX = 0.85, 0.9995
DEN_EPS = 1e-6
STATES = HD4 + 1
W_Q, W_QS, W_K, W_KS, W_V, W_BETA, W_MIX = 0, 1, 2, 3, 4, 8, 10
RET_WEIGHTS = 12
DVE_PROJ = 8
ACT_PROJ = 3

def retention_stage(nc, x, const, w, loaded, name, fetch=None):
    with ExitStack() as ctx:
        def sb(n, shape, dt=F32):
            return ctx.enter_context(nc.sbuf_tensor(f"{name}_{n}", shape, dt))

        def sem(n):
            return nc.alloc_semaphore(f"{name}_{n}")

        banks = Banks(const["psum"])
        norm = Prenorm(nc, ctx, const, x, name + "_n", parities=1, xt_ps=banks.take(GT, P))
        dproj_ps = banks.take(2, BLK)
        aproj_ps = banks.take(BLK)
        nd_ps = banks.take(2, BLK)
        y_ps = banks.take(GT, P)
        mix_w = sb("mix_w", [P, P])
        half_b = sb("half_b", [P, ACT_PROJ])
        rope_a = sb("rope_a", [P, 2, BLK])
        rope_b = sb("rope_b", [P, 2, BLK])
        rot = sb("rot", [P, 2, BLK])
        phi = sb("phi", [P, 2, BLK])
        ex = sb("ex", [P, 2, BLK])
        kv = sb("kv", [P, HD4, BLK])
        beta = sb("beta", [P, DECAYS, BLK])
        mix = sb("mix", [P, DECAYS, BLK])
        th = sb("th", [P, ACT_PROJ, BLK])
        state = sb("state", [P, DECAYS, STATES, BLK])
        carry = sb("carry", [P, DECAYS, STATES])
        rd = sb("rd", [P, BLK])
        ym = sb("ym", [P, DECAYS, BLK])
        yt = sb("yt", [P, BLK])
        z = sb("z", [P, GT, P])
        zn = sb("zn", [P, GT, P])
        z_stats = sb("z_stats", [P, GT, 6])
        z_mv = sb("z_mv", [P, GT, 2])
        z_rstd = sb("z_rstd", [P, GT])

        weights_ready = sem("weights_ready")
        dproj_ready, dproj_used = sem("dproj_ready"), sem("dproj_used")
        aproj_ready, tanh_done, th_used = sem("aproj_ready"), sem("tanh_done"), sem("th_used")
        rot_ready, neg_ready, exp_done = sem("rot_ready"), sem("neg_ready"), sem("exp_done")
        carried, prod_dve, prod_pool = sem("carried"), sem("prod_dve"), sem("prod_pool")
        nd_ready, nd_used, yt_ready, y_ready = sem("nd_ready"), sem("nd_used"), sem("yt_ready"), sem("y_ready")
        z_ready, z_stats_ready, z_rstd_ready, zn_ready = sem("z_ready"), sem("z_stats_ready"), sem("z_rstd_ready"), sem("zn_ready")
        x_done, dve_link, z_stat_link = sem("x_done"), sem("dve_link"), sem("z_stat_link")

        block = ctx.enter_context(nc.Block())

        if fetch is not None:
            @block.sync
            def _(sp):
                for dst, src in fetch[0]:
                    sp.dma_start(dst, src).then_inc(fetch[1], 16)

        @block.gpsimd
        def _(pool):
            def body(q):
                norm.invert(pool, q)
                for i in range(2):
                    pool.wait_ge(dproj_used, DVE_PROJ * q + 2 * i + 2)
                    nc.gpsimd.tensor_tensor(rot[:, i, :], rope_a[:, i, :], rope_b[:, i, :], ALU.add)\
                        .then_inc(rot_ready, 1)
                for m in range(DECAYS):
                    pool.wait_ge(carried, DECAYS * q + m + 1)
                    for c in range(2):
                        s = state[:, m, 1 + c, :]
                        ins = nc.gpsimd.tensor_tensor(s, s, phi[:, 0, :], ALU.mult)
                    ins.then_inc(prod_pool, 1)
                pool.wait_ge(z_stats_ready, q + 1)
                nc.gpsimd.tensor_tensor(z_rstd[:, :], z_mv[:, :, 1], const["minus_half"][:, 0:GT],
                                        ALU.pow).then_inc(z_rstd_ready, 1)
                pool.wait_ge(weights_ready, 2)
                pool.wait_ge(z_rstd_ready, q + 1)
                pool.wait_ge(x_done, q)
                for j in range(GT):
                    ins = nc.gpsimd.tensor_scalar(zn[:, j, :], z[:, j, :], z_mv[:, j, 0:1],
                                                  z_rstd[:, j:j + 1], ALU.subtract, ALU.mult)
                ins.then_inc(zn_ready, 1)

            with pool.Fori(0, BATCH) as b:
                for p in range(BPB):
                    body(BPB * b + p)

        @block.tensor
        def _(pe):
            pe.wait_ge(*loaded)
            pe.wait_ge(weights_ready, 2)

            def body(q):
                norm.transpose(pe, q)
                pe.wait_ge(norm.xt_ready, q + 1)

                def for_dve(i, lhs):
                    pe.wait_ge(dproj_used, DVE_PROJ * q + max(i - 1, 0))
                    pe.matmul(dproj_ps[:, i % 2, :], lhs, norm.xt[:, 0, :], start=True, stop=True)\
                        .then_inc(dproj_ready, 1)

                for i in range(4):
                    for_dve(i, w["w"][:, i, :])
                for i in range(ACT_PROJ):
                    pe.wait_ge(tanh_done, ACT_PROJ * q + i)
                    lhs = w["w"][:, W_BETA + i, :] if i < DECAYS else mix_w[:, :]
                    pe.matmul(aproj_ps[:, :], lhs, norm.xt[:, 0, :], start=True, stop=True).then_inc(aproj_ready, 1)
                for i in range(4, DVE_PROJ):
                    for_dve(i, w["w"][:, i, :])
                for m in range(DECAYS):
                    pe.wait_ge(nd_used, DECAYS * q + m)
                    pe.wait_ge(prod_dve, DECAYS * q + m + 1)
                    pe.matmul(nd_ps[:, 1, :], const["head4"][:, :], state[:, m, 0, :], start=True, stop=True)
                    pe.wait_ge(prod_pool, DECAYS * q + m + 1)
                    for c in range(HD4):
                        ins = pe.matmul(nd_ps[:, 0, :], w["gather4"][:, c, :], state[:, m, 1 + c, :],
                                        start=(c == 0), stop=(c == HD4 - 1))
                    ins.then_inc(nd_ready, 1)
                pe.wait_ge(yt_ready, q + 1)
                pe.wait_ge(z_ready, q)
                for j in range(GT):
                    pe.matmul(y_ps[:, j, :], yt[:, j * P:(j + 1) * P], w["out"][:, :], start=True, stop=False)
                    ins = pe.matmul(y_ps[:, j, :], const["ones"][0:1, 0:P], w["out_b"][:, :], start=False, stop=True)
                ins.then_inc(y_ready, 1)

            with pe.Fori(0, BATCH) as b:
                for p in range(BPB):
                    body(BPB * b + p)

        @block.scalar
        def _(act):
            act.wait_ge(weights_ready, 2)

            def body(q):
                norm.copy(act, q, 0, (dproj_ready, DVE_PROJ * q))
                act.wait_ge(th_used, q)
                for i in range(ACT_PROJ):
                    act.wait_ge(aproj_ready, ACT_PROJ * q + i + 1)
                    nc.scalar.activation(th[:, i, :], aproj_ps[:, :], ACT.Tanh, bias=half_b[:, i:i + 1],
                                         scale=0.5).then_inc(tanh_done, 1)
                for i in range(2):
                    act.wait_ge(neg_ready, 2 * q + i + 1)
                    nc.scalar.activation(ex[:, i, :], ex[:, i, :], ACT.Exp).then_inc(exp_done, 1)

            with act.Fori(0, BATCH) as b:
                for p in range(BPB):
                    body(BPB * b + p)

        @block.vector
        def _(dve):
            dve.wait_ge(*loaded)
            nc.vector.tensor_tensor(mix_w[:, :], w["w"][:, W_MIX, :], w["w"][:, W_MIX + 1, :], ALU.subtract)\
                .then_inc(weights_ready, 1)
            setup = Chain(dve, dve_link)
            setup.link(nc.vector.tensor_copy(half_b[:, 0:DECAYS], w["b"][:, 0:DECAYS]))
            setup.link(nc.vector.tensor_tensor(half_b[:, 2:3], w["b"][:, 2:3], w["b"][:, 3:4], ALU.subtract))
            nc.vector.tensor_scalar(half_b[:, :], half_b[:, :], 0.5, None, ALU.mult).then_inc(weights_ready, 1)
            SETUP, STEPS = 2, 26

            def body(q, p):
                chain = Chain(dve, dve_link, SETUP + STEPS * q)
                link = chain.link
                now = slice(p * BLK, (p + 1) * BLK)
                norm.statistics(dve, q)
                norm.scale(dve, q, xn_used=z_ready)
                for i in range(4):
                    dve.wait_ge(dproj_ready, DVE_PROJ * q + i + 1)
                    if i % 2 == 0:
                        dst, table = rope_a, w["cos"]
                        dve.wait_ge(rot_ready, 2 * q)
                    else:
                        dst, table = rope_b, w["sin"]
                    nc.vector.tensor_tensor(dst[:, i // 2, :], dproj_ps[:, i % 2, :], table[:, now], ALU.mult)\
                        .then_inc(dproj_used, 1)
                for i in range(2):
                    dve.wait_ge(rot_ready, 2 * q + i + 1)
                    nc.vector.tensor_scalar_min(ex[:, i, :], rot[:, i, :], 0.0).then_inc(neg_ready, 1)
                dve.wait_ge(tanh_done, ACT_PROJ * q + ACT_PROJ)
                for m in range(DECAYS):
                    link(nc.vector.tensor_scalar(beta[:, m, :], th[:, m, :], 0.5, 0.5, ALU.mult, ALU.add))
                    link(nc.vector.tensor_scalar(beta[:, m, :], beta[:, m, :], BETA_MIN, BETA_MAX, ALU.max, ALU.min))
                link(nc.vector.tensor_scalar(mix[:, 0, :], th[:, 2, :], 0.5, 0.5, ALU.mult, ALU.add))
                nc.vector.tensor_scalar(mix[:, 1, :], th[:, 2, :], -0.5, 0.5, ALU.mult, ALU.add).then_inc(th_used, 1)
                dve.wait_ge(th_used, q + 1)
                for i in (1, 0):
                    dve.wait_ge(exp_done, 2 * q + 2)
                    link(nc.vector.scalar_tensor_tensor(phi[:, i, :], rot[:, i, :], 0.0, ex[:, i, :],
                                                        ALU.max, ALU.add))
                for c in range(HD4):
                    dve.wait_ge(dproj_ready, DVE_PROJ * q + 4 + c + 1)
                    nc.vector.tensor_tensor(kv[:, c, :], dproj_ps[:, c % 2, :], phi[:, 1, :], ALU.mult)\
                        .then_inc(dproj_used, 1)
                dve.wait_ge(dproj_used, DVE_PROJ * (q + 1))

                def scans(m):
                    for s in range(STATES):
                        link(nc.vector.tensor_tensor_scan(
                            state[:, m, s, :], beta[:, m, :], phi[:, 1, :] if s == 0 else kv[:, s - 1, :],
                            0.0 if p == 0 else carry[:, m, s:s + 1], ALU.mult, ALU.add))
                    nc.vector.tensor_copy(carry[:, m, :], state[:, m, :, BLK - 1]).then_inc(carried, 1)
                    dve.wait_ge(carried, DECAYS * q + m + 1)
                    for s in (3, 4, 0):
                        st = state[:, m, s, :]
                        ins = nc.vector.tensor_tensor(st, st, phi[:, 0, :], ALU.mult)
                    ins.then_inc(prod_dve, 1)

                def divide(m):
                    dve.wait_ge(nd_ready, DECAYS * q + m + 1)
                    link(nc.vector.tensor_scalar_add(rd[:, :], nd_ps[:, 1, :], DEN_EPS))
                    link(nc.vector.reciprocal(rd[:, :], rd[:, :]))
                    link(nc.vector.tensor_tensor(rd[:, :], rd[:, :], mix[:, m, :], ALU.mult))
                    nc.vector.tensor_tensor(ym[:, m, :], nd_ps[:, 0, :], rd[:, :], ALU.mult).then_inc(nd_used, 1)

                scans(0)
                scans(1)
                divide(0)
                divide(1)
                dve.wait_ge(nd_used, DECAYS * (q + 1))
                nc.vector.tensor_tensor(yt[:, :], ym[:, 0, :], ym[:, 1, :], ALU.add).then_inc(yt_ready, 1)

                dve.wait_ge(y_ready, q + 1)
                dve.wait_ge(zn_ready, q)
                nc.vector.tensor_tensor(z[:, :, :], y_ps[:, :, :], norm.xn[:, :, :], ALU.add).then_inc(z_ready, 1)
                dve.wait_ge(z_ready, q + 1)
                for j in range(GT):
                    ins = nc.vector.bn_stats(z_stats[:, j, :], z[:, j, :])
                ins.then_inc(z_stat_link, 1)
                dve.wait_ge(z_stat_link, q + 1)
                nc.vector.memset(norm.pause[:, :], 0.0)
                for j in range(GT):
                    ins = nc.vector.bn_aggr(z_mv[:, j, :], z_stats[:, j, :])
                link(ins)
                nc.vector.tensor_scalar_add(z_mv[:, :, 1], z_mv[:, :, 1], LN_EPS).then_inc(z_stats_ready, 1)
                dve.wait_ge(zn_ready, q + 1)
                for j in range(GT):
                    ins = nc.vector.tensor_tensor(zn[:, j, :], zn[:, j, :], w["ln_g"][:, :], ALU.mult)
                link(ins)
                for j in range(GT):
                    ins = nc.vector.tensor_tensor(zn[:, j, :], zn[:, j, :], w["ln_b"][:, :], ALU.add)
                link(ins)
                xq = x[:, bass.ds(q * GT, GT), :]
                nc.vector.tensor_tensor(xq, xq, zn[:, :, :], ALU.add).then_inc(x_done, 1)
                assert chain.n == STEPS, chain.n

            with dve.Fori(0, BATCH) as b:
                for p in range(BPB):
                    body(BPB * b + p, p)

HEADS, HD = 16, 8
UH = HEADS // 2
PARTS = 3
STACK = PARTS * PARTS * HD
ROWS = 96
VW = 32
GH = 4
E_STEPS = 2 * 2 * (GT + 2 * GT)
M_STEPS = UH * (GT + 2 * GT)
M_FIRST = UH * GT
LEAD = 10

def exp_steps():
    out = []
    for qb in range(2):
        for g in range(UH // GH):
            kts = GT * (qb + 1)
            for kt in range(kts):
                for pair in range(GH // 2):
                    out.append((qb, g, kt, pair, kt == 0, kt == kts - 1))
    return out

def max_steps():
    return [(i, half, h) for i in range(TPB) for half in range(1 + i // GT) for h in range(UH)]

MISC = ("shA", "shB", "xt", "q", "k", "v", "otr", "ao", "y")

def softmax_schedule():
    prep = [("stat", 0), ("xt", 0), ("q", 0), ("k", 0), ("v", 0), ("stat", 1), ("xt", 1), ("q", 1), ("k", 1), ("v", 1),
            ("store", 0)]
    prologue = prep + [("vpad", 0), ("stack", 0)]
    prologue += [("m", j) for j in range(M_FIRST)] + [("shA", 0)] + [("m", j) for j in range(M_FIRST, M_STEPS)]
    units = []
    for half in range(2):
        at = [[] for _ in range(E_STEPS)]
        at[0].append(("stack", 0))
        at[2].append(("shB", 0))
        if half == 1:
            at[1].append(("oev", -1))
            at[3].append(("otr", -1))
        for k, end in enumerate((8, 16, 32)):
            at[end + 1].append(("oev", k))
            at[end + 2].append(("otr", k))
        for j in range(M_STEPS):
            at[LEAD + j * (E_STEPS - LEAD) // M_STEPS].append(("m", j))
            if j == M_FIRST + 4:
                at[LEAD + j * (E_STEPS - LEAD) // M_STEPS].append(("shA", 0))
        if half == 0:
            for n, ev in zip((11, 13, 14, 15, 16, 19, 21, 22, 23, 24, 30), prep):
                at[n].append(ev)
        units.append(at)
    tail = [("oev", 3), ("otr", 3), ("vpad", 0), ("ao", 0), ("y", 0), ("ao", 1), ("y", 1)]
    return prologue, units, tail

def softmax_stage(nc, x, const, w, loaded, name):
    with ExitStack() as ctx:
        def sb(n, shape, dt=F32):
            return ctx.enter_context(nc.sbuf_tensor(f"{name}_{n}", shape, dt))

        def sem(n):
            return nc.alloc_semaphore(f"{name}_{n}")

        banks = Banks(const["psum"])
        e_ps = banks.take(2, 2, BLK)
        m_ps = banks.take(2, BLK)
        o_ps = banks.take(BLK)
        misc_ps = banks.take(GT, P)
        norm = Prenorm(nc, ctx, const, x, name + "_n", parities=1, xt_ps=misc_ps)
        full = sb("full", [P, BLK])
        rest = sb("rest", [P, BLK])
        parts = sb("parts", [P, 2, PARTS, SEQ], BF16)
        stack = sb("stack", [ROWS, 2, 2, UH, SEQ], BF16)
        v_raw = sb("v_raw", [P, TPB, P])
        v_pad = sb("v_pad", [P, TPB, HEADS, VW])
        prob = sb("prob", [P, 3, 2, BLK])
        mx = sb("mx", [P, TPB, 2, UH])
        neg = sb("neg", [P, 2, GT, UH])
        mt = sb("mt", [UH, BLK])
        mt_rest = sb("mt_rest", [UH, BLK])
        mt_parts = sb("mt_parts", [UH, PARTS, BLK], BF16)
        o_sb = sb("o_sb", [P, BLK])
        rsum = sb("rsum", [P, GT, GH])
        ao = sb("ao", [P, TPB, HEADS, HD])
        aot = sb("aot", [P, BLK])

        parts_dram = nc.dram_tensor(f"{name}_parts_dram", [2, PARTS, P, SEQ], BF16, kind="Internal").ap()

        init_done, parts_link, parts_ready = sem("init_done"), sem("parts_link"), sem("parts_ready")
        stack_loaded, shift_loaded = sem("stack_loaded"), sem("shift_loaded")
        score_ready, exp_done, pv_done = sem("score_ready"), sem("exp_done"), sem("pv_done")
        m_ready, m_done = sem("m_ready"), sem("m_done")
        neg_link, neg_ready, mt_link, mt_ready = sem("neg_link"), sem("neg_ready"), sem("mt_link"), sem("mt_ready")
        vpad_ready = sem("vpad_ready")
        o_copied, rsum_ready = sem("o_copied"), sem("rsum_ready")
        misc_ready, misc_used = sem("misc_ready"), sem("misc_used")
        pad_loaded, parts_stored = sem("pad_loaded"), sem("parts_stored")

        PROLOGUE, UNITS, TAIL = softmax_schedule()
        ESTEPS, MSTEPS = exp_steps(), max_steps()
        before = sum(ev[0] in MISC for ev in PROLOGUE)
        body_events = [(half, ev) for half in range(2) for step in UNITS[half] for ev in step] + [(2, ev) for ev in TAIL]
        place = {key: n for n, key in enumerate(k for k in body_events if k[1][0] in MISC)}
        place.update({(-1, ev): n for n, ev in enumerate(e for e in PROLOGUE if e[0] in MISC)})
        per_body = sum(ev[0] in MISC for _, ev in body_events)
        DMAS = 2 * PARTS * PARTS + 1

        NEXT_UNIT = ("stack", "m", "shA")
        NEXT_BATCH = ("store", "stat", "xt", "q", "k", "v", "vpad")

        def skip(half, ev, more):
            return not more and (ev[0] in NEXT_BATCH or (half == 1 and ev[0] in NEXT_UNIT))

        def run(eng, event, step=lambda n, u, par, b: None, unit_end=lambda u, par: None):
            for ev in PROLOGUE:
                event(ev, place.get((-1, ev), 0), 0, 0, 0)

            def body(b, more):
                skipped = 0
                for half in range(3):
                    steps = UNITS[half] if half < 2 else [TAIL]
                    for n, events in enumerate(steps):
                        if half < 2:
                            step(n, 2 * b + half, half, b)
                        for ev in events:
                            misc = 0
                            if ev[0] in MISC:
                                misc = before + per_body * b + place[half, ev] - skipped
                            if skip(half, ev, more):
                                skipped += ev[0] in MISC
                            elif ev[0] in NEXT_UNIT:
                                event(ev, misc, 2 * b + half + 1, 1 - half, b + half)
                            elif ev[0] in NEXT_BATCH:
                                event(ev, misc, 0, 0, b + 1)
                            else:
                                event(ev, misc, 2 * b + min(half, 1), min(half, 1), b)
                    if half < 2:
                        unit_end(2 * b + half, half)

            with eng.Fori(0, BATCH - 1) as b:
                body(b, True)
            body(BATCH - 1, False)

        def zeroth(u):
            return isinstance(u, int) and u == 0

        block = ctx.enter_context(nc.Block())

        @block.sync
        def _(sp):
            rows = slice(STACK + PARTS, ROWS)
            flat = stack[:, :, :, :, :].rearrange("r u i h n -> r (u i) (h n)")
            sp.dma_start(flat[rows, :, :], w["dram_zero"].unsqueeze(1).to_broadcast([ROWS - STACK - PARTS, 4, UH * SEQ]))\
                .then_inc(pad_loaded, 16)
            for par in range(2):
                sp.dma_start(flat[STACK:STACK + PARTS, 2 * par + 1, :],
                             w["dram_one"].to_broadcast([PARTS, UH * SEQ])).then_inc(pad_loaded, 16)

            def event(ev, misc, u, par, b):
                if ev[0] == "store":
                    sp.wait_ge(stack_loaded, 32 * DMAS * b)
                    sp.wait_ge(pad_loaded, 48)
                    sp.wait_ge(parts_ready, 4 * b + 4)
                    sp.dma_start(parts_dram.rearrange("i a c n -> c i a n"), parts[:, :, :, :]).then_inc(parts_stored, 16)
                if ev[0] == "stack":
                    if not zeroth(u):
                        sp.wait_ge(score_ready, E_STEPS * (u - 1))
                    sp.wait_ge(parts_stored, 16 * (b + 1))
                    for s in range(PARTS * PARTS):
                        for i, part in ((0, s // PARTS), (1, s % PARTS)):
                            src = parts_dram[i, part, UH * HD * par:UH * HD * (par + 1), :]
                            sp.dma_start(stack[HD * s:HD * (s + 1), par, i, :, :],
                                         src.rearrange("(h r) n -> r h n", r=HD)).then_inc(stack_loaded, 16)
                    sp.dma_start(flat[STACK:STACK + PARTS, 2 * par, :],
                                 w["dram_zero"].to_broadcast([PARTS, UH * SEQ])).then_inc(stack_loaded, 16)
                if ev[0] in ("shA", "shB"):
                    qb = int(ev[0] == "shB")
                    sp.wait_ge(mt_ready, 2 * u + 1 + qb)
                    for i in range(PARTS):
                        sp.dma_start(stack[STACK + i:STACK + i + 1, par, 0, :, qb * BLK:(qb + 1) * BLK],
                                     mt_parts[:, i, :]).then_inc(shift_loaded, 16)

            run(sp, event)

        @block.gpsimd
        def _(pool):
            nc.gpsimd.memset(v_pad[:, :, :, HD + 1:VW], 0.0)
            nc.gpsimd.memset(v_pad[:, :, :, HD:HD + 1], 1.0).then_inc(init_done, 1)

            def event(ev, misc, u, par, b):
                if ev[0] == "stat":
                    norm.invert(pool, 2 * b + ev[1])
                if ev[0] in ("q", "k"):
                    i, p = int(ev[0] == "k"), ev[1]
                    n = 4 * b + 2 * p + i
                    cols = slice(p * BLK, (p + 1) * BLK)
                    pool.wait_ge(misc_used, misc + 1)
                    nc.gpsimd.tensor_tensor(rest[:, :], full[:, :], parts[:, i, 0, cols], ALU.subtract)
                    nc.gpsimd.tensor_tensor(parts[:, i, 1, cols], full[:, :], parts[:, i, 0, cols], ALU.subtract)\
                        .then_inc(parts_link, 1)
                    pool.wait_ge(parts_link, n + 1)
                    nc.gpsimd.tensor_tensor(parts[:, i, 2, cols], rest[:, :], parts[:, i, 1, cols], ALU.subtract)\
                        .then_inc(parts_ready, 1)
                if ev[0] in ("shA", "shB"):
                    n = 2 * u + int(ev[0] == "shB")
                    pool.wait_ge(misc_used, misc + 1)
                    nc.gpsimd.tensor_tensor(mt_rest[:, :], mt[:, :], mt_parts[:, 0, :], ALU.subtract)
                    nc.gpsimd.tensor_tensor(mt_parts[:, 1, :], mt[:, :], mt_parts[:, 0, :], ALU.subtract)\
                        .then_inc(mt_link, 1)
                    pool.wait_ge(mt_link, n + 1)
                    nc.gpsimd.tensor_tensor(mt_parts[:, 2, :], mt_rest[:, :], mt_parts[:, 1, :], ALU.subtract)\
                        .then_inc(mt_ready, 1)

            run(pool, event)

        @block.tensor
        def _(pe):
            pe.wait_ge(*loaded)
            pe.wait_ge(pad_loaded, 48)
            pe.wait_ge(init_done, 1)

            def scores(n, u, par):
                qb, g, kt, pair, _, _ = ESTEPS[n]
                diag = kt - GT * qb
                lo = P * max(diag, 0)
                if n == 0:
                    pe.wait_ge(shift_loaded, 16 * PARTS * (2 * u + 1))
                if n == E_STEPS // 3:
                    pe.wait_ge(shift_loaded, 16 * PARTS * (2 * u + 2))
                pe.wait_ge(exp_done, E_STEPS * u + max(n - 1, 0))
                for j in range(2):
                    h = GH * g + 2 * pair + j
                    out = e_ps[:, n % 2, j, lo:BLK]
                    ins = pe.matmul(out, stack[:, par, 1, h, kt * P:(kt + 1) * P],
                                    stack[:, par, 0, h, qb * BLK + lo:(qb + 1) * BLK], start=True, stop=(diag < 0))
                    if diag >= 0:
                        ins = pe.matmul(e_ps[:, n % 2, j, lo:lo + P], w["ident_bf"][:, :], w["causal_kq"][:, :],
                                        start=False, stop=True)
                ins.then_inc(score_ready, 1)

            def values(n, u, par):
                qb, g, kt, pair, first, last = ESTEPS[n]
                lo = P * max(kt - GT * qb, 0)
                pe.wait_ge(exp_done, E_STEPS * u + n + 1)
                if first and pair == 0:
                    k = 2 * qb + g
                    pe.wait_ge(o_copied, 4 * u + k)
                for j in range(2):
                    q = 2 * pair + j
                    head = UH * par + GH * g + q
                    ins = pe.matmul(o_ps[VW * q:VW * (q + 1), lo:BLK], v_pad[:, kt, head, :],
                                    prob[:, n % 3, j, lo:BLK], start=first, stop=last, skip_group_check=True,
                                    tile_position=(0, VW * q))
                ins.then_inc(pv_done, 1)

            def step(n, u, par, b):
                scores(n, u, par)
                if n == 0:
                    pe.wait_ge(vpad_ready, b + 1)
                if n >= 1:
                    values(n - 1, u, par)

            def unit_end(u, par):
                values(E_STEPS - 1, u, par)

            def event(ev, misc, u, par, b):
                kind = ev[0]
                if kind in MISC:
                    pe.wait_ge(misc_used, misc)
                if kind == "xt":
                    pe.wait_ge(norm.xn_ready, 2 * b + ev[1] + 1)
                    for j in range(GT):
                        ins = pe.transpose(misc_ps[:, j, :], norm.xn[:, j, :], const["ident"][:, :])
                    ins.then_inc(misc_ready, 1)
                if kind in ("q", "k"):
                    pe.matmul(misc_ps[:, :, :], w[kind][:, :], norm.xt[:, 0, :], start=True, stop=True)\
                        .then_inc(misc_ready, 1)
                if kind == "v":
                    for j in range(GT):
                        pe.matmul(misc_ps[:, j, :], norm.xt[:, 0, j * P:(j + 1) * P], w["v"][:, :], start=True, stop=False)
                        ins = pe.matmul(misc_ps[:, j, :], const["ones"][0:1, 0:P], w["v_b"][:, :], start=False, stop=True)
                    ins.then_inc(misc_ready, 1)
                if kind == "m":
                    i, half, h = MSTEPS[ev[1]]
                    width = min(BLK, (i + 1) * P - half * BLK)
                    diag = half == i // GT
                    if ev[1] == 0:
                        pe.wait_ge(stack_loaded, 16 * DMAS * (u + 1))
                    pe.wait_ge(m_done, M_STEPS * u + max(ev[1] - 1, 0))
                    ins = pe.matmul(m_ps[:, ev[1] % 2, 0:width], stack[:, par, 0, h, i * P:(i + 1) * P],
                                    stack[:, par, 1, h, half * BLK:half * BLK + width], start=True, stop=not diag)
                    if diag:
                        ins = pe.matmul(m_ps[:, ev[1] % 2, width - P:width], w["ident_bf"][:, :],
                                        w["causal_qk"][:, :], start=False, stop=True)
                    ins.then_inc(m_ready, 1)
                if kind in ("shA", "shB"):
                    n = 2 * u + int(kind == "shB")
                    pe.wait_ge(neg_ready, n + 1)
                    for j in range(GT):
                        ins = pe.transpose(misc_ps[0:UH, j, :], neg[:, int(kind == "shB"), j, :], const["ident"][:, :])
                    ins.then_inc(misc_ready, 1)
                if kind == "otr":
                    pe.wait_ge(o_copied, 4 * u + ev[1] + 1)
                    for j in range(GT):
                        ins = pe.transpose(misc_ps[:, j, :], o_sb[:, j * P:(j + 1) * P], const["ident"][:, :])
                    ins.then_inc(misc_ready, 1)
                if kind == "ao":
                    for j in range(GT):
                        ins = pe.transpose(misc_ps[:, j, :], ao[:, GT * ev[1] + j, :, :], const["ident"][:, :])
                    ins.then_inc(misc_ready, 1)
                if kind == "y":
                    for j in range(GT):
                        pe.matmul(misc_ps[:, j, :], aot[:, j * P:(j + 1) * P], w["o"][:, :], start=True, stop=False)
                        ins = pe.matmul(misc_ps[:, j, :], const["ones"][0:1, 0:P], w["o_b"][:, :], start=False, stop=True)
                    ins.then_inc(misc_ready, 1)

            run(pe, event, step, unit_end)

        @block.scalar
        def _(act):
            act.wait_ge(*loaded)
            act.wait_ge(init_done, 1)

            def step(n, u, par, b):
                qb, g, kt, pair, _, _ = ESTEPS[n]
                lo = P * max(kt - GT * qb, 0)
                act.wait_ge(score_ready, E_STEPS * u + n + 1)
                act.wait_ge(pv_done, E_STEPS * u + max(n - 2, 0))
                nc.scalar.activation(prob[:, n % 3, :, lo:BLK], e_ps[:, n % 2, :, lo:BLK], ACT.Exp,
                                     scale=float(HD) ** -0.5).then_inc(exp_done, 1)

            def event(ev, misc, u, par, b):
                if ev[0] == "xt":
                    act.wait_ge(misc_ready, misc + 1)
                    cut = BLK // 2
                    nc.scalar.copy(norm.xt[:, 0, 0:cut], misc_ps[:, 0:GT // 2, :]).then_inc(norm.xt_ready, 1)
                    nc.scalar.copy(norm.xt[:, 0, cut:BLK], misc_ps[:, GT // 2:GT, :]).then_inc(misc_used, 1)
                if ev[0] in ("q", "k"):
                    i, p = int(ev[0] == "k"), ev[1]
                    act.wait_ge(misc_ready, misc + 1)
                    act.wait_ge(parts_ready, 4 * b + 2 * p + i)
                    nc.scalar.activation(full[:, :], misc_ps[:, :, :], ACT.Identity, bias=w["qk_b"][:, i:i + 1])
                    act.wait_ge(stack_loaded, 16 * DMAS * 2 * b)
                    nc.scalar.activation(parts[:, i, 0, p * BLK:(p + 1) * BLK], misc_ps[:, :, :], ACT.Identity,
                                         bias=w["qk_b"][:, i:i + 1]).then_inc(misc_used, 1)
                if ev[0] == "v":
                    act.wait_ge(misc_used, misc + 1)
                if ev[0] == "vpad":
                    act.wait_ge(pv_done, 2 * E_STEPS * b)
                    nc.scalar.copy(v_pad[:, :, :, 0:HD], v_raw[:, :, :].rearrange("p t (h d) -> p t h d", d=HD))\
                        .then_inc(vpad_ready, 1)
                if ev[0] == "ao":
                    act.wait_ge(misc_ready, misc + 1)
                    nc.scalar.copy(aot[:, :], misc_ps[:, :, :]).then_inc(misc_used, 1)

            run(act, event, step)

        @block.vector
        def _(dve):
            dve.wait_ge(*loaded)

            def event(ev, misc, u, par, b):
                kind = ev[0]
                if kind == "stat":
                    norm.statistics(dve, 2 * b + ev[1])
                    norm.scale(dve, 2 * b + ev[1], xn_free=norm.xt_ready)
                if kind == "v":
                    p = ev[1]
                    dve.wait_ge(misc_ready, misc + 1)
                    dve.wait_ge(vpad_ready, b)
                    nc.vector.tensor_copy(v_raw[:, GT * p:GT * (p + 1), :], misc_ps[:, :, :]).then_inc(misc_used, 1)
                if kind == "m":
                    i, half, h = MSTEPS[ev[1]]
                    width = min(BLK, (i + 1) * P - half * BLK)
                    dve.wait_ge(m_ready, M_STEPS * u + ev[1] + 1)
                    nc.vector.tensor_reduce(mx[:, i, half, h:h + 1], m_ps[:, ev[1] % 2, 0:width], AX.X, ALU.max)\
                        .then_inc(m_done, 1)
                    if ev[1] == M_FIRST - 1:
                        dve.wait_ge(m_done, M_STEPS * u + M_FIRST)
                        nc.vector.tensor_scalar(neg[:, 0, :, :], mx[:, 0:GT, 0, :], -1.0, None, ALU.mult)\
                            .then_inc(neg_ready, 1)
                    if ev[1] == M_STEPS - 1:
                        dve.wait_ge(m_done, M_STEPS * (u + 1))
                        nc.vector.tensor_tensor(neg[:, 1, :, :], mx[:, GT:TPB, 0, :], mx[:, GT:TPB, 1, :], ALU.max)\
                            .then_inc(neg_link, 1)
                        dve.wait_ge(neg_link, u + 1)
                        nc.vector.tensor_scalar(neg[:, 1, :, :], neg[:, 1, :, :], -1.0, None, ALU.mult)\
                            .then_inc(neg_ready, 1)
                if kind in ("shA", "shB"):
                    n = 2 * u + int(kind == "shB")
                    dve.wait_ge(misc_ready, misc + 1)
                    dve.wait_ge(mt_ready, n)
                    dve.wait_ge(shift_loaded, 16 * PARTS * n)
                    nc.vector.tensor_copy(mt[:, :], misc_ps[0:UH, :, :])
                    nc.vector.tensor_copy(mt_parts[:, 0, :], misc_ps[0:UH, :, :]).then_inc(misc_used, 1)
                if kind == "oev":
                    k = 4 * u + ev[1]
                    end = (8, 16, 32, 48)[ev[1]] if ev[1] >= 0 else 0
                    dve.wait_ge(pv_done, E_STEPS * u + end)
                    dve.wait_ge(rsum_ready, k)
                    nc.vector.tensor_copy(o_sb[:, :], o_ps[:, :]).then_inc(o_copied, 1)
                if kind == "otr":
                    k = 4 * u + ev[1]
                    unit_par, group = (par, ev[1]) if ev[1] >= 0 else (1 - par, 3)
                    qb, g = group // 2, group % 2
                    dve.wait_ge(misc_ready, misc + 1)
                    heads = misc_ps[:, :, :].rearrange("p t (h c) -> p t h c", c=VW)
                    nc.vector.reciprocal(rsum[:, :, :], heads[:, :, :, HD]).then_inc(rsum_ready, 1)
                    dve.wait_ge(rsum_ready, k + 1)
                    head = UH * unit_par + GH * g
                    nc.vector.tensor_tensor(ao[:, GT * qb:GT * (qb + 1), head:head + GH, :], heads[:, :, :, 0:HD],
                                            wide(rsum[:, :, :], HD), ALU.mult).then_inc(misc_used, 1)
                if kind == "y":
                    dve.wait_ge(misc_ready, misc + 1)
                    xq = x[:, bass.ds(b * TPB + GT * ev[1], GT), :]
                    nc.vector.tensor_tensor(xq, misc_ps[:, :, :], xq, ALU.add).then_inc(misc_used, 1)

            run(dve, event)

def hybrid_kernel(nc, arrays, out):
    with ExitStack() as ctx:
        def resident(prefix):
            names = [n for n in arrays if n.startswith(prefix)]
            homes, copies = {}, []
            for n in names:
                src, key = arrays[n], n[len(prefix):]
                if key.startswith("dram_"):
                    homes[key] = src
                    continue
                shape = list(src.shape)
                if key in ROW_FOR_ALL:
                    shape[0] = P
                    src = src.to_broadcast(shape)
                homes[key] = ctx.enter_context(nc.sbuf_tensor("s_" + n, shape, src.dtype))
                index = tuple(slice(None) for _ in shape)
                copies.append((homes[key][index], src))
            return homes, copies

        x = ctx.enter_context(nc.sbuf_tensor("x", [P, TILES, P], F32))
        load_first = ctx.enter_context(nc.semaphore("load_first"))
        load_rest = ctx.enter_context(nc.semaphore("load_rest"))
        const, const_copies = resident("const_")
        mamba, mamba_copies = resident("mamba_")
        const["psum"] = ctx.enter_context(nc.psum_tensor("psum", [P, 8, BLK], F32))
        ffn0, ffn0_copies = resident("ffn0_")
        lin, lin_copies = resident("lin_")
        first = [(x[:, :, :], arrays["x"].rearrange("b (t p) c -> p (b t) c", p=P))] + const_copies + mamba_copies
        rest = ffn0_copies + lin_copies

        with nc.Block() as block:
            @block.sync
            def _(sp):
                for dst, src in first:
                    sp.dma_start(dst, src).then_inc(load_first, 16)
                for dst, src in rest:
                    sp.dma_start(dst, src).then_inc(load_rest, 16)

        have_first, have_rest = (load_first, 16 * len(first)), (load_rest, 16 * len(rest))
        def stage(build, *args, **kwargs):
            with nc.cleanup_on_exit():
                build(nc, *args, **kwargs)

        stage(mamba_stage, x, const, mamba, have_first, "mamba")
        ret, ret_copies = resident("ret_")
        soft, soft_copies = resident("soft_")
        layer1 = ret_copies + soft_copies
        ffn1_copies = [(dst, arrays["ffn1_" + n]) for n, (dst, _) in zip(ffn0, ffn0_copies)]
        load_layer1 = ctx.enter_context(nc.semaphore("load_layer1"))
        load_ffn1 = ctx.enter_context(nc.semaphore("load_ffn1"))
        have_ffn1 = (load_ffn1, 16 * len(ffn1_copies))
        have_layer1 = (load_layer1, 16 * len(layer1))
        stage(ffn_stage, x, const, ffn0, have_rest, "ffn0a", fetch=(layer1, load_layer1))
        stage(linear_attention_stage, x, const, lin, have_rest, "lin")
        stage(ffn_stage, x, const, ffn0, have_rest, "ffn0b")
        stage(retention_stage, x, const, ret, have_layer1, "ret", fetch=(ffn1_copies, load_ffn1))
        stage(ffn_stage, x, const, ffn0, have_ffn1, "ffn1a")
        stage(softmax_stage, x, const, soft, have_layer1, "soft")
        stage(ffn_stage, x, const, ffn0, have_ffn1, "ffn1b", out=out.rearrange("b (t p) c -> p (b t) c", p=P))

ROW_FOR_ALL = ("a_log", "ln_g", "ln_b")

def host_layout(a):
    def t(m):
        return np.swapaxes(m, -1, -2)

    def ffn(p):
        w1 = np.concatenate([a[p + "eW1"], a[p + "sW1"][None]])
        w2 = np.concatenate([a[p + "eW2"], a[p + "sW2"][None]])
        return {
            "w1": w1.transpose(1, 0, 2), "w2": w2.transpose(1, 0, 2),
            "b1": t(np.concatenate([a[p + "eb1"], a[p + "sb1"][None]])),
            "b2": np.concatenate([a[p + "eb2"], a[p + "sb2"][None]]),
            "router": a[p + "router_W"], "router_b": a[p + "router_b"][None],
        }

    d_half = P
    m = "L0_attn_a_"
    mamba = {
        "in": t(a[m + "W_in"]).reshape(P, 2 * HALVES, P),
        "conv_w": a[m + "conv_w"].reshape(HALVES, d_half, CONV).transpose(1, 0, 2),
        "conv_b": t(a[m + "conv_b"].reshape(HALVES, d_half)),
        "xproj": t(a[m + "W_xproj"]).reshape(HALVES, d_half, NDBL).transpose(1, 0, 2),
        "a_log": a[m + "A_log"][None],
        "d": t(a[m + "D_param"].reshape(HALVES, d_half)),
        "out": t(a[m + "W_out"]).reshape(HALVES, d_half, P).transpose(1, 0, 2),
    }
    m = "L0_attn_b_"
    qkv = a[m + "qkv_weight"]
    lin = {"q": t(qkv[:P]), "kv": t(qkv[P:]), "proj": t(a[m + "proj_weight"]), "proj_b": a[m + "proj_bias"][None]}
    m = "L1_attn_a_"
    c = np.arange(P)
    head, swapped = c // HD4, c // HD4 * HD4 + (c + HD4 // 2) % HD4
    rows = [a[m + "Wq"], a[m + "Wq"][swapped], a[m + "Wk"], a[m + "Wk"][swapped]]
    rows += [a[m + "Wv"][head * HD4 + i] for i in range(HD4)]
    rows += [a[m + n][head * DECAYS + i] for n in ("Wbeta", "Wmix") for i in range(DECAYS)]
    ret = {
        "w": np.stack([t(r) for r in rows], axis=1),
        "b": np.stack([a[m + n][head * DECAYS + i] for n in ("bbeta", "bmix") for i in range(DECAYS)], axis=1),
        "out": t(a[m + "Wout"]), "out_b": a[m + "bout"][None],
        "ln_g": a[m + "ln_g"][None], "ln_b": a[m + "ln_b"][None],
    }
    m = "L1_attn_b_"
    qkv, b = a[m + "W_qkv"], a[m + "b_qkv"]
    soft = {
        "q": t(qkv[:P]), "k": t(qkv[P:2 * P]), "v": t(qkv[2 * P:]),
        "qk_b": t(b[:2 * P].reshape(2, P)), "v_b": b[None, 2 * P:],
        "o": t(a[m + "W_o"]), "o_b": a[m + "b_o"][None],
    }
    groups = shape_constants()
    for name, group in (("mamba", mamba), ("ffn0", ffn("L0_ffn_")), ("lin", lin), ("ret", ret),
                        ("ffn1", ffn("L1_ffn_")), ("soft", soft)):
        groups[name] = {**group, **groups.get(name, {})}
    sent = {"x": a["L0_attn_a_x"]}
    sent.update({f"{name}_{n}": v for name, group in groups.items() for n, v in group.items()})
    return {n: np.ascontiguousarray(v) for n, v in sent.items()}

def kernel(**inputs):
    import concourse.bacc as bacc
    from concourse.bass_utils import run_bass_kernel_spmd

    sent = host_layout({n: np.asarray(v) for n, v in inputs.items()})
    nc = bacc.Bacc("TRN2", target_bir_lowering=False, num_devices=1)
    arrays = {n: nc.dram_tensor("in_" + n, v.shape, mybir.dt.from_np(v.dtype), kind="ExternalInput").ap()
              for n, v in sent.items()}
    out = nc.dram_tensor("out_x", (BATCH, SEQ, P), F32, kind="ExternalOutput").ap()
    hybrid_kernel(nc, arrays, out)
    result = run_bass_kernel_spmd(nc, [{"in_" + n: v for n, v in sent.items()}], core_ids=[0])
    return result.results[0]["out_x"]
```

```python
from contextlib import ExitStack

import numpy as np

import concourse.bass as bass
from concourse import mybir

P = 128
BATCH, SEQ = 4, 1024
TILES = BATCH * SEQ // P
TPB = SEQ // P
GT = 4
BLK = GT * P
BLOCKS = TILES // GT
LN_EPS = 1e-5

F32 = mybir.dt.float32
F32R = mybir.dt.float32r
BF16 = mybir.dt.bfloat16
I32 = mybir.dt.int32
ALU = mybir.AluOpType
ACT = mybir.ActivationFunctionType
AX = mybir.AxisListType

class Chain:

    def __init__(self, eng, sem, base=0):
        self.eng, self.sem, self.base, self.n = eng, sem, base, 0

    def link(self, ins):
        self.n += 1
        ins.then_inc(self.sem, 1)
        self.eng.wait_ge(self.sem, self.base + self.n)

class Banks:

    def __init__(self, psum):
        self.psum, self.taken = psum, 0

    def take(self, *dims):
        n = int(np.prod(dims)) // BLK
        banks = self.psum[:, self.taken:self.taken + n, :].rearrange("p n k -> p (n k)")
        self.taken += n
        letters = " ".join("abcd"[:len(dims)])
        return banks.rearrange(f"p ({letters}) -> p {letters}", **dict(zip("abcd", dims)))

def wide(col, n):
    return col.unsqueeze(len(col.shape)).to_broadcast(list(col.shape) + [n])

def shape_constants():
    HOST_BF16 = mybir.dt.np(BF16)
    ident = np.eye(P, dtype=np.float32)
    d = np.arange(P) % 4
    inv_freq = (np.float32(1.0) / np.float32(10000.0) ** (np.arange(2, dtype=np.float32) / np.float32(2))).astype(np.float32)
    angle = np.arange(SEQ, dtype=np.float32)[None, :] * inv_freq[d % 2][:, None]
    later = np.triu(np.ones((P, P), np.float32), 1)
    minus = np.float32(-1e30)
    t = np.arange(P)
    chunk, middle = t // 32, t // 32 * 32 + 15
    same = chunk[:, None] == chunk[None, :]
    before_mid = (same & (t[:, None] <= middle[None, :])).astype(np.float32)
    to_target = (same & (t[:, None] <= t[None, :])).astype(np.float32)
    totals = (chunk[:, None] == np.arange(4)[None, :]).astype(np.float32)
    return {
        "const": {
            "ident": ident,
            "ones": np.ones((1, BLK), np.float32),
            "minus_half": np.full((P, 8), -0.5, np.float32),
            "head4": np.kron(np.eye(P // 4, dtype=np.float32), np.ones((4, 4), np.float32)),
            "order": np.tile(np.arange(15, 0, -1, dtype=np.float32), (P, GT, 1)),
        },
        "mamba": {
            "sum_mid": to_target - before_mid,
            "sum_rest": (same & (t[:, None] > t[None, :])).astype(np.float32),
            "sum_sel": np.concatenate([totals, totals * (t <= middle).astype(np.float32)[:, None]], axis=1),
            "chunk_mask": totals,
            "chunk_causal": to_target,
            "ones_col": np.ones((P, 1), np.float32),
        },
        "ret": {
            "head_sel": np.kron(np.eye(P // 4, dtype=np.float32), np.ones((4, 1), np.float32)),
            "half": np.full((P, 1), 0.5, np.float32),
            "cos": np.cos(angle),
            "sin": np.sin(angle) * np.where(d < 2, -1, 1).astype(np.float32)[:, None],
        },
        "soft": {
            "ident_bf": ident.astype(HOST_BF16),
            "causal_kq": (later.T * minus).astype(HOST_BF16),
            "causal_qk": (later * minus).astype(HOST_BF16),
            "dram_zero": np.zeros((1, 8 * SEQ), HOST_BF16),
            "dram_one": np.ones((1, 8 * SEQ), HOST_BF16),
        },
    }

class Prenorm:

    def __init__(self, nc, ctx, const, x, name, xt_ps, parities=2):
        self.nc, self.const, self.x = nc, const, x

        def sb(n, shape):
            return ctx.enter_context(nc.sbuf_tensor(f"{name}_{n}", shape, F32))

        def sem(n):
            return nc.alloc_semaphore(f"{name}_{n}")

        self.stats = sb("stats", [P, GT, 6])
        self.mv = sb("mv", [P, GT, 2])
        self.rstd = sb("rstd", [P, GT])
        self.pause = sb("pause", [1, 4])
        self.xn = sb("xn", [P, GT, P])
        self.xt = sb("xt", [P, parities, BLK])
        self.xt_ps = xt_ps
        self.stat_link, self.stats_ready = sem("stat_link"), sem("stats_ready")
        self.rstd_ready, self.xn_ready = sem("rstd_ready"), sem("xn_ready")
        self.xt_ps_ready, self.xt_ready = sem("xt_ps_ready"), sem("xt_ready")

    def statistics(self, dve, q, tile=None):
        self.moments(dve, q, tile)
        self.aggregate(dve, q)

    def moments(self, dve, q, tile=None):
        tile = tile or (lambda j: q * GT + j)
        dve.wait_ge(self.xn_ready, q)
        for j in range(GT):
            ins = self.nc.vector.bn_stats(self.stats[:, j, :], self.x[:, tile(j), :])
        ins.then_inc(self.stat_link, 1)

    def aggregate(self, dve, q):
        dve.wait_ge(self.stat_link, 2 * q + 1)
        self.nc.vector.memset(self.pause[:, 0:1], 0.0)
        for j in range(GT):
            ins = self.nc.vector.bn_aggr(self.mv[:, j, :], self.stats[:, j, :])
        ins.then_inc(self.stat_link, 1)
        dve.wait_ge(self.stat_link, 2 * q + 2)
        self.nc.vector.tensor_scalar_add(self.mv[:, :, 1], self.mv[:, :, 1], LN_EPS).then_inc(self.stats_ready, 1)

    def invert(self, pool, q):
        pool.wait_ge(self.stats_ready, q + 1)
        self.nc.gpsimd.tensor_tensor(self.rstd[:, :], self.mv[:, :, 1], self.const["minus_half"][:, 0:GT],
                                     ALU.pow).then_inc(self.rstd_ready, 1)

    def scale(self, dve, q, tile=None, xn_used=None, xn_free=None):
        tile = tile or (lambda j: q * GT + j)
        dve.wait_ge(self.rstd_ready, q + 1)
        dve.wait_ge(xn_free if xn_free is not None else self.xt_ps_ready, q)
        if xn_used is not None:
            dve.wait_ge(xn_used, q)
        for j in range(GT):
            ins = self.nc.vector.tensor_scalar(self.xn[:, j, :], self.x[:, tile(j), :], self.mv[:, j, 0:1],
                                               self.rstd[:, j:j + 1], ALU.subtract, ALU.mult)
        ins.then_inc(self.xn_ready, 1)

    def transpose(self, pe, q):
        pe.wait_ge(self.xn_ready, q + 1)
        pe.wait_ge(self.xt_ready, q)
        for j in range(GT):
            ins = pe.transpose(self.xt_ps[:, j, :], self.xn[:, j, :], self.const["ident"][:, :])
        ins.then_inc(self.xt_ps_ready, 1)

    def copy(self, act, q, p, xt_used=None):
        act.wait_ge(self.xt_ps_ready, q + 1)
        if xt_used is not None:
            act.wait_ge(*xt_used)
        self.nc.scalar.copy(self.xt[:, p, :], self.xt_ps[:, :, :]).then_inc(self.xt_ready, 1)

NS = 16
SW = 32
DI = 2 * P
HALVES = 2
CONV = 4
CHUNK = 32
CHUNKS = P // CHUNK
NDBL = 2 * NS + 1
DT_MIN, DT_MAX = 0.001, 0.1
DECAY_FLOOR, INPUT_CLIP, STATE_CLIP = -20.0, 10.0, 100.0
STATE_PROVED, LOG_PROVED = 99.0, 40.0
DT_LO, DT_HI = -8.0, -2.2
STEP_ROWS = 16

def mamba_stage(nc, x, const, w, loaded, name):
    with ExitStack() as ctx:
        def sb(n, shape, dt=F32):
            return ctx.enter_context(nc.sbuf_tensor(f"{name}_{n}", shape, dt))

        def sem(n):
            return nc.alloc_semaphore(f"{name}_{n}")

        y = sb("y", [P, HALVES, BATCH, SEQ])
        gate = sb("gate", [P, HALVES, BATCH, SEQ])
        xc = sb("xc", [P, HALVES, BATCH, SEQ])
        flag = sb("flag", [1, 1], I32)
        coef_dram = nc.dram_tensor(f"{name}_coef_dram", [SEQ, 3 * BATCH * NS], F32, kind="Internal").ap()
        mamba_scan(nc, x, const, w, loaded, name, y, gate, xc, flag, coef_dram)
        mamba_steps(nc, name, y, xc, flag, coef_dram)
        mamba_output(nc, x, const, w, name, y, gate, xc)

def mamba_scan(nc, x, const, w, loaded, name, y, gate, xc, flag, coef_dram):
    with ExitStack() as ctx:
        def sb(n, shape, dt=F32):
            return ctx.enter_context(nc.sbuf_tensor(f"{name}_{n}", shape, dt))

        def sem(n):
            return nc.alloc_semaphore(f"{name}_{n}")

        banks = Banks(const["psum"])
        tr_ps = banks.take(GT, P)
        ring_ps = banks.take(2, BATCH, P)
        small_ps = banks.take(BLK)
        g_ps = tr_ps
        y_ps = banks.take(HALVES, BATCH, P)
        u_ps = banks.take(CHUNKS, DI)
        DBL, CUM, REST, SEL = 0, 160, 288, 416
        norm = Prenorm(nc, ctx, const, x, name + "_n", parities=1, xt_ps=tr_ps)

        xp = sb("xp", [P, HALVES, BATCH, CONV - 1 + P])
        tz = sb("tz", [P, HALVES, BATCH, P])
        cv = sb("cv", [P, HALVES, BATCH, P])
        tc = sb("tc", [P, HALVES, BATCH, P])
        xc_now = sb("xc_now", [P, HALVES, BATCH, P])
        xtok = sb("xtok", [P, BATCH, DI])
        dbl = sb("dbl", [P, BATCH, NDBL])
        dt1 = sb("dt1", [P, 6, BATCH])
        la = sb("la", [P, BATCH, SW])
        bbar = sb("bbar", [P, BATCH, SW])
        cc = sb("cc", [P, BATCH, SW])
        cum = sb("cum", [P, BATCH * SW])
        e_pos = sb("e_pos", [P, BATCH * SW])
        e_neg = sb("e_neg", [P, BATCH * SW])
        e_rest = sb("e_rest", [P, BATCH * SW])
        coef = sb("coef", [P, 4, BATCH * SW])
        wk = sb("wk", [P, CHUNKS, BATCH * SW])
        out_coef = sb("out_coef", [P, 3, BATCH, NS])
        bt = sb("bt", [P, P])
        ct = sb("ct", [P, BATCH, P])
        bound_a = sb("bound_a", [P, SEQ])
        bound_v = sb("bound_v", [P, SEQ])
        gt = sb("gt", [P, BATCH, P])
        sel = sb("sel", [P, 2 * CHUNKS])
        hm = sb("hm", [P, CHUNKS, DI])
        h = sb("h", [P, CHUNKS, DI])
        umax = sb("umax", [P, BATCH])
        cmax = sb("cmax", [P, TPB])
        verdict = sb("verdict", [P, 4])
        neg_a = sb("neg_a", [P, NS])

        init_done, a_ready = sem("init_done"), sem("a_ready")
        ring_ready, ring_used = sem("ring_ready"), sem("ring_used")
        halo_done, tz_done, cv_ready = sem("halo_done"), sem("tz_done"), sem("cv_ready")
        tc_done, xc2_ready, xc_ready, kept = sem("tc_done"), sem("xc2_ready"), sem("xc_ready"), sem("kept")
        dbl_ready, dtexp_ready, dtexp_done = sem("dbl_ready"), sem("dtexp_ready"), sem("dtexp_done")
        la_ready, sums_ready, exps_done = sem("la_ready"), sem("sums_ready"), sem("exps_done")
        coef_ready, tr_ready, tr_used = sem("coef_ready"), sem("tr_ready"), sem("tr_used")
        g_ready, gt_ready, u_ready = sem("g_ready"), sem("gt_ready"), sem("u_ready")
        hm_ready, y_ready, y_copied = sem("hm_ready"), sem("y_ready"), sem("y_copied")
        link_sem, coef_stored, verdict_ready, sum_ready, flag_ready = (
            sem("link"), sem("coef_stored"), sem("verdict_ready"), sem("sum_ready"), sem("flag_ready"))
        out_coef_ready, conv_link, prep_link = sem("out_coef_ready"), sem("conv_link"), sem("prep_link")

        block = ctx.enter_context(nc.Block())
        RING = 6

        def tiles(eng, scan):
            with eng.Fori(0, TPB - 2) as tt:
                scan(tt, 2)
            scan(TPB - 2, 1)
            scan(TPB - 1, 0)

        @block.sync
        def _(sp):
            with sp.Fori(0, TPB) as tt:
                sp.wait_ge(out_coef_ready, tt + 1)
                sp.dma_start(coef_dram[bass.ds(tt * P, P), :], out_coef[:, :, :, :]).then_inc(coef_stored, 16)
            sp.wait_ge(coef_stored, 16 * TPB)

        @block.gpsimd
        def _(pool):
            nc.gpsimd.memset(la[:, :, :], 0.0)
            nc.gpsimd.memset(bbar[:, :, :], 0.0)
            nc.gpsimd.memset(cc[:, :, :], 0.0)
            nc.gpsimd.memset(ct[:, :, :], 0.0)
            nc.gpsimd.memset(h[:, :, :], 0.0)
            nc.gpsimd.memset(xp[:, :, :, 0:CONV - 1], 0.0).then_inc(init_done, 1)

            def scan(tt, more):
                pool.wait_ge(init_done, 1)
                pool.wait_ge(xc_ready, tt + 1)
                nc.gpsimd.tensor_copy(xc[:, :, :, bass.ds(tt * P, P)], xc_now[:, :, :, :]).then_inc(kept, 1)
                if more == 2:
                    norm.invert(pool, tt + 2)

            norm.invert(pool, 0)
            norm.invert(pool, 1)
            tiles(pool, scan)

        @block.tensor
        def _(pe):
            pe.wait_ge(*loaded)
            pe.wait_ge(init_done, 1)

            def project(a, tr_free):
                pe.wait_ge(norm.xn_ready, a + 1)
                pe.wait_ge(gt_ready, tr_free)
                for j in range(BATCH):
                    ins = pe.transpose(tr_ps[:, j, :], norm.xn[:, j, :], const["ident"][:, :])
                ins.then_inc(norm.xt_ps_ready, 1)
                pe.wait_ge(norm.xt_ready, a + 1)
                for i in range(2 * HALVES):
                    pe.wait_ge(ring_used, RING * a + max(i - 1, 0))
                    pe.matmul(ring_ps[:, i % 2, :, :], w["in"][:, i, :], norm.xt[:, 0, :], start=True, stop=True)\
                        .then_inc(ring_ready, 1)

            def step_inputs(a):
                pe.wait_ge(xc_ready, a + 1)
                for b in range(BATCH):
                    for i in range(HALVES):
                        ins = pe.matmul(small_ps[:, DBL + NDBL * b:DBL + NDBL * (b + 1)], xc_now[:, i, b, :],
                                        w["xproj"][:, i, :], start=(i == 0), stop=(i == HALVES - 1), skip_group_check=True)
                ins.then_inc(dbl_ready, 1)

            def decay_sums(a):
                pe.wait_ge(la_ready, a + 1)
                pe.matmul(small_ps[:, CUM:CUM + P], w["sum_mid"][:, :], la[:, :, :], start=True, stop=True,
                          skip_group_check=True)
                pe.matmul(small_ps[:, REST:REST + P], w["sum_rest"][:, :], la[:, :, :], start=True, stop=True,
                          skip_group_check=True)
                pe.matmul(small_ps[:, SEL:SEL + 2 * CHUNKS], la[:, :, :], w["sum_sel"][:, :], start=True, stop=True,
                          skip_group_check=True).then_inc(sums_ready, 1)

            def scan(tt, more):
                for i in range(HALVES):
                    pe.wait_ge(ring_used, RING * tt + 4 + i - 1)
                    for b in range(BATCH):
                        ins = pe.transpose(ring_ps[:, i, b, :], xc_now[:, i, b, :], const["ident"][:, :])
                    ins.then_inc(ring_ready, 1)
                if more:
                    project(tt + 1, tt)
                pe.wait_ge(coef_ready, tt + 1)
                for i in range(4):
                    ins = pe.transpose(tr_ps[:, i, :], coef[:, i, :], const["ident"][:, :])
                ins.then_inc(tr_ready, 1)
                pe.wait_ge(tr_used, tt + 1)
                pe.matmul(g_ps[:, :, :], bt[:, :], ct[:, :, :], start=True, stop=True).then_inc(g_ready, 1)
                pe.wait_ge(ring_used, RING * (tt + 1))
                for b in range(BATCH):
                    for k in range(CHUNKS):
                        ins = pe.matmul(u_ps[SW * b:SW * (b + 1), k, :], wk[:, k, SW * b:SW * (b + 1)], xtok[:, b, :],
                                        start=True, stop=True, skip_group_check=True, tile_position=(0, SW * b))
                ins.then_inc(u_ready, 1)
                pe.wait_ge(gt_ready, tt + 1)
                pe.wait_ge(y_copied, tt)
                for i in range(HALVES):
                    for b in range(BATCH):
                        pe.matmul(y_ps[:, i, b, :], xtok[:, b, P * i:P * (i + 1)], gt[:, b, :],
                                  start=(b == 0), stop=False, skip_group_check=True)
                if more:
                    step_inputs(tt + 1)
                pe.wait_ge(hm_ready, tt + 1)
                for i in range(HALVES):
                    for k in range(CHUNKS):
                        cols = slice(CHUNK * k, CHUNK * (k + 1))
                        ins = pe.matmul(y_ps[:, i, :, cols], hm[:, k, P * i:P * (i + 1)], ct[:, :, cols],
                                        start=False, stop=(k == CHUNKS - 1), skip_group_check=True)
                ins.then_inc(y_ready, 1)
                if more:
                    decay_sums(tt + 1)

            project(0, 0)
            step_inputs(0)
            decay_sums(0)
            tiles(pe, scan)
            pe.wait_ge(verdict_ready, 1)
            pe.matmul(small_ps[0:1, 0:1], verdict[:, 3:4], w["ones_col"][:, :], start=True, stop=True)\
                .then_inc(sum_ready, 1)

        @block.scalar
        def _(act):
            act.wait_ge(*loaded)
            act.wait_ge(init_done, 1)
            nc.scalar.activation(neg_a[:, :], w["a_log"][:, :], ACT.Exp).then_inc(a_ready, 1)

            def project(a):
                norm.copy(act, a, 0)
                for i in range(HALVES):
                    act.wait_ge(ring_ready, RING * a + i + 1)
                    act.wait_ge(halo_done, a)
                    nc.scalar.copy(xp[:, i, :, CONV - 1:], ring_ps[:, i, :, :]).then_inc(ring_used, 1)
                for i in range(HALVES):
                    act.wait_ge(ring_ready, RING * a + 2 + i + 1)
                    nc.scalar.activation(tz[:, i, :, :], ring_ps[:, i, :, :], ACT.Tanh, scale=0.5).then_inc(tz_done, 1)

            def silu(a):
                for i in range(HALVES):
                    act.wait_ge(cv_ready, HALVES * a + i + 1)
                    nc.scalar.activation(tc[:, i, :, :], cv[:, i, :, :], ACT.Tanh, scale=0.5).then_inc(tc_done, 1)
                act.wait_ge(xc2_ready, a + 1)
                act.wait_ge(kept, a)
                nc.scalar.mul(xc_now[:, :, :, :], tc[:, :, :, :], 0.5).then_inc(xc_ready, 1)

            def decays(a):
                act.wait_ge(hm_ready, a)
                act.wait_ge(sums_ready, a + 1)
                nc.scalar.activation(e_pos[:, :], small_ps[:, CUM:CUM + P], ACT.Exp)
                nc.scalar.activation(e_neg[:, :], small_ps[:, CUM:CUM + P], ACT.Exp, scale=-1.0)
                nc.scalar.activation(e_rest[:, :], small_ps[:, REST:REST + P], ACT.Exp)
                nc.scalar.activation(coef[:, 2, :], la[:, :, :], ACT.Exp)
                nc.scalar.activation(sel[:, :], small_ps[:, SEL:SEL + 2 * CHUNKS], ACT.Exp).then_inc(exps_done, 1)

            def exp_dt(a):
                act.wait_ge(dtexp_ready, a + 1)
                nc.scalar.activation(dt1[:, 1, :], dt1[:, 0, :], ACT.Exp).then_inc(dtexp_done, 1)

            def scan(tt, more):
                act.wait_ge(u_ready, tt)
                act.wait_ge(y_ready, tt)
                for i in range(HALVES):
                    act.wait_ge(ring_ready, RING * tt + 4 + i + 1)
                    nc.scalar.copy(xtok[:, :, P * i:P * (i + 1)], ring_ps[:, i, :, :]).then_inc(ring_used, 1)
                if more:
                    project(tt + 1)
                    silu(tt + 1)
                    exp_dt(tt + 1)
                act.wait_ge(y_ready, tt + 1)
                nc.scalar.copy(y[:, :, :, bass.ds(tt * P, P)], y_ps[:, :, :, :]).then_inc(y_copied, 1)
                if more:
                    decays(tt + 1)

            project(0)
            silu(0)
            exp_dt(0)
            decays(0)
            tiles(act, scan)

        @block.vector
        def _(dve):
            dve.wait_ge(*loaded)
            dve.wait_ge(init_done, 1)
            STEPS, PREP_STEPS, CONV_STEPS = 16, 16, HALVES * (CONV - 1)
            dve.wait_ge(a_ready, 1)
            setup = Chain(dve, link_sem)
            setup.link(nc.vector.tensor_scalar(neg_a[:, :], neg_a[:, :], -1.0, None, ALU.mult))

            def tile_of(a):
                return lambda j: j * TPB + a

            def convolve(a):
                link = Chain(dve, conv_link, CONV_STEPS * a).link
                for i in range(HALVES):
                    dve.wait_ge(ring_used, RING * a + i + 1)
                    link(nc.vector.tensor_scalar(cv[:, i, :, :], xp[:, i, :, 0:P], w["conv_w"][:, i, 0:1],
                                                 w["conv_b"][:, i:i + 1], ALU.mult, ALU.add))
                    for k in range(1, CONV):
                        ins = nc.vector.scalar_tensor_tensor(cv[:, i, :, :], xp[:, i, :, k:k + P],
                                                             w["conv_w"][:, i, k:k + 1], cv[:, i, :, :],
                                                             ALU.mult, ALU.add)
                        if k < CONV - 1:
                            link(ins)
                    ins.then_inc(cv_ready, 1)
                nc.vector.tensor_copy(xp[:, :, :, 0:CONV - 1], xp[:, :, :, P:]).then_inc(halo_done, 1)

            def gates(a):
                for i in range(HALVES):
                    dve.wait_ge(tz_done, HALVES * a + i + 1)
                    nc.vector.scalar_tensor_tensor(gate[:, i, :, bass.ds(a * P, P)], tz[:, i, :, :], 1.0,
                                                   ring_ps[:, i, :, :], ALU.add, ALU.mult).then_inc(ring_used, 1)

            def silu(a):
                for i in range(HALVES):
                    dve.wait_ge(tc_done, HALVES * a + i + 1)
                    ins = nc.vector.scalar_tensor_tensor(tc[:, i, :, :], tc[:, i, :, :], 1.0, cv[:, i, :, :],
                                                         ALU.add, ALU.mult)
                ins.then_inc(xc2_ready, 1)

            def step_inputs(a):
                chain = Chain(dve, prep_link, PREP_STEPS * a)
                link = chain.link
                dve.wait_ge(dbl_ready, a + 1)
                link(nc.vector.tensor_copy(dbl[:, :, :], small_ps[:, DBL:DBL + NDBL * BATCH]
                                           .rearrange("p (b n) -> p b n", b=BATCH)))
                nc.vector.tensor_scalar(dt1[:, 0, :], dbl[:, :, NDBL - 1], DT_LO, DT_HI, ALU.max, ALU.min)\
                    .then_inc(dtexp_ready, 1)
                dve.wait_ge(dtexp_done, a + 1)
                u, s, s2, poly, dt = (dt1[:, n, :] for n in range(1, 6))
                link(nc.vector.tensor_scalar_add(s, u, 2.0))
                link(nc.vector.reciprocal(s, s))
                link(nc.vector.tensor_tensor(s, s, u, ALU.mult))
                link(nc.vector.tensor_tensor(s2, s, s, ALU.mult))
                link(nc.vector.tensor_scalar(poly, s2, 2.0 / 7, 2.0 / 5, ALU.mult, ALU.add))
                link(nc.vector.tensor_tensor(poly, poly, s2, ALU.mult))
                link(nc.vector.tensor_scalar(poly, poly, 2.0 / 3, None, ALU.add))
                link(nc.vector.tensor_tensor(poly, poly, s2, ALU.mult))
                link(nc.vector.tensor_scalar(poly, poly, 2.0, None, ALU.add))
                link(nc.vector.tensor_tensor(dt, poly, s, ALU.mult))
                link(nc.vector.tensor_scalar(dt, dt, DT_MIN, DT_MAX, ALU.max, ALU.min))
                dtw = wide(dt, NS)
                a_all = neg_a[:, :].unsqueeze(1).to_broadcast([P, BATCH, NS])
                link(nc.vector.tensor_tensor(la[:, :, 0:NS], dtw, a_all, ALU.mult))
                nc.vector.tensor_scalar(la[:, :, 0:NS], la[:, :, 0:NS], DECAY_FLOOR, 0.0, ALU.max, ALU.min)\
                    .then_inc(la_ready, 1)
                link(nc.vector.tensor_tensor(bbar[:, :, 0:NS], dtw, dbl[:, :, 0:NS], ALU.mult))
                link(nc.vector.tensor_scalar(bbar[:, :, 0:NS], bbar[:, :, 0:NS], -INPUT_CLIP, INPUT_CLIP,
                                             ALU.max, ALU.min))
                link(nc.vector.tensor_copy(cc[:, :, 0:NS], dbl[:, :, NS:2 * NS]))
                assert chain.n == PREP_STEPS, chain.n

            def scan(tt, more):
                chain = Chain(dve, link_sem, 1 + STEPS * tt)
                link = chain.link
                now = bass.ds(tt * P, P)
                dve.wait_ge(exps_done, tt + 1)
                link(nc.vector.tensor_tensor(coef[:, 0, :], flat(bbar), e_neg[:, :], ALU.mult))
                link(nc.vector.tensor_tensor(coef[:, 1, :], flat(cc), e_pos[:, :], ALU.mult))
                link(nc.vector.tensor_tensor(cum[:, :], flat(bbar), e_rest[:, :], ALU.mult))
                dve.wait_ge(u_ready, tt)
                for k in range(CHUNKS):
                    ins = nc.vector.tensor_scalar(wk[:, k, :], cum[:, :], w["chunk_mask"][:, k:k + 1], None, ALU.mult)
                link(ins)
                dve.wait_ge(ring_used, RING * (tt + 1))
                link(nc.vector.tensor_reduce(umax[:, :], xtok[:, :, :], AX.X, ALU.max, apply_absolute_value=True))
                link(nc.vector.scalar_tensor_tensor(states_of(coef, 3), bbar[:, :, :], -1.0, bbar[:, :, :],
                                                    ALU.mult, ALU.max))
                nc.vector.tensor_tensor(states_of(coef, 3), states_of(coef, 3), wide(umax[:, :], SW), ALU.mult)\
                    .then_inc(coef_ready, 1)
                link(nc.vector.tensor_reduce(cmax[:, bass.ds(tt, 1)], small_ps[:, CUM:CUM + P], AX.X, ALU.max,
                                             apply_absolute_value=True))
                dve.wait_ge(coef_stored, 16 * tt)
                states = states_of(coef, 2)
                link(nc.vector.tensor_copy(out_coef[:, 0, :, :], states[:, :, 0:NS]))
                link(nc.vector.tensor_copy(out_coef[:, 1, :, :], bbar[:, :, 0:NS]))
                nc.vector.tensor_copy(out_coef[:, 2, :, :], cc[:, :, 0:NS]).then_inc(out_coef_ready, 1)

                dve.wait_ge(tr_ready, tt + 1)
                dve.wait_ge(y_ready, tt)
                link(nc.vector.tensor_copy(bt[:, :], tr_ps[:, 0, :]))
                for b in range(BATCH):
                    rows = slice(SW * b, SW * (b + 1))
                    ins = nc.vector.tensor_copy(ct[rows, b, :], tr_ps[rows, 1, :])
                link(ins)
                link(nc.vector.tensor_copy(bound_a[:, now], tr_ps[:, 2, :]))
                nc.vector.tensor_copy(bound_v[:, now], tr_ps[:, 3, :]).then_inc(tr_used, 1)
                if more:
                    convolve(tt + 1)
                dve.wait_ge(g_ready, tt + 1)
                nc.vector.tensor_tensor(gt[:, :, :], g_ps[:, :, :],
                                        w["chunk_causal"][:, :].unsqueeze(1).to_broadcast([P, BATCH, P]),
                                        ALU.mult).then_inc(gt_ready, 1)
                if more:
                    gates(tt + 1)
                    silu(tt + 1)
                dve.wait_ge(u_ready, tt + 1)
                for k in range(CHUNKS):
                    last = h[:, (k - 1) % CHUNKS, :]
                    def to_middle():
                        return nc.vector.tensor_scalar(hm[:, k, :], last, sel[:, CHUNKS + k:CHUNKS + k + 1], None, ALU.mult)

                    if k < CHUNKS - 1:
                        to_middle()
                    link(nc.vector.scalar_tensor_tensor(h[:, k, :], last, sel[:, k:k + 1], u_ps[:, k, :],
                                                        ALU.mult, ALU.add))
                    if k == CHUNKS - 1:
                        to_middle().then_inc(hm_ready, 1)
                if more == 2:
                    norm.statistics(dve, tt + 2, tile_of(tt + 2))
                if more:
                    step_inputs(tt + 1)
                if more == 2:
                    norm.scale(dve, tt + 2, tile_of(tt + 2))
                assert chain.n == STEPS, chain.n

            for a in range(2):
                norm.statistics(dve, a, tile_of(a))
                norm.scale(dve, a, tile_of(a))
            convolve(0)
            gates(0)
            silu(0)
            step_inputs(0)
            tiles(dve, scan)
            end = Chain(dve, link_sem, 1 + STEPS * TPB)
            end.link(nc.vector.tensor_tensor_scan(bound_v[:, :], bound_a[:, :], bound_v[:, :], 0.0, ALU.mult, ALU.add))
            end.link(nc.vector.tensor_reduce(verdict[:, 0:1], bound_v[:, :], AX.X, ALU.max))
            end.link(nc.vector.tensor_reduce(verdict[:, 1:2], cmax[:, :], AX.X, ALU.max))
            end.link(nc.vector.tensor_scalar(verdict[:, 2:3], verdict[:, 1:2], LOG_PROVED, None, ALU.is_le))
            nc.vector.scalar_tensor_tensor(verdict[:, 3:4], verdict[:, 0:1], STATE_PROVED, verdict[:, 2:3],
                                           ALU.is_le, ALU.mult).then_inc(verdict_ready, 1)
            dve.wait_ge(sum_ready, 1)
            nc.vector.tensor_scalar(flag[:, :], small_ps[0:1, 0:1], float(P), None, ALU.not_equal).then_inc(flag_ready, 1)
            dve.wait_ge(flag_ready, 1)

def flat(t):
    return t[:, :, :].rearrange("p b s -> p (b s)")

def states_of(coef, i):
    return coef[:, i, :].rearrange("p (b s) -> p b s", b=BATCH)

def mamba_steps(nc, name, y, xc, flag, coef_dram):
    with ExitStack() as ctx:
        rows = ctx.enter_context(nc.sbuf_tensor(f"{name}_rows", [P, STEP_ROWS, 3, BATCH, NS], F32))
        hs = ctx.enter_context(nc.sbuf_tensor(f"{name}_hs", [P, HALVES, BATCH, NS], F32))
        hx = ctx.enter_context(nc.sbuf_tensor(f"{name}_hx", [P, HALVES, BATCH, NS], F32))
        rows_loaded = nc.alloc_semaphore(f"{name}_rows_loaded")
        rows_used = nc.alloc_semaphore(f"{name}_rows_used")
        step_link = nc.alloc_semaphore(f"{name}_step_link")
        block = ctx.enter_context(nc.Block())
        PIECES = SEQ // STEP_ROWS

        @block.sync
        def _(sp):
            failed = sp.value_load(flag[0:1, 0:1], min_val=0, max_val=1)
            with sp.If(failed > 0):
                with sp.Fori(0, PIECES) as n:
                    sp.wait_ge(rows_used, n)
                    src = coef_dram[bass.ds(n * STEP_ROWS, STEP_ROWS), :]
                    sp.dma_start(rows[:, :, :, :, :].rearrange("p t k b s -> p t (k b s)"),
                                 src.unsqueeze(0).to_broadcast([P, STEP_ROWS, 3 * BATCH * NS])).then_inc(rows_loaded, 16)

        @block.vector
        def _(dve):
            failed = dve.value_load(flag[0:1, 0:1], min_val=0, max_val=1)
            with dve.If(failed > 0):
                OPS = 6
                nc.vector.memset(hs[:, :, :, :], 0.0).then_inc(step_link, 1)
                dve.wait_ge(step_link, 1)
                with dve.Fori(0, PIECES) as n:
                    dve.wait_ge(rows_loaded, 16 * (n + 1))
                    chain = Chain(dve, step_link, 1 + n * (OPS * STEP_ROWS))
                    for r in range(STEP_ROWS):
                        def row(k):
                            return rows[:, r, k, :, :].unsqueeze(1).to_broadcast([P, HALVES, BATCH, NS])
                        t = n * STEP_ROWS + r
                        xt = xc[:, :, :, bass.ds(t, 1)].to_broadcast([P, HALVES, BATCH, NS])
                        chain.link(nc.vector.tensor_tensor(hx[:, :, :, :], row(1), xt, ALU.mult))
                        chain.link(nc.vector.tensor_tensor(hs[:, :, :, :], row(0), hs[:, :, :, :], ALU.mult))
                        chain.link(nc.vector.tensor_tensor(hs[:, :, :, :], hs[:, :, :, :], hx[:, :, :, :], ALU.add))
                        chain.link(nc.vector.tensor_scalar(hs[:, :, :, :], hs[:, :, :, :], -STATE_CLIP, STATE_CLIP,
                                                           ALU.max, ALU.min))
                        chain.link(nc.vector.tensor_tensor(hx[:, :, :, :], hs[:, :, :, :], row(2), ALU.mult))
                        chain.link(nc.vector.tensor_reduce(y[:, :, :, bass.ds(t, 1)], hx[:, :, :, :], AX.X, ALU.add))
                    nc.vector.tensor_copy(hx[:, 0, 0, 0:1], rows[:, 0, 0, 0, 0:1]).then_inc(rows_used, 1)
                    dve.wait_ge(rows_used, n + 1)

def mamba_output(nc, x, const, w, name, y, gate, xc):
    with ExitStack() as ctx:
        o_ps = Banks(const["psum"]).take(2, GT, P)
        mixed = ctx.enter_context(nc.sbuf_tensor(f"{name}_mixed", [P, 2, HALVES, BLK], F32))
        half_y = ctx.enter_context(nc.sbuf_tensor(f"{name}_half_y", [P, HALVES, BLK], F32))
        gated, mixed_ready = (nc.alloc_semaphore(f"{name}_{n}") for n in ("gated", "mixed_ready"))
        o_ready, added = (nc.alloc_semaphore(f"{name}_{n}") for n in ("o_ready", "added"))
        block = ctx.enter_context(nc.Block())

        @block.vector
        def _(dve):
            def mix(q, b, p):
                cols = slice(p * BLK, (p + 1) * BLK)
                dve.wait_ge(mixed_ready, q)
                for i in range(HALVES):
                    ins = nc.vector.scalar_tensor_tensor(half_y[:, i, :], y[:, i, bass.ds(b, 1), cols], 0.5,
                                                         gate[:, i, bass.ds(b, 1), cols], ALU.mult, ALU.mult)
                ins.then_inc(gated, 1)
                dve.wait_ge(gated, q + 1)
                dve.wait_ge(o_ready, 2 * b)
                for i in range(HALVES):
                    ins = nc.vector.scalar_tensor_tensor(mixed[:, p, i, :], xc[:, i, bass.ds(b, 1), cols],
                                                         w["d"][:, i:i + 1], half_y[:, i, :], ALU.mult, ALU.add)
                ins.then_inc(mixed_ready, 1)

            with dve.Fori(0, BATCH) as b:
                for p in range(2):
                    mix(2 * b + p, b, p)
                for p in range(2):
                    q = 2 * b + p
                    dve.wait_ge(o_ready, q + 1)
                    xq = x[:, bass.ds(q * GT, GT), :]
                    nc.vector.tensor_tensor(xq, o_ps[:, p, :, :], xq, ALU.add).then_inc(added, 1)

        @block.tensor
        def _(pe):
            with pe.Fori(0, BATCH) as b:
                for p in range(2):
                    q = 2 * b + p
                    pe.wait_ge(mixed_ready, q + 1)
                    pe.wait_ge(added, 2 * b)
                    for j in range(GT):
                        for i in range(HALVES):
                            ins = pe.matmul(o_ps[:, p, j, :], mixed[:, p, i, j * P:(j + 1) * P], w["out"][:, i, :],
                                            start=(i == 0), stop=(i == HALVES - 1))
                    ins.then_inc(o_ready, 1)

E = 15
NE = E + 1
TOPK = 3
Y_BANKS = 4

def ffn_stage(nc, x, const, w, loaded, name, out=None, fetch=None):
    with ExitStack() as ctx:
        def sb(n, shape, dt=F32):
            return ctx.enter_context(nc.sbuf_tensor(f"{name}_{n}", shape, dt))

        def sem(n):
            return nc.alloc_semaphore(f"{name}_{n}")

        banks = Banks(const["psum"])
        h_ps = banks.take(2, BLK)
        y_ps = banks.take(Y_BANKS, GT, P)
        norm = Prenorm(nc, ctx, const, x, name + "_n", xt_ps=banks.take(GT, P))
        logit_ps = banks.take(GT, P)
        cwt_ps = logit_ps

        xt_parts = sb("xt_parts", [P, 2, 2, BLK], F32R)
        w1_parts = sb("w1_parts", [P, 2, NE, P], F32R)
        h = sb("h", [P, 2, BLK])
        cw = sb("cw", [P, 2, GT, NE])
        cwt = sb("cwt", [NE, 2, BLK])
        top = sb("top", [P, GT])
        prob = sb("prob", [P, GT, E])
        left = sb("left", [P, GT, E])
        eq = sb("eq", [P, GT, E])

        logit_ready, shifted, exp_done = sem("logit_ready"), sem("shifted"), sem("exp_done")
        cw_ready, cwt_ps_ready, cwt_ready = sem("cw_ready"), sem("cwt_ps_ready"), sem("cwt_ready")
        h_ready, relu_done, y_ready, acc_done = sem("h_ready"), sem("relu_done"), sem("y_ready"), sem("acc_done")
        dve_link = sem("dve_link")
        cw_one, w1_high, w1_ready = sem("cw_one"), sem("w1_high"), sem("w1_ready")
        xt_high, xt_split = sem("xt_high"), sem("xt_split")

        block = ctx.enter_context(nc.Block())

        def blocks(eng, body):
            with eng.Fori(0, BLOCKS // 2 - 1) as i:
                body(2 * i, 0, True)
                body(2 * i + 1, 1, True)
            body(BLOCKS - 2, 0, True)
            body(BLOCKS - 1, 1, False)

        if fetch is not None:
            @block.sync
            def _(sp):
                for dst, src in fetch[0]:
                    sp.dma_start(dst, src).then_inc(fetch[1], 16)

        if out is not None:
            stored = sem("stored")

            @block.sync
            def _(sp):
                with sp.Fori(0, BLOCKS) as g:
                    sp.wait_ge(acc_done, NE * (g + 1) + Y_BANKS - 1)
                    rows = bass.ds(g * GT, GT)
                    sp.dma_start(out[:, rows, :], x[:, rows, :]).then_inc(stored, 16)
                sp.wait_ge(stored, 16 * BLOCKS)

        @block.gpsimd
        def _(pool):
            def split_x(q, p):
                pool.wait_ge(xt_high, q + 1)
                nc.gpsimd.tensor_tensor(xt_parts[:, p, 1, :], norm.xt[:, p, :], xt_parts[:, p, 0, :], ALU.subtract)\
                    .then_inc(xt_split, 1)

            def body(g, p, more):
                if more:
                    norm.invert(pool, g + 1)
                    split_x(g + 1, 1 - p)

            norm.invert(pool, 0)
            pool.wait_ge(w1_high, 1)
            nc.gpsimd.tensor_tensor(w1_parts[:, 1, :, :], w["w1"][:, :, :], w1_parts[:, 0, :, :], ALU.subtract)\
                .then_inc(w1_ready, 1)
            split_x(0, 0)
            blocks(pool, body)

        @block.tensor
        def _(pe):
            sem_loaded, count = loaded
            pe.wait_ge(sem_loaded, count)

            def route(q, p):
                pe.wait_ge(norm.xt_ready, q + 1)
                pe.wait_ge(shifted, q)
                pe.wait_ge(cwt_ready, q)
                for j in range(GT):
                    pe.matmul(logit_ps[:, j, 0:E], norm.xt[:, p, j * P:(j + 1) * P], w["router"][:, :],
                              start=True, stop=False)
                    ins = pe.matmul(logit_ps[:, j, 0:E], const["ones"][0:1, 0:P], w["router_b"][:, :],
                                    start=False, stop=True)
                ins.then_inc(logit_ready, 1)

            def transpose_cw(q, p):
                pe.wait_ge(cw_ready, q + 1)
                pe.wait_ge(cwt_ready, q)
                for j in range(GT):
                    ins = pe.transpose(cwt_ps[0:NE, j, :], cw[:, p, j, :], const["ident"][:, :])
                ins.then_inc(cwt_ps_ready, 1)

            def up(g, p, e):
                pe.wait_ge(relu_done, NE * g + e)
                for n, (i, j) in enumerate(((0, 0), (0, 1), (1, 0))):
                    ins = pe.matmul(h_ps[:, e % 2, :], w1_parts[:, i, e, :], xt_parts[:, p, j, :],
                                    start=(n == 0), stop=(n == 2))
                ins.then_inc(h_ready, 1)

            def down(g, p, e):
                pe.wait_ge(relu_done, NE * g + e + 2)
                pe.wait_ge(acc_done, NE * g + e)
                if e == E:
                    pe.wait_ge(cwt_ready, g + 1)
                for j in range(GT):
                    if e == E:
                        pe.matmul(y_ps[:, e % Y_BANKS, j, :], cwt[:, p, j * P:(j + 1) * P], w["b2"][:, :],
                                  start=True, stop=False)
                    ins = pe.matmul(y_ps[:, e % Y_BANKS, j, :], h[:, e % 2, j * P:(j + 1) * P], w["w2"][:, e, :],
                                    start=(e != E), stop=True)
                ins.then_inc(y_ready, 1)

            def body(g, p, more):
                for e in range(NE):
                    if e == 0:
                        pe.wait_ge(xt_split, g + 1)
                    up(g, p, e)
                    if e >= 1:
                        down(g, p, e - 1)
                    if more and e == 5:
                        norm.transpose(pe, g + 1)
                    if more and e == 6:
                        route(g + 1, 1 - p)
                    if e == 3:
                        transpose_cw(g, p)
                down(g, p, E)

            norm.transpose(pe, 0)
            route(0, 0)
            pe.wait_ge(w1_ready, 1)
            blocks(pe, body)

        @block.scalar
        def _(act):
            act.wait_ge(loaded[0], loaded[1])

            def copy_x(q, p):
                norm.copy(act, q, p)
                nc.scalar.copy(xt_parts[:, p, 0, :], norm.xt_ps[:, :, :]).then_inc(xt_high, 1)

            def exp(q):
                act.wait_ge(shifted, q + 1)
                nc.scalar.activation(prob[:, :, :], prob[:, :, :], ACT.Exp).then_inc(exp_done, 1)

            def relu(g, e):
                act.wait_ge(h_ready, NE * g + e + 1)
                act.wait_ge(y_ready, NE * g + e)
                nc.scalar.activation(h[:, e % 2, :], h_ps[:, e % 2, :], ACT.Relu,
                                     bias=w["b1"][:, e:e + 1]).then_inc(relu_done, 1)

            def copy_cwt(q, p):
                act.wait_ge(cwt_ps_ready, q + 1)
                nc.scalar.copy(cwt[:, p, :], cwt_ps[0:NE, :, :]).then_inc(cwt_ready, 1)

            def body(g, p, more):
                for e in range(NE):
                    relu(g, e)
                    if more and e == 5:
                        copy_x(g + 1, 1 - p)
                    if more and e == 8:
                        exp(g + 1)
                    if e == 3:
                        copy_cwt(g, p)

            nc.scalar.copy(w1_parts[:, 0, :, :], w["w1"][:, :, :]).then_inc(w1_high, 1)
            copy_x(0, 0)
            exp(0)
            blocks(act, body)

        @block.vector
        def _(dve):
            STEPS = 1 + 3 + 6 * TOPK

            def shift(q):
                chain = Chain(dve, dve_link, STEPS * q)
                dve.wait_ge(logit_ready, q + 1)
                chain.link(nc.vector.tensor_reduce(top[:, :], logit_ps[:, :, 0:E], AX.X, ALU.max))
                nc.vector.tensor_tensor(prob[:, :, :], logit_ps[:, :, 0:E], wide(top[:, :], E),
                                        ALU.subtract).then_inc(shifted, 1)

            def probabilities(q):
                chain = Chain(dve, dve_link, STEPS * q + 1)
                dve.wait_ge(exp_done, q + 1)
                chain.link(nc.vector.tensor_reduce(top[:, :], prob[:, :, :], AX.X, ALU.add))
                chain.link(nc.vector.reciprocal(top[:, :], top[:, :]))
                chain.link(nc.vector.tensor_tensor(prob[:, :, :], prob[:, :, :], wide(top[:, :], E), ALU.mult))

            order = const["order"][:, :, :]

            def find_largest(q, k):
                src = prob if k == 0 else left
                chain = Chain(dve, dve_link, STEPS * q + 4 + 6 * k)
                chain.link(nc.vector.tensor_reduce(top[:, :], src[:, :, :], AX.X, ALU.max))
                chain.link(nc.vector.tensor_tensor(eq[:, :, :], src[:, :, :], wide(top[:, :], E), ALU.is_equal))
                chain.link(nc.vector.tensor_tensor(eq[:, :, :], eq[:, :, :], order, ALU.mult))

            def take_largest(q, k):
                src = prob if k == 0 else left
                chain = Chain(dve, dve_link, STEPS * q + 4 + 6 * k + 3)
                chain.link(nc.vector.tensor_reduce(top[:, :], eq[:, :, :], AX.X, ALU.max))
                chain.link(nc.vector.tensor_tensor(eq[:, :, :], order, wide(top[:, :], E), ALU.is_equal))
                chain.link(nc.vector.scalar_tensor_tensor(left[:, :, :], eq[:, :, :], -2.0, src[:, :, :],
                                                          ALU.mult, ALU.add))

            def combine_weights(q, p):
                nc.vector.scalar_tensor_tensor(cw[:, p, :, 0:E], left[:, :, :], 0.0, prob[:, :, :],
                                               ALU.is_lt, ALU.mult).then_inc(cw_ready, 1)

            def add_expert(g, p, e):
                dve.wait_ge(y_ready, NE * g + e + 2)
                dve.wait_ge(acc_done, NE * g + e + Y_BANKS - 1)
                for j in range(GT):
                    xg = x[:, g * GT + j, :]
                    ins = nc.vector.scalar_tensor_tensor(xg, y_ps[:, e % Y_BANKS, j, :], cw[:, p, j, e:e + 1], xg,
                                                         ALU.mult, ALU.add)
                ins.then_inc(acc_done, 1)

            def body(g, p, more):
                dve.wait_ge(cw_ready, g + 1)
                for e in range(NE):
                    add_expert(g, p, e)
                    if more and e == 0:
                        norm.moments(dve, g + 1)
                    if more and e == 1:
                        norm.aggregate(dve, g + 1)
                    if more and e == 2:
                        norm.scale(dve, g + 1)
                    if more and e == 6:
                        shift(g + 1)
                    if more and e == 8:
                        probabilities(g + 1)
                    if more and 9 <= e < 9 + 2 * TOPK:
                        k = (e - 9) // 2
                        (find_largest if e % 2 == 1 else take_largest)(g + 1, k)
                    if more and e == 8 + 2 * TOPK:
                        combine_weights(g + 1, 1 - p)

            nc.vector.memset(cw[:, :, :, E:NE], 1.0).then_inc(cw_one, 1)
            dve.wait_ge(cw_one, 1)
            for i, (count, start) in enumerate(((relu_done, 1), (y_ready, 1), (acc_done, Y_BANKS - 1))):
                nc.vector.memset(norm.pause[:, i + 1:i + 2], 0.0).then_inc(count, start)
            norm.statistics(dve, 0)
            norm.scale(dve, 0)
            shift(0)
            probabilities(0)
            for k in range(TOPK):
                find_largest(0, k)
                take_largest(0, k)
            combine_weights(0, 0)
            blocks(dve, body)

LIN_EPS = 1e-15
BPB = BLOCKS // BATCH

def linear_attention_stage(nc, x, const, w, loaded, name):
    with ExitStack() as ctx:
        def sb(n, shape, dt=F32):
            return ctx.enter_context(nc.sbuf_tensor(f"{name}_{n}", shape, dt))

        def sem(n):
            return nc.alloc_semaphore(f"{name}_{n}")

        banks = Banks(const["psum"])
        norm = Prenorm(nc, ctx, const, x, name + "_n", xt_ps=banks.take(GT, P))
        q_ps = banks.take(BLK)
        kv_ps = banks.take(GT, 2 * P)
        vk_ps = banks.take(BLK)
        den_ps = banks.take(4, GT, P // 4)
        num_ps = banks.take(GT, P)
        y_ps = banks.take(GT, P)
        qt = sb("qt", [P, BPB, BLK])
        kv = sb("kv", [P, GT, 2 * P + 1])
        num_w = sb("num_w", [P, P])
        den_w = sb("den_w", [P, P // 4])
        rden = sb("rden", [P, 2, GT, P // 4])
        ratio = sb("ratio", [P, 2, GT, P])
        rt = sb("rt", [P, 2, BLK])

        one_set, q_ready, qt_ready = sem("one_set"), sem("q_ready"), sem("qt_ready")
        kv_ps_ready, kv_ready, vk_added = sem("kv_ps_ready"), sem("kv_ready"), sem("vk_added")
        heads_ready = sem("heads_ready")
        ratio_ps_ready, ratio_link, ratio_ready = sem("ratio_ps_ready"), sem("ratio_link"), sem("ratio_ready")
        rt_ps_ready, rt_ready = sem("rt_ps_ready"), sem("rt_ready")
        y_ready, x_done = sem("y_ready"), sem("x_done")

        block = ctx.enter_context(nc.Block())

        def batches(eng, body):
            with eng.Fori(0, BATCH - 1) as b:
                body(b, True)
            body(BATCH - 1, False)

        @block.gpsimd
        def _(pool):
            def invert(b):
                for p in range(BPB):
                    norm.invert(pool, BPB * b + p)

            invert(0)
            batches(pool, lambda b, more: invert(b + 1) if more else None)

        @block.tensor
        def _(pe):
            pe.wait_ge(*loaded)

            def first(b, p):
                q = BPB * b + p
                norm.transpose(pe, q)
                pe.wait_ge(norm.xt_ready, q + 1)
                pe.wait_ge(qt_ready, q)
                pe.matmul(q_ps[:, :], w["q"][:, :], norm.xt[:, p, :], start=True, stop=True).then_inc(q_ready, 1)
                pe.wait_ge(kv_ready, 2 * q)
                for j in range(GT):
                    ins = pe.matmul(kv_ps[:, j, :], norm.xt[:, p, j * P:(j + 1) * P], w["kv"][:, :],
                                    start=True, stop=True)
                ins.then_inc(kv_ps_ready, 1)

            def state(b, p):
                pe.wait_ge(kv_ready, 2 * (BPB * b + p + 1))
                if p == 0:
                    pe.wait_ge(heads_ready, b)
                for j in range(GT):
                    ins = pe.matmul(vk_ps[:, 0:P + 1], kv[:, j, 0:P], kv[:, j, P:2 * P + 1],
                                    start=(p == 0 and j == 0), stop=(p == BPB - 1 and j == GT - 1))
                ins.then_inc(vk_added, 1)

            def second(b, p):
                q = BPB * b + p
                pe.wait_ge(heads_ready, b + 1)
                pe.wait_ge(qt_ready, q + 1)
                pe.wait_ge(ratio_ready, q)
                for j in range(GT):
                    tokens = qt[:, p, j * P:(j + 1) * P]
                    pe.matmul(num_ps[:, j, :], tokens, num_w[:, :], start=True, stop=True)
                    ins = pe.matmul(den_ps[:, 0, j, :], tokens, den_w[:, :], start=True, stop=True)
                ins.then_inc(ratio_ps_ready, 1)

            def transpose_ratio(b, p):
                q = BPB * b + p
                pe.wait_ge(ratio_ready, q + 1)
                pe.wait_ge(x_done, q)
                for j in range(GT):
                    ins = pe.transpose(y_ps[:, j, :], ratio[:, p, j, :], const["ident"][:, :])
                ins.then_inc(rt_ps_ready, 1)

            def project(b, p):
                q = BPB * b + p
                pe.wait_ge(rt_ready, q + 1)
                for j in range(GT):
                    pe.matmul(y_ps[:, j, :], rt[:, p, j * P:(j + 1) * P], w["proj"][:, :], start=True, stop=False)
                    ins = pe.matmul(y_ps[:, j, :], const["ones"][0:1, 0:P], w["proj_b"][:, :],
                                    start=False, stop=True)
                ins.then_inc(y_ready, 1)

            def body(b, more):
                second(b, 0)
                second(b, 1)
                if more:
                    first(b + 1, 0)
                transpose_ratio(b, 0)
                if more:
                    first(b + 1, 1)
                    state(b + 1, 0)
                project(b, 0)
                transpose_ratio(b, 1)
                if more:
                    state(b + 1, 1)
                project(b, 1)

            first(0, 0)
            state(0, 0)
            first(0, 1)
            state(0, 1)
            batches(pe, body)

        @block.scalar
        def _(act):
            act.wait_ge(one_set, 1)

            def first(b, p, start=False):
                q = BPB * b + p
                if not start:
                    norm.copy(act, q, p, (kv_ps_ready, BPB * b))
                    act.wait_ge(ratio_ps_ready, BPB * b)
                else:
                    norm.copy(act, q, p)
                act.wait_ge(q_ready, q + 1)
                nc.scalar.activation(qt[:, p, :], q_ps[:, :], ACT.Relu).then_inc(qt_ready, 1)
                act.wait_ge(kv_ps_ready, q + 1)
                act.wait_ge(vk_added, q)
                for half in range(2):
                    tiles = slice(half * GT // 2, (half + 1) * GT // 2)
                    nc.scalar.activation(kv[:, tiles, 0:2 * P], kv_ps[:, tiles, :], ACT.Relu).then_inc(kv_ready, 1)

            def copy_ratio(b, p):
                act.wait_ge(rt_ps_ready, BPB * b + p + 1)
                act.wait_ge(y_ready, BPB * b)
                nc.scalar.copy(rt[:, p, :], y_ps[:, :, :]).then_inc(rt_ready, 1)

            def body(b, more):
                for p in range(BPB):
                    if more:
                        first(b + 1, p)
                    copy_ratio(b, p)

            for p in range(BPB):
                first(0, p, start=True)
            batches(act, body)

        @block.vector
        def _(dve):
            nc.vector.memset(kv[:, :, 2 * P:2 * P + 1], 1.0).then_inc(one_set, 1)

            def normalise(b, p):
                norm.statistics(dve, BPB * b + p)
                norm.scale(dve, BPB * b + p)

            def heads(b):
                dve.wait_ge(vk_added, BPB * (b + 1))
                dve.wait_ge(ratio_ps_ready, BPB * b)
                nc.vector.tensor_tensor(num_w[:, :], vk_ps[:, 0:P], const["head4"][:, :], ALU.mult)
                nc.vector.tensor_scalar(den_w[:, :], const["head4"][:, 0:P:4], vk_ps[:, P:P + 1], None, ALU.mult)\
                    .then_inc(heads_ready, 1)

            def divide(b, p):
                q = BPB * b + p
                dve.wait_ge(ratio_ps_ready, q + 1)
                nc.vector.tensor_scalar_add(rden[:, p, :, :], den_ps[:, 0, :, :], LIN_EPS).then_inc(ratio_link, 1)
                dve.wait_ge(ratio_link, 2 * q + 1)
                nc.vector.reciprocal(rden[:, p, :, :], rden[:, p, :, :]).then_inc(ratio_link, 1)
                dve.wait_ge(ratio_link, 2 * q + 2)
                dve.wait_ge(rt_ps_ready, BPB * b)
                per_head = [P, GT, P // 4, 4]
                nc.vector.tensor_tensor(ratio[:, p, :, :].rearrange("p t (h c) -> p t h c", c=4),
                                        num_ps[:, :, :].rearrange("p t (h c) -> p t h c", c=4),
                                        rden[:, p, :, :].unsqueeze(3).to_broadcast(per_head), ALU.mult)\
                    .then_inc(ratio_ready, 1)

            def add(b, p):
                q = BPB * b + p
                dve.wait_ge(y_ready, q + 1)
                xq = x[:, bass.ds(q * GT, GT), :]
                nc.vector.tensor_tensor(xq, y_ps[:, :, :], xq, ALU.add).then_inc(x_done, 1)

            def body(b, more):
                for p in range(BPB):
                    divide(b, p)
                    if more:
                        normalise(b + 1, p)
                add(b, 0)
                if more:
                    heads(b + 1)
                add(b, 1)

            for p in range(BPB):
                normalise(0, p)
            heads(0)
            batches(dve, body)

HD4 = 4
RH = P // HD4
DECAYS = 2
BETA_MIN, BETA_MAX = 0.85, 0.9995
DEN_EPS = 1e-6
STATES = HD4 + 1
POOL_STATES = ((1, 2), (1,))
W_V, W_BETA = 4, 8
RING = 8

def retention_stage(nc, x, const, w, loaded, name, fetch=None):
    with ExitStack() as ctx:
        def sb(n, shape, dt=F32):
            return ctx.enter_context(nc.sbuf_tensor(f"{name}_{n}", shape, dt))

        def sem(n):
            return nc.alloc_semaphore(f"{name}_{n}")

        banks = Banks(const["psum"])
        norm = Prenorm(nc, ctx, const, x, name + "_n", xt_ps=banks.take(GT, P))
        ring_ps = banks.take(2, BLK)
        beta_ps = banks.take(BLK)
        num_ps = banks.take(DECAYS, GT, HD4, RH)
        den_ps = banks.take(4, GT, RH)
        y_ps = banks.take(GT, P)
        mix_ps = beta_ps[:, 0:GT * RH].rearrange("p (t h) -> p t h", t=GT)
        mix_w = sb("mix_w", [P, RH])
        mix_b = sb("mix_b", [1, RH])
        half_b = sb("half_b", [P, DECAYS])
        rope_a = sb("rope_a", [P, 2, BLK])
        rope_b = sb("rope_b", [P, 2, BLK])
        rot = sb("rot", [P, 2, BLK])
        ex = sb("ex", [P, 2, BLK])
        th = sb("th", [P, DECAYS, BLK])
        mix_th = sb("mix_th", [P, GT, RH])
        phi = sb("phi", [P, 2, 2, BLK])
        kv = sb("kv", [P, 2, HD4, BLK])
        beta = sb("beta", [P, 2, DECAYS, BLK])
        mix = sb("mix", [P, 2, DECAYS, GT, RH])
        state = sb("state", [P, DECAYS, STATES, BLK])
        carry = sb("carry", [P, DECAYS, STATES])
        rd = sb("rd", [P, DECAYS, GT, RH])
        ym = sb("ym", [P, DECAYS, GT, HD4, RH])
        ytok = sb("ytok", [P, GT, P])
        yt = sb("yt", [P, BLK])
        res = sb("res", [P, TILES, P])
        z = sb("z", [P, GT, P])
        zn = sb("zn", [P, GT, P])
        z_stats = sb("z_stats", [P, GT, 6])
        z_mv = sb("z_mv", [P, GT, 2])
        z_rstd = sb("z_rstd", [P, GT])

        weights_ready, res_ready = sem("weights_ready"), sem("res_ready")
        ring_ready, ring_used = sem("ring_ready"), sem("ring_used")
        beta_ps_ready, tanh_done, beta_ready, clipped = sem("beta_ps_ready"), sem("tanh_done"), sem("beta_ready"), sem("clipped")
        mix_ps_ready, mix_tanh_done, mix_ready = sem("mix_ps_ready"), sem("mix_tanh_done"), sem("mix_ready")
        rot_ready, neg_done, exp_done, phi_ready = sem("rot_ready"), sem("neg_done"), sem("exp_done"), sem("phi_ready")
        scanned, carried, prod_dve, prod_pool = sem("scanned"), sem("carried"), sem("prod_dve"), sem("prod_pool")
        nd_ready, den_used, div_link = sem("nd_ready"), sem("den_used"), sem("div_link")
        ytok_ready, yt_ps_ready, yt_ready, y_ready = sem("ytok_ready"), sem("yt_ps_ready"), sem("yt_ready"), sem("y_ready")
        z_ready, z_link, z_stats_ready, z_rstd_ready = sem("z_ready"), sem("z_link"), sem("z_stats_ready"), sem("z_rstd_ready")
        zn_link, setup_link, x_done = sem("zn_link"), sem("setup_link"), sem("x_done")

        block = ctx.enter_context(nc.Block())

        def exists(q):
            return not isinstance(q, int) or 0 <= q < BLOCKS

        def run(eng, prologue, iteration, epilogue):
            prologue()
            iteration(0, 0)
            iteration(1, 1)
            with eng.Fori(1, BATCH - 1) as b:
                iteration(BPB * b, 0)
                iteration(BPB * b + 1, 1)
            iteration(BLOCKS - 2, 0)
            iteration(BLOCKS - 1, 1)
            epilogue()

        if fetch is not None:
            @block.sync
            def _(sp):
                for dst, src in fetch[0]:
                    sp.dma_start(dst, src).then_inc(fetch[1], 16)

        @block.gpsimd
        def _(pool):
            pool.wait_ge(*loaded)

            def rotate(a):
                for i in range(2):
                    pool.wait_ge(ring_used, RING * a + 2 * i + 2)
                    pool.wait_ge(phi_ready, a)
                    nc.gpsimd.tensor_tensor(rot[:, i, :], rope_a[:, i, :], rope_b[:, i, :], ALU.add)\
                        .then_inc(rot_ready, 1)

            def products(q, p, m):
                pool.wait_ge(carried, DECAYS * q + m + 1)
                for s in POOL_STATES[m]:
                    st = state[:, m, s, :]
                    ins = nc.gpsimd.tensor_tensor(st, st, phi[:, p, 0, :], ALU.mult)
                ins.then_inc(prod_pool, 1)

            def z_power(q):
                pool.wait_ge(z_stats_ready, q + 1)
                nc.gpsimd.tensor_tensor(z_rstd[:, :], z_mv[:, :, 1], const["minus_half"][:, 0:GT],
                                        ALU.pow).then_inc(z_rstd_ready, 1)

            def keep(a):
                tiles = bass.ds(a * GT, GT)
                pool.wait_ge(norm.xn_ready, a + 1)
                row = [P, GT, P]
                nc.gpsimd.tensor_tensor(res[:, tiles, :], norm.xn[:, :, :], w["out_bias"][:, :].unsqueeze(1).to_broadcast(row),
                                        ALU.add)
                nc.gpsimd.tensor_tensor(x[:, tiles, :], x[:, tiles, :], w["ln_b"][:, :].unsqueeze(1).to_broadcast(row),
                                        ALU.add).then_inc(res_ready, 1)

            def prologue():
                norm.invert(pool, 0)
                rotate(0)
                keep(0)
                norm.invert(pool, 1)
                keep(1)

            def iteration(q, p):
                if exists(q + 2):
                    norm.invert(pool, q + 2)
                if exists(q + 1):
                    rotate(q + 1)
                products(q, p, 0)
                if exists(q - 1):
                    z_power(q - 1)
                products(q, p, 1)
                if exists(q + 2):
                    keep(q + 2)

            run(pool, prologue, iteration, lambda: z_power(BLOCKS - 1))

        @block.tensor
        def _(pe):
            pe.wait_ge(*loaded)
            pe.wait_ge(weights_ready, 3)

            def ring(a, p, which):
                for i in which:
                    pe.wait_ge(ring_used, RING * a + max(i - 1, 0))
                    pe.matmul(ring_ps[:, i % 2, :], w["w"][:, i, :], norm.xt[:, p, :], start=True, stop=True)\
                        .then_inc(ring_ready, 1)

            def decay(a, p, i):
                pe.wait_ge(mix_tanh_done, a)
                pe.wait_ge(tanh_done, DECAYS * a + i)
                pe.matmul(beta_ps[:, :], w["w"][:, W_BETA + i, :], norm.xt[:, p, :], start=True, stop=True)\
                    .then_inc(beta_ps_ready, 1)

            def mix_logits(a, p):
                pe.wait_ge(tanh_done, DECAYS * (a + 1))
                for j in range(GT):
                    pe.matmul(mix_ps[:, j, :], norm.xt[:, p, j * P:(j + 1) * P], mix_w[:, :], start=True, stop=False)
                    ins = pe.matmul(mix_ps[:, j, :], const["ones"][0:1, 0:P], mix_b[:, :], start=False, stop=True)
                ins.then_inc(mix_ps_ready, 1)

            def sums(q, m):
                pe.wait_ge(prod_dve, DECAYS * q + m + 1)
                pe.wait_ge(prod_pool, DECAYS * q + m + 1)
                pe.wait_ge(ytok_ready, q)
                for j in range(GT):
                    cols = slice(j * P, (j + 1) * P)
                    pe.matmul(den_ps[:, m, j, :], state[:, m, 0, cols], w["head_sel"][:, :], start=True, stop=True)
                    for c in range(HD4):
                        ins = pe.matmul(num_ps[:, m, j, c, :], state[:, m, 1 + c, cols], w["head_sel"][:, :],
                                        start=True, stop=True)
                ins.then_inc(nd_ready, 1)

            def transpose_y(q):
                pe.wait_ge(ytok_ready, q + 1)
                pe.wait_ge(z_ready, q)
                for j in range(GT):
                    ins = pe.transpose(y_ps[:, j, :], ytok[:, j, :], const["ident"][:, :])
                ins.then_inc(yt_ps_ready, 1)

            def project(q):
                pe.wait_ge(yt_ready, q + 1)
                for j in range(GT):
                    ins = pe.matmul(y_ps[:, j, :], yt[:, j * P:(j + 1) * P], w["out"][:, :], start=True, stop=True)
                ins.then_inc(y_ready, 1)

            def prologue():
                norm.transpose(pe, 0)
                pe.wait_ge(norm.xt_ready, 1)
                ring(0, 0, range(4))
                decay(0, 0, 0)
                decay(0, 0, 1)
                mix_logits(0, 0)
                ring(0, 0, range(4, RING))
                norm.transpose(pe, 1)

            def iteration(q, p):
                more = exists(q + 1)
                if more:
                    pe.wait_ge(norm.xt_ready, q + 2)
                    ring(q + 1, 1 - p, (0, 1))
                    decay(q + 1, 1 - p, 0)
                if exists(q - 1):
                    transpose_y(q - 1)
                if more:
                    ring(q + 1, 1 - p, (2, 3))
                    decay(q + 1, 1 - p, 1)
                if exists(q - 1):
                    project(q - 1)
                if more:
                    mix_logits(q + 1, 1 - p)
                sums(q, 0)
                if exists(q + 2):
                    norm.transpose(pe, q + 2)
                if more:
                    ring(q + 1, 1 - p, range(4, RING))
                sums(q, 1)

            def epilogue():
                transpose_y(BLOCKS - 1)
                project(BLOCKS - 1)

            run(pe, prologue, iteration, epilogue)

        @block.scalar
        def _(act):
            act.wait_ge(*loaded)
            act.wait_ge(weights_ready, 3)

            def tanh(a, i):
                act.wait_ge(beta_ps_ready, DECAYS * a + i + 1)
                act.wait_ge(beta_ready, a)
                nc.scalar.activation(th[:, i, :], beta_ps[:, :], ACT.Tanh, bias=half_b[:, i:i + 1],
                                     scale=0.5).then_inc(tanh_done, 1)

            def sigmoids(a, p, first=False):
                act.wait_ge(mix_ps_ready, a + 1)
                nc.scalar.activation(mix_th[:, :, :], mix_ps[:, :, :], ACT.Tanh, scale=0.5).then_inc(mix_tanh_done, 1)
                act.wait_ge(tanh_done, DECAYS * (a + 1))
                if not first:
                    act.wait_ge(carried, DECAYS * (a - 1))
                nc.scalar.activation(beta[:, p, :, :], th[:, :, :], ACT.Identity, bias=w["half"][:, :], scale=0.5)\
                    .then_inc(beta_ready, 1)
                act.wait_ge(mix_tanh_done, a + 1)
                if not first:
                    act.wait_ge(ytok_ready, a - 1)
                nc.scalar.activation(mix[:, p, 0, :, :], mix_th[:, :, :], ACT.Identity, bias=w["half"][:, :], scale=0.5)
                nc.scalar.activation(mix[:, p, 1, :, :], mix_th[:, :, :], ACT.Identity, bias=w["half"][:, :], scale=-0.5)\
                    .then_inc(mix_ready, 1)

            def exponentials(a):
                act.wait_ge(phi_ready, a)
                for i in range(2):
                    act.wait_ge(rot_ready, 2 * a + i + 1)
                    nc.scalar.activation(ex[:, i, :], rot[:, i, :], ACT.Relu, scale=-1.0).then_inc(neg_done, 1)
                act.wait_ge(neg_done, 2 * a + 2)
                nc.scalar.activation(ex[:, :, :], ex[:, :, :], ACT.Exp, scale=-1.0).then_inc(exp_done, 1)

            def copy_yt(q):
                act.wait_ge(yt_ps_ready, q + 1)
                act.wait_ge(y_ready, q)
                nc.scalar.copy(yt[:, :], y_ps[:, :, :]).then_inc(yt_ready, 1)

            def prologue():
                norm.copy(act, 0, 0)
                tanh(0, 0)
                tanh(0, 1)
                sigmoids(0, 0, first=True)
                exponentials(0)
                norm.copy(act, 1, 1)

            def iteration(q, p):
                if exists(q + 1):
                    tanh(q + 1, 0)
                if exists(q - 1):
                    copy_yt(q - 1)
                if exists(q + 1):
                    tanh(q + 1, 1)
                    sigmoids(q + 1, 1 - p)
                    exponentials(q + 1)
                if exists(q + 2):
                    norm.copy(act, q + 2, p, (ring_ready, RING * (q + 1)))

            run(act, prologue, iteration, lambda: copy_yt(BLOCKS - 1))

        @block.vector
        def _(dve):
            dve.wait_ge(*loaded)
            nc.vector.tensor_tensor(mix_w[:, :], w["mix"][:, 0, :], w["mix"][:, 1, :], ALU.subtract).then_inc(weights_ready, 1)
            nc.vector.tensor_tensor(mix_b[:, :], w["mix_b"][:, 0, :], w["mix_b"][:, 1, :], ALU.subtract)\
                .then_inc(weights_ready, 1)
            nc.vector.tensor_scalar(half_b[:, :], w["b"][:, :], 0.5, None, ALU.mult).then_inc(weights_ready, 1)

            def rope(a, p):
                now = slice(p * BLK, (p + 1) * BLK)
                for i in range(4):
                    dve.wait_ge(ring_ready, RING * a + i + 1)
                    dve.wait_ge(rot_ready, 2 * a)
                    dst, table = (rope_a, w["cos"]) if i % 2 == 0 else (rope_b, w["sin"])
                    nc.vector.tensor_tensor(dst[:, i // 2, :], ring_ps[:, i % 2, :], table[:, now], ALU.mult)\
                        .then_inc(ring_used, 1)

            def features(a, p, first=False):
                dve.wait_ge(beta_ready, a + 1)
                nc.vector.tensor_scalar(beta[:, p, :, :], beta[:, p, :, :], BETA_MIN, BETA_MAX, ALU.max, ALU.min)\
                    .then_inc(clipped, 1)
                dve.wait_ge(exp_done, a + 1)
                if not first:
                    dve.wait_ge(prod_pool, DECAYS * (a - 1))
                nc.vector.scalar_tensor_tensor(phi[:, p, :, :], rot[:, :, :], 0.0, ex[:, :, :], ALU.max, ALU.add)\
                    .then_inc(phi_ready, 1)

            def key_values(a, p):
                dve.wait_ge(phi_ready, a + 1)
                for c in range(HD4):
                    dve.wait_ge(ring_ready, RING * a + W_V + c + 1)
                    nc.vector.tensor_tensor(kv[:, p, c, :], ring_ps[:, c % 2, :], phi[:, p, 1, :], ALU.mult)\
                        .then_inc(ring_used, 1)

            def scans(q, p, m):
                n = DECAYS * q + m
                if m == 0:
                    dve.wait_ge(ring_used, RING * (q + 1))
                    dve.wait_ge(clipped, q + 1)
                    dve.wait_ge(nd_ready, DECAYS * q)
                for s in range(STATES):
                    ins = nc.vector.tensor_tensor_scan(
                        state[:, m, s, :], beta[:, p, m, :], phi[:, p, 1, :] if s == 0 else kv[:, p, s - 1, :],
                        0.0 if p == 0 else carry[:, m, s:s + 1], ALU.mult, ALU.add)
                ins.then_inc(scanned, 1)
                dve.wait_ge(scanned, n + 1)
                nc.vector.tensor_copy(carry[:, m, :], state[:, m, :, BLK - 1]).then_inc(carried, 1)
                dve.wait_ge(carried, n + 1)
                for s in range(STATES):
                    if s in POOL_STATES[m]:
                        continue
                    st = state[:, m, s, :]
                    ins = nc.vector.tensor_tensor(st, st, phi[:, p, 0, :], ALU.mult)
                ins.then_inc(prod_dve, 1)

            def divide(q, p):
                dve.wait_ge(nd_ready, DECAYS * (q + 1))
                chain = Chain(dve, div_link, 3 * q)
                nc.vector.tensor_scalar_add(rd[:, :, :, :], den_ps[:, 0:DECAYS, :, :], DEN_EPS).then_inc(den_used, 1)
                dve.wait_ge(den_used, q + 1)
                chain.link(nc.vector.reciprocal(rd[:, :, :, :], rd[:, :, :, :]))
                dve.wait_ge(mix_ready, q + 1)
                chain.link(nc.vector.tensor_tensor(rd[:, :, :, :], rd[:, :, :, :], mix[:, p, :, :, :], ALU.mult))
                for m in range(DECAYS):
                    ins = nc.vector.tensor_tensor(ym[:, m, :, :, :], num_ps[:, m, :, :, :],
                                                  rd[:, m, :, :].unsqueeze(2).to_broadcast([P, GT, HD4, RH]), ALU.mult)
                chain.link(ins)
                dve.wait_ge(yt_ps_ready, q)
                y0, y1 = (ym[:, m, :, :, :].rearrange("p t c h -> p t (c h)") for m in range(DECAYS))
                nc.vector.tensor_tensor(ytok[:, :, :], y0, y1, ALU.add).then_inc(ytok_ready, 1)

            def add_residual(q):
                dve.wait_ge(res_ready, q + 1)
                dve.wait_ge(y_ready, q + 1)
                nc.vector.tensor_tensor(z[:, :, :], y_ps[:, :, :], res[:, bass.ds(q * GT, GT), :], ALU.add)\
                    .then_inc(z_ready, 1)
                dve.wait_ge(z_ready, q + 1)
                for j in range(GT):
                    ins = nc.vector.bn_stats(z_stats[:, j, :], z[:, j, :])
                ins.then_inc(z_link, 1)
                dve.wait_ge(z_link, 2 * q + 1)
                nc.vector.memset(norm.pause[:, 0:1], 0.0)
                for j in range(GT):
                    ins = nc.vector.bn_aggr(z_mv[:, j, :], z_stats[:, j, :])
                ins.then_inc(z_link, 1)
                dve.wait_ge(z_link, 2 * q + 2)
                nc.vector.tensor_scalar_add(z_mv[:, :, 1], z_mv[:, :, 1], LN_EPS).then_inc(z_stats_ready, 1)

            def finish(q):
                dve.wait_ge(z_rstd_ready, q + 1)
                chain = Chain(dve, zn_link, 2 * q)
                for j in range(GT):
                    ins = nc.vector.tensor_scalar(zn[:, j, :], z[:, j, :], z_mv[:, j, 0:1], z_rstd[:, j:j + 1],
                                                  ALU.subtract, ALU.mult)
                chain.link(ins)
                chain.link(nc.vector.tensor_tensor(zn[:, :, :], zn[:, :, :],
                                                   w["ln_g"][:, :].unsqueeze(1).to_broadcast([P, GT, P]), ALU.mult))
                xq = x[:, bass.ds(q * GT, GT), :]
                nc.vector.tensor_tensor(xq, xq, zn[:, :, :], ALU.add).then_inc(x_done, 1)
                dve.wait_ge(x_done, q + 1)

            def prologue():
                norm.statistics(dve, 0)
                norm.scale(dve, 0)
                rope(0, 0)
                features(0, 0, first=True)
                key_values(0, 0)
                norm.statistics(dve, 1)
                norm.scale(dve, 1, xn_used=res_ready)

            def iteration(q, p):
                if exists(q + 2):
                    norm.statistics(dve, q + 2)
                if exists(q + 1):
                    rope(q + 1, 1 - p)
                scans(q, p, 0)
                if exists(q - 1):
                    add_residual(q - 1)
                if exists(q + 2):
                    norm.scale(dve, q + 2, xn_used=res_ready)
                scans(q, p, 1)
                if exists(q + 1):
                    features(q + 1, 1 - p)
                if exists(q + 1):
                    key_values(q + 1, 1 - p)
                if exists(q - 1):
                    finish(q - 1)
                divide(q, p)

            def epilogue():
                add_residual(BLOCKS - 1)
                finish(BLOCKS - 1)

            run(dve, prologue, iteration, epilogue)

HEADS, HD = 16, 8
UH = HEADS // 2
PARTS = 3
STACK = PARTS * PARTS * HD
ROWS = 96
PROBS = 4
VW = 32
GH = 4
E_STEPS = 2 * 2 * (GT + 2 * GT)
M_STEPS = UH * (GT + 2 * GT)
M_FIRST = UH * GT
LEAD = 8

def exp_steps():
    out = []
    for qb in range(2):
        for g in range(UH // GH):
            kts = GT * (qb + 1)
            for kt in range(kts):
                for pair in range(GH // 2):
                    out.append((qb, g, kt, pair, kt == 0, kt == kts - 1))
    return out

def max_steps():
    return [(i, half, h) for i in range(TPB) for half in range(1 + i // GT) for h in range(UH)]

MISC = ("shA", "shB", "xt", "q", "k", "v", "otr", "ao", "y")

def softmax_schedule():
    prep = [("stat", 0), ("xt", 0), ("q", 0), ("k", 0), ("v", 0), ("stat", 1), ("xt", 1), ("q", 1), ("k", 1), ("v", 1),
            ("store", 0)]
    prologue = prep + [("vpad", 0), ("stack", 0)]
    prologue += [("m", j) for j in range(M_FIRST)] + [("shA", 0)] + [("m", j) for j in range(M_FIRST, M_STEPS)]
    units = []
    for half in range(2):
        at = [[] for _ in range(E_STEPS)]
        at[0].append(("stack", 0))
        at[2].append(("shB", 0))
        if half == 1:
            at[2].append(("oev", -1))
            at[3].append(("otr", -1))
        for k, end in enumerate((8, 16, 32)):
            at[end + 2].append(("oev", k))
            at[end + 3].append(("otr", k))
        for j in range(M_STEPS):
            n = LEAD + j * (E_STEPS - LEAD) // M_STEPS
            at[n].append(("m", j))
            if j == M_FIRST + 4:
                at[n].append(("shA", 0))
        if half == 0:
            for n, ev in zip((11, 13, 14, 15, 16, 19, 21, 22, 23, 24, 30), prep):
                at[n].append(ev)
        units.append(at)
    tail = [("oev", 3), ("otr", 3), ("vpad", 0), ("ao", 0), ("y", 0), ("ao", 1), ("y", 1)]
    return prologue, units, tail

def softmax_stage(nc, x, const, w, loaded, name):
    with ExitStack() as ctx:
        def sb(n, shape, dt=F32):
            return ctx.enter_context(nc.sbuf_tensor(f"{name}_{n}", shape, dt))

        def sem(n):
            return nc.alloc_semaphore(f"{name}_{n}")

        banks = Banks(const["psum"])
        e_ps = banks.take(2, 2, BLK)
        m_ps = banks.take(2, BLK)
        o_ps = banks.take(BLK)
        misc_ps = banks.take(GT, P)
        norm = Prenorm(nc, ctx, const, x, name + "_n", parities=1, xt_ps=misc_ps)
        full = sb("full", [P, BLK])
        rest = sb("rest", [P, BLK])
        parts = sb("parts", [P, 2, PARTS, SEQ], BF16)
        stack = sb("stack", [ROWS, 2, 2, UH, SEQ], BF16)
        v_raw = sb("v_raw", [P, TPB, P])
        v_pad = sb("v_pad", [P, TPB, HEADS, VW])
        prob = sb("prob", [P, PROBS, 2, BLK])
        mx = sb("mx", [P, TPB, 2, UH])
        neg = sb("neg", [P, 2, GT, UH])
        mt = sb("mt", [UH, BLK])
        mt_rest = sb("mt_rest", [UH, BLK])
        mt_parts = sb("mt_parts", [UH, PARTS, BLK], BF16)
        o_sb = sb("o_sb", [P, BLK])
        rsum = sb("rsum", [P, GT, GH])
        ao = sb("ao", [P, TPB, HEADS, HD])
        aot = sb("aot", [P, BLK])

        parts_dram = nc.dram_tensor(f"{name}_parts_dram", [2, PARTS, P, SEQ], BF16, kind="Internal").ap()

        init_done, parts_link, parts_ready = sem("init_done"), sem("parts_link"), sem("parts_ready")
        stack_loaded, shift_loaded = sem("stack_loaded"), sem("shift_loaded")
        score_ready, exp_done, pv_done = sem("score_ready"), sem("exp_done"), sem("pv_done")
        m_ready, m_done = sem("m_ready"), sem("m_done")
        neg_link, neg_ready, mt_link, mt_ready = sem("neg_link"), sem("neg_ready"), sem("mt_link"), sem("mt_ready")
        vpad_ready = sem("vpad_ready")
        o_copied, rsum_ready = sem("o_copied"), sem("rsum_ready")
        misc_ready, misc_used = sem("misc_ready"), sem("misc_used")
        pad_loaded, parts_stored = sem("pad_loaded"), sem("parts_stored")

        PROLOGUE, UNITS, TAIL = softmax_schedule()
        ESTEPS, MSTEPS = exp_steps(), max_steps()
        before = sum(ev[0] in MISC for ev in PROLOGUE)
        body_events = [(half, ev) for half in range(2) for step in UNITS[half] for ev in step] + [(2, ev) for ev in TAIL]
        place = {key: n for n, key in enumerate(k for k in body_events if k[1][0] in MISC)}
        place.update({(-1, ev): n for n, ev in enumerate(e for e in PROLOGUE if e[0] in MISC)})
        per_body = sum(ev[0] in MISC for _, ev in body_events)
        DMAS = 2 * PARTS * PARTS + 1

        NEXT_UNIT = ("stack", "m", "shA")
        NEXT_BATCH = ("store", "stat", "xt", "q", "k", "v", "vpad")

        def skip(half, ev, more):
            return not more and (ev[0] in NEXT_BATCH or (half == 1 and ev[0] in NEXT_UNIT))

        def run(eng, event, step=lambda n, u, par, b: None, late=lambda n, u, par: None, unit_end=lambda u, par: None):
            for ev in PROLOGUE:
                event(ev, place.get((-1, ev), 0), 0, 0, 0)

            def body(b, more):
                skipped = 0
                for half in range(3):
                    steps = UNITS[half] if half < 2 else [TAIL]
                    for n, events in enumerate(steps):
                        before_step = int(half < 2 and bool(events) and events[0][0] == "m")
                        after_late = len(events) - int(half < 2 and len(events) > 2 and events[-1][0] == "m")
                        for i, ev in enumerate(events + [None]):
                            if half < 2 and i == before_step:
                                step(n, 2 * b + half, half, b)
                            if half < 2 and i == after_late:
                                late(n, 2 * b + half, half)
                            if ev is None:
                                break
                            misc = 0
                            if ev[0] in MISC:
                                misc = before + per_body * b + place[half, ev] - skipped
                            if skip(half, ev, more):
                                skipped += ev[0] in MISC
                            elif ev[0] in NEXT_UNIT:
                                event(ev, misc, 2 * b + half + 1, 1 - half, b + half)
                            elif ev[0] in NEXT_BATCH:
                                event(ev, misc, 0, 0, b + 1)
                            else:
                                event(ev, misc, 2 * b + min(half, 1), min(half, 1), b)
                    if half < 2:
                        unit_end(2 * b + half, half)

            with eng.Fori(0, BATCH - 1) as b:
                body(b, True)
            body(BATCH - 1, False)

        def zeroth(u):
            return isinstance(u, int) and u == 0

        def m_bank(j, u):
            if zeroth(u) and j % 6 >= 2:
                return e_ps[:, (j % 6 - 2) // 2, j % 2, :], 6
            return (m_ps[:, j % 6, :], 6) if zeroth(u) else (m_ps[:, j % 2, :], 2)

        block = ctx.enter_context(nc.Block())

        @block.sync
        def _(sp):
            rows = slice(STACK + PARTS, ROWS)
            flat = stack[:, :, :, :, :].rearrange("r u i h n -> r (u i) (h n)")
            sp.dma_start(flat[rows, :, :], w["dram_zero"].unsqueeze(1).to_broadcast([ROWS - STACK - PARTS, 4, UH * SEQ]))\
                .then_inc(pad_loaded, 16)
            for par in range(2):
                sp.dma_start(flat[STACK:STACK + PARTS, 2 * par + 1, :],
                             w["dram_one"].to_broadcast([PARTS, UH * SEQ])).then_inc(pad_loaded, 16)

            def event(ev, misc, u, par, b):
                if ev[0] == "store":
                    sp.wait_ge(stack_loaded, 32 * DMAS * b)
                    sp.wait_ge(pad_loaded, 48)
                    sp.wait_ge(parts_ready, 4 * b + 4)
                    sp.dma_start(parts_dram.rearrange("i a c n -> c i a n"), parts[:, :, :, :]).then_inc(parts_stored, 16)
                if ev[0] == "stack":
                    if not zeroth(u):
                        sp.wait_ge(score_ready, E_STEPS * (u - 1))
                    sp.wait_ge(parts_stored, 16 * (b + 1))
                    for s in range(PARTS * PARTS):
                        for i, part in ((0, s // PARTS), (1, s % PARTS)):
                            src = parts_dram[i, part, UH * HD * par:UH * HD * (par + 1), :]
                            sp.dma_start(stack[HD * s:HD * (s + 1), par, i, :, :],
                                         src.rearrange("(h r) n -> r h n", r=HD)).then_inc(stack_loaded, 16)
                    sp.dma_start(flat[STACK:STACK + PARTS, 2 * par, :],
                                 w["dram_zero"].to_broadcast([PARTS, UH * SEQ])).then_inc(stack_loaded, 16)
                if ev[0] in ("shA", "shB"):
                    qb = int(ev[0] == "shB")
                    sp.wait_ge(mt_ready, 2 * u + 1 + qb)
                    for i in range(PARTS):
                        sp.dma_start(stack[STACK + i:STACK + i + 1, par, 0, :, qb * BLK:(qb + 1) * BLK],
                                     mt_parts[:, i, :]).then_inc(shift_loaded, 16)

            run(sp, event)

        @block.gpsimd
        def _(pool):
            nc.gpsimd.memset(v_pad[:, :, :, HD + 1:VW], 0.0)
            nc.gpsimd.memset(v_pad[:, :, :, HD:HD + 1], 1.0).then_inc(init_done, 1)

            def event(ev, misc, u, par, b):
                if ev[0] == "stat":
                    norm.invert(pool, 2 * b + ev[1])
                if ev[0] in ("q", "k"):
                    i, p = int(ev[0] == "k"), ev[1]
                    n = 4 * b + 2 * p + i
                    cols = slice(p * BLK, (p + 1) * BLK)
                    pool.wait_ge(misc_used, misc + 1)
                    nc.gpsimd.tensor_tensor(rest[:, :], full[:, :], parts[:, i, 0, cols], ALU.subtract)
                    nc.gpsimd.tensor_tensor(parts[:, i, 1, cols], full[:, :], parts[:, i, 0, cols], ALU.subtract)\
                        .then_inc(parts_link, 1)
                    pool.wait_ge(parts_link, n + 1)
                    nc.gpsimd.tensor_tensor(parts[:, i, 2, cols], rest[:, :], parts[:, i, 1, cols], ALU.subtract)\
                        .then_inc(parts_ready, 1)
                if ev[0] in ("shA", "shB"):
                    n = 2 * u + int(ev[0] == "shB")
                    pool.wait_ge(misc_used, misc + 1)
                    nc.gpsimd.tensor_tensor(mt_rest[:, :], mt[:, :], mt_parts[:, 0, :], ALU.subtract)
                    nc.gpsimd.tensor_tensor(mt_parts[:, 1, :], mt[:, :], mt_parts[:, 0, :], ALU.subtract)\
                        .then_inc(mt_link, 1)
                    pool.wait_ge(mt_link, n + 1)
                    nc.gpsimd.tensor_tensor(mt_parts[:, 2, :], mt_rest[:, :], mt_parts[:, 1, :], ALU.subtract)\
                        .then_inc(mt_ready, 1)

            run(pool, event)

        @block.tensor
        def _(pe):
            pe.wait_ge(*loaded)
            pe.wait_ge(pad_loaded, 48)
            pe.wait_ge(init_done, 1)

            def scores(n, u, par):
                qb, g, kt, pair, _, _ = ESTEPS[n]
                diag = kt - GT * qb
                lo = P * max(diag, 0)
                if n == 0:
                    pe.wait_ge(shift_loaded, 16 * PARTS * (2 * u + 1))
                    pe.wait_ge(m_done, M_STEPS * (u + 1))
                if n == E_STEPS // 3:
                    pe.wait_ge(shift_loaded, 16 * PARTS * (2 * u + 2))
                pe.wait_ge(exp_done, E_STEPS * u + max(n - 1, 0))
                for j in range(2):
                    h = GH * g + 2 * pair + j
                    out = e_ps[:, n % 2, j, lo:BLK]
                    ins = pe.matmul(out, stack[:, par, 1, h, kt * P:(kt + 1) * P],
                                    stack[:, par, 0, h, qb * BLK + lo:(qb + 1) * BLK], start=True, stop=(diag < 0))
                    if diag >= 0:
                        ins = pe.matmul(e_ps[:, n % 2, j, lo:lo + P], w["ident_bf"][:, :], w["causal_kq"][:, :],
                                        start=False, stop=True)
                ins.then_inc(score_ready, 1)

            def values(n, u, par):
                qb, g, kt, _, first, last = ESTEPS[n]
                lo = P * max(kt - GT * qb, 0)
                pe.wait_ge(exp_done, E_STEPS * u + n + 2)
                if first:
                    k = 2 * qb + g
                    pe.wait_ge(o_copied, 4 * u + k)
                for q in range(GH):
                    head = UH * par + GH * g + q
                    ins = pe.matmul(o_ps[VW * q:VW * (q + 1), lo:BLK], v_pad[:, kt, head, :],
                                    prob[:, (n + q // 2) % PROBS, q % 2, lo:BLK], start=first, stop=last, skip_group_check=True,
                                    tile_position=(0, VW * q))
                ins.then_inc(pv_done, 2)

            def step(n, u, par, b):
                scores(n, u, par)
                if n == 0:
                    pe.wait_ge(vpad_ready, b + 1)

            def late(n, u, par):
                if n == 1 and par == 1:
                    values(E_STEPS - 2, u - 1, 0)
                if n >= 3 and n % 2 == 1:
                    values(n - 3, u, par)

            def unit_end(u, par):
                if par == 1:
                    values(E_STEPS - 2, u, 1)

            def event(ev, misc, u, par, b):
                kind = ev[0]
                if kind in MISC:
                    pe.wait_ge(misc_used, misc)
                if kind == "xt":
                    pe.wait_ge(norm.xn_ready, 2 * b + ev[1] + 1)
                    for j in range(GT):
                        ins = pe.transpose(misc_ps[:, j, :], norm.xn[:, j, :], const["ident"][:, :])
                    ins.then_inc(misc_ready, 1)
                if kind in ("q", "k"):
                    pe.matmul(misc_ps[:, :, :], w[kind][:, :], norm.xt[:, 0, :], start=True, stop=True)\
                        .then_inc(misc_ready, 1)
                if kind == "v":
                    for j in range(GT):
                        pe.matmul(misc_ps[:, j, :], norm.xt[:, 0, j * P:(j + 1) * P], w["v"][:, :], start=True, stop=False)
                        ins = pe.matmul(misc_ps[:, j, :], const["ones"][0:1, 0:P], w["v_b"][:, :], start=False, stop=True)
                    ins.then_inc(misc_ready, 1)
                if kind == "m":
                    i, half, h = MSTEPS[ev[1]]
                    width = min(BLK, (i + 1) * P - half * BLK)
                    diag = half == i // GT
                    if ev[1] == 0:
                        pe.wait_ge(stack_loaded, 16 * DMAS * (u + 1))
                    bank, banks_back = m_bank(ev[1], u)
                    pe.wait_ge(m_done, M_STEPS * u + max(ev[1] + 1 - banks_back, 0))
                    ins = pe.matmul(bank[:, 0:width], stack[:, par, 0, h, i * P:(i + 1) * P],
                                    stack[:, par, 1, h, half * BLK:half * BLK + width], start=True, stop=not diag)
                    if diag:
                        ins = pe.matmul(bank[:, width - P:width], w["ident_bf"][:, :],
                                        w["causal_qk"][:, :], start=False, stop=True)
                    ins.then_inc(m_ready, 1)
                if kind in ("shA", "shB"):
                    n = 2 * u + int(kind == "shB")
                    pe.wait_ge(neg_ready, n + 1)
                    for j in range(GT):
                        ins = pe.transpose(misc_ps[0:UH, j, :], neg[:, int(kind == "shB"), j, :], const["ident"][:, :])
                    ins.then_inc(misc_ready, 1)
                if kind == "otr":
                    pe.wait_ge(o_copied, 4 * u + ev[1] + 1)
                    for j in range(GT):
                        ins = pe.transpose(misc_ps[:, j, :], o_sb[:, j * P:(j + 1) * P], const["ident"][:, :])
                    ins.then_inc(misc_ready, 1)
                if kind == "ao":
                    for j in range(GT):
                        ins = pe.transpose(misc_ps[:, j, :], ao[:, GT * ev[1] + j, :, :], const["ident"][:, :])
                    ins.then_inc(misc_ready, 1)
                if kind == "y":
                    for j in range(GT):
                        pe.matmul(misc_ps[:, j, :], aot[:, j * P:(j + 1) * P], w["o"][:, :], start=True, stop=False)
                        ins = pe.matmul(misc_ps[:, j, :], const["ones"][0:1, 0:P], w["o_b"][:, :], start=False, stop=True)
                    ins.then_inc(misc_ready, 1)

            run(pe, event, step, late, unit_end)

        @block.scalar
        def _(act):
            act.wait_ge(*loaded)
            act.wait_ge(init_done, 1)

            def step(n, u, par, b):
                qb, g, kt, pair, _, _ = ESTEPS[n]
                lo = P * max(kt - GT * qb, 0)
                act.wait_ge(score_ready, E_STEPS * u + n + 1)
                act.wait_ge(pv_done, E_STEPS * u + (n - PROBS + 1 if par == 1 else max(n - PROBS + 1, 0)))
                nc.scalar.activation(prob[:, n % PROBS, :, lo:BLK], e_ps[:, n % 2, :, lo:BLK], ACT.Exp,
                                     scale=float(HD) ** -0.5).then_inc(exp_done, 1)

            def event(ev, misc, u, par, b):
                if ev[0] == "xt":
                    act.wait_ge(misc_ready, misc + 1)
                    cut = BLK // 2
                    nc.scalar.copy(norm.xt[:, 0, 0:cut], misc_ps[:, 0:GT // 2, :]).then_inc(norm.xt_ready, 1)
                    nc.scalar.copy(norm.xt[:, 0, cut:BLK], misc_ps[:, GT // 2:GT, :]).then_inc(misc_used, 1)
                if ev[0] in ("q", "k"):
                    i, p = int(ev[0] == "k"), ev[1]
                    act.wait_ge(misc_ready, misc + 1)
                    act.wait_ge(parts_ready, 4 * b + 2 * p + i)
                    nc.scalar.activation(full[:, :], misc_ps[:, :, :], ACT.Identity, bias=w["qk_b"][:, i:i + 1])
                    act.wait_ge(stack_loaded, 16 * DMAS * 2 * b)
                    nc.scalar.activation(parts[:, i, 0, p * BLK:(p + 1) * BLK], misc_ps[:, :, :], ACT.Identity,
                                         bias=w["qk_b"][:, i:i + 1]).then_inc(misc_used, 1)
                if ev[0] == "v":
                    act.wait_ge(misc_used, misc + 1)
                if ev[0] == "vpad":
                    act.wait_ge(pv_done, 2 * E_STEPS * b)
                    nc.scalar.copy(v_pad[:, :, :, 0:HD], v_raw[:, :, :].rearrange("p t (h d) -> p t h d", d=HD))\
                        .then_inc(vpad_ready, 1)
                if ev[0] == "ao":
                    act.wait_ge(misc_ready, misc + 1)
                    nc.scalar.copy(aot[:, :], misc_ps[:, :, :]).then_inc(misc_used, 1)

            run(act, event, step)

        @block.vector
        def _(dve):
            dve.wait_ge(*loaded)

            def event(ev, misc, u, par, b):
                kind = ev[0]
                if kind == "stat":
                    norm.statistics(dve, 2 * b + ev[1])
                    norm.scale(dve, 2 * b + ev[1], xn_free=norm.xt_ready)
                if kind == "v":
                    p = ev[1]
                    dve.wait_ge(misc_ready, misc + 1)
                    dve.wait_ge(vpad_ready, b)
                    nc.vector.tensor_copy(v_raw[:, GT * p:GT * (p + 1), :], misc_ps[:, :, :]).then_inc(misc_used, 1)
                if kind == "m":
                    i, half, h = MSTEPS[ev[1]]
                    width = min(BLK, (i + 1) * P - half * BLK)
                    dve.wait_ge(m_ready, M_STEPS * u + ev[1] + 1)
                    bank, _ = m_bank(ev[1], u)
                    nc.vector.tensor_reduce(mx[:, i, half, h:h + 1], bank[:, 0:width], AX.X, ALU.max)\
                        .then_inc(m_done, 1)
                    if ev[1] == M_FIRST - 1:
                        dve.wait_ge(m_done, M_STEPS * u + M_FIRST)
                        nc.vector.tensor_scalar(neg[:, 0, :, :], mx[:, 0:GT, 0, :], -1.0, None, ALU.mult)\
                            .then_inc(neg_ready, 1)
                    if ev[1] == M_STEPS - 1:
                        dve.wait_ge(m_done, M_STEPS * (u + 1))
                        nc.vector.tensor_tensor(neg[:, 1, :, :], mx[:, GT:TPB, 0, :], mx[:, GT:TPB, 1, :], ALU.max)\
                            .then_inc(neg_link, 1)
                        dve.wait_ge(neg_link, u + 1)
                        nc.vector.tensor_scalar(neg[:, 1, :, :], neg[:, 1, :, :], -1.0, None, ALU.mult)\
                            .then_inc(neg_ready, 1)
                if kind in ("shA", "shB"):
                    n = 2 * u + int(kind == "shB")
                    dve.wait_ge(misc_ready, misc + 1)
                    dve.wait_ge(mt_ready, n)
                    dve.wait_ge(shift_loaded, 16 * PARTS * n)
                    nc.vector.tensor_copy(mt[:, :], misc_ps[0:UH, :, :])
                    nc.vector.tensor_copy(mt_parts[:, 0, :], misc_ps[0:UH, :, :]).then_inc(misc_used, 1)
                if kind == "oev":
                    k = 4 * u + ev[1]
                    end = (8, 16, 32, 48)[ev[1]] if ev[1] >= 0 else 0
                    dve.wait_ge(pv_done, E_STEPS * u + end)
                    dve.wait_ge(rsum_ready, k)
                    nc.vector.tensor_copy(o_sb[:, :], o_ps[:, :]).then_inc(o_copied, 1)
                if kind == "otr":
                    k = 4 * u + ev[1]
                    unit_par, group = (par, ev[1]) if ev[1] >= 0 else (1 - par, 3)
                    qb, g = group // 2, group % 2
                    dve.wait_ge(misc_ready, misc + 1)
                    heads = misc_ps[:, :, :].rearrange("p t (h c) -> p t h c", c=VW)
                    nc.vector.reciprocal(rsum[:, :, :], heads[:, :, :, HD]).then_inc(rsum_ready, 1)
                    dve.wait_ge(rsum_ready, k + 1)
                    head = UH * unit_par + GH * g
                    nc.vector.tensor_tensor(ao[:, GT * qb:GT * (qb + 1), head:head + GH, :], heads[:, :, :, 0:HD],
                                            wide(rsum[:, :, :], HD), ALU.mult).then_inc(misc_used, 1)
                if kind == "y":
                    dve.wait_ge(misc_ready, misc + 1)
                    xq = x[:, bass.ds(b * TPB + GT * ev[1], GT), :]
                    nc.vector.tensor_tensor(xq, misc_ps[:, :, :], xq, ALU.add).then_inc(misc_used, 1)

            run(dve, event)

def hybrid_kernel(nc, arrays, out):
    with ExitStack() as ctx:
        def resident(prefix):
            names = [n for n in arrays if n.startswith(prefix)]
            homes, copies = {}, []
            for n in names:
                src, key = arrays[n], n[len(prefix):]
                if key.startswith("dram_"):
                    homes[key] = src
                    continue
                shape = list(src.shape)
                if key in ROW_FOR_ALL:
                    shape[0] = P
                    src = src.to_broadcast(shape)
                homes[key] = ctx.enter_context(nc.sbuf_tensor("s_" + n, shape, src.dtype))
                index = tuple(slice(None) for _ in shape)
                copies.append((homes[key][index], src))
            return homes, copies

        x = ctx.enter_context(nc.sbuf_tensor("x", [P, TILES, P], F32))
        load_first = ctx.enter_context(nc.semaphore("load_first"))
        load_rest = ctx.enter_context(nc.semaphore("load_rest"))
        const, const_copies = resident("const_")
        mamba, mamba_copies = resident("mamba_")
        const["psum"] = ctx.enter_context(nc.psum_tensor("psum", [P, 8, BLK], F32))
        ffn0, ffn0_copies = resident("ffn0_")
        lin, lin_copies = resident("lin_")
        first = [(x[:, :, :], arrays["x"].rearrange("b (t p) c -> p (b t) c", p=P))] + const_copies + mamba_copies
        rest = ffn0_copies + lin_copies

        with nc.Block() as block:
            @block.sync
            def _(sp):
                for dst, src in first:
                    sp.dma_start(dst, src).then_inc(load_first, 16)
                for dst, src in rest:
                    sp.dma_start(dst, src).then_inc(load_rest, 16)

        have_first, have_rest = (load_first, 16 * len(first)), (load_rest, 16 * len(rest))
        def stage(build, *args, **kwargs):
            with nc.cleanup_on_exit():
                build(nc, *args, **kwargs)

        stage(mamba_stage, x, const, mamba, have_first, "mamba")
        ret, ret_copies = resident("ret_")
        soft, soft_copies = resident("soft_")
        layer1 = ret_copies + soft_copies
        ffn1_copies = [(dst, arrays["ffn1_" + n]) for n, (dst, _) in zip(ffn0, ffn0_copies)]
        load_layer1 = ctx.enter_context(nc.semaphore("load_layer1"))
        load_ffn1 = ctx.enter_context(nc.semaphore("load_ffn1"))
        have_ffn1 = (load_ffn1, 16 * len(ffn1_copies))
        have_layer1 = (load_layer1, 16 * len(layer1))
        stage(ffn_stage, x, const, ffn0, have_rest, "ffn0a", fetch=(layer1, load_layer1))
        stage(linear_attention_stage, x, const, lin, have_rest, "lin")
        stage(ffn_stage, x, const, ffn0, have_rest, "ffn0b")
        stage(retention_stage, x, const, ret, have_layer1, "ret", fetch=(ffn1_copies, load_ffn1))
        stage(ffn_stage, x, const, ffn0, have_ffn1, "ffn1a")
        stage(softmax_stage, x, const, soft, have_layer1, "soft")
        stage(ffn_stage, x, const, ffn0, have_ffn1, "ffn1b", out=out.rearrange("b (t p) c -> p (b t) c", p=P))

ROW_FOR_ALL = ("a_log", "ln_g", "ln_b", "out_bias")

def host_layout(a):
    def t(m):
        return np.swapaxes(m, -1, -2)

    def ffn(p):
        w1 = np.concatenate([a[p + "eW1"], a[p + "sW1"][None]])
        w2 = np.concatenate([a[p + "eW2"], a[p + "sW2"][None]])
        return {
            "w1": w1.transpose(1, 0, 2), "w2": w2.transpose(1, 0, 2),
            "b1": t(np.concatenate([a[p + "eb1"], a[p + "sb1"][None]])),
            "b2": np.concatenate([a[p + "eb2"], a[p + "sb2"][None]]),
            "router": a[p + "router_W"], "router_b": a[p + "router_b"][None],
        }

    d_half = P
    m = "L0_attn_a_"
    mamba = {
        "in": t(a[m + "W_in"]).reshape(P, 2 * HALVES, P),
        "conv_w": a[m + "conv_w"].reshape(HALVES, d_half, CONV).transpose(1, 0, 2),
        "conv_b": t(a[m + "conv_b"].reshape(HALVES, d_half)),
        "xproj": t(a[m + "W_xproj"]).reshape(HALVES, d_half, NDBL).transpose(1, 0, 2),
        "a_log": a[m + "A_log"][None],
        "d": t(a[m + "D_param"].reshape(HALVES, d_half)),
        "out": t(a[m + "W_out"]).reshape(HALVES, d_half, P).transpose(1, 0, 2),
    }
    m = "L0_attn_b_"
    qkv = a[m + "qkv_weight"]
    lin = {"q": t(qkv[:P]), "kv": t(qkv[P:]), "proj": t(a[m + "proj_weight"]), "proj_b": a[m + "proj_bias"][None]}
    m = "L1_attn_a_"
    c = np.arange(P)
    head, swapped = c // HD4, c // HD4 * HD4 + (c + HD4 // 2) % HD4
    rows = [a[m + "Wq"], a[m + "Wq"][swapped], a[m + "Wk"], a[m + "Wk"][swapped]]
    rows += [a[m + "Wv"][head * HD4 + i] for i in range(HD4)]
    rows += [a[m + "Wbeta"][head * DECAYS + i] for i in range(DECAYS)]
    ret = {
        "w": np.stack([t(r) for r in rows], axis=1),
        "b": a[m + "bbeta"].reshape(RH, DECAYS)[head],
        "mix": a[m + "Wmix"].reshape(RH, DECAYS, P).transpose(2, 1, 0),
        "mix_b": t(a[m + "bmix"].reshape(1, RH, DECAYS)),
        "out": t(a[m + "Wout"]).reshape(RH, HD4, P).transpose(1, 0, 2).reshape(P, P), "out_bias": a[m + "bout"][None],
        "ln_g": a[m + "ln_g"][None], "ln_b": a[m + "ln_b"][None],
    }
    m = "L1_attn_b_"
    qkv, b = a[m + "W_qkv"], a[m + "b_qkv"]
    soft = {
        "q": t(qkv[:P]), "k": t(qkv[P:2 * P]), "v": t(qkv[2 * P:]),
        "qk_b": t(b[:2 * P].reshape(2, P)), "v_b": b[None, 2 * P:],
        "o": t(a[m + "W_o"]), "o_b": a[m + "b_o"][None],
    }
    groups = shape_constants()
    for name, group in (("mamba", mamba), ("ffn0", ffn("L0_ffn_")), ("lin", lin), ("ret", ret),
                        ("ffn1", ffn("L1_ffn_")), ("soft", soft)):
        groups[name] = {**group, **groups.get(name, {})}
    sent = {"x": a["L0_attn_a_x"]}
    sent.update({f"{name}_{n}": v for name, group in groups.items() for n, v in group.items()})
    return {n: np.ascontiguousarray(v) for n, v in sent.items()}

def kernel(**inputs):
    import concourse.bacc as bacc
    from concourse.bass_utils import run_bass_kernel_spmd

    sent = host_layout({n: np.asarray(v) for n, v in inputs.items()})
    nc = bacc.Bacc("TRN2", target_bir_lowering=False, num_devices=1)
    arrays = {n: nc.dram_tensor("in_" + n, v.shape, mybir.dt.from_np(v.dtype), kind="ExternalInput").ap()
              for n, v in sent.items()}
    out = nc.dram_tensor("out_x", (BATCH, SEQ, P), F32, kind="ExternalOutput").ap()
    hybrid_kernel(nc, arrays, out)
    result = run_bass_kernel_spmd(nc, [{"in_" + n: v for n, v in sent.items()}], core_ids=[0])
    return result.results[0]["out_x"]
```
